# Optimizing a Trainium2 kernel written in Bass

```python
import numpy as np
import jax
import jax.numpy as jnp

def _softmax(x, axis=-1):
    return jax.nn.softmax(x, axis=axis)

def _gelu(x):
    return jax.nn.gelu(x, approximate=True)

def _silu(x):
    return jax.nn.silu(x)

def _sigmoid(x):
    return jax.nn.sigmoid(x)

def _layernorm(x, axis=-1, eps=1e-05):
    m = jnp.mean(x, axis=axis, keepdims=True)
    v = jnp.var(x, axis=axis, keepdims=True)
    return (x - m) / jnp.sqrt(v + eps)

def _scatter_add(tgt, idx, src, axis=0):
    return tgt.at[idx].add(src)

def _segment_sum(src, seg, n):
    return jax.ops.segment_sum(src, seg, n)
kernel_name = 'mk_hybrid_d2_jaxref_r8_07108c'

def setup_inputs(seed: int=0):
    np.random.seed(seed)
    _w = jnp.asarray

    def _L0_attn_a_setup():
        import jax, jax.numpy as jnp
        import numpy as np
        D_MODEL = 256
        N_HEADS = 32
        N_KV_HEADS = 8
        HEAD_DIM = D_MODEL // N_HEADS
        N_GROUPS = N_HEADS // N_KV_HEADS
        THETA = 10000.0

        def _rope_tables(T, dim):
            inv_freq = 1.0 / THETA ** (jnp.arange(0, dim, 2, dtype=jnp.float32) / dim)
            t = jnp.arange(T, dtype=jnp.float32)
            freqs = jnp.outer(t, inv_freq)
            return (jnp.cos(freqs), jnp.sin(freqs))

        def _apply_rope(x, cos, sin):
            half = x.shape[-1] // 2
            x1, x2 = (x[..., :half], x[..., half:])
            c = cos[None, None, :, :]
            s = sin[None, None, :, :]
            return jnp.concatenate([x1 * c - x2 * s, x2 * c + x1 * s], axis=-1)
        key = jax.random.key(seed)
        ks = jax.random.split(key, 6)
        b, T = (2, 256)
        d = D_MODEL
        dkv = N_KV_HEADS * HEAD_DIM
        sc = 1.0 / np.sqrt(d)
        x = jax.random.normal(ks[0], (b, T, d), dtype=jnp.float32)
        Wq = jax.random.normal(ks[1], (d, d), dtype=jnp.float32) * sc
        Wk = jax.random.normal(ks[2], (d, dkv), dtype=jnp.float32) * sc
        Wv = jax.random.normal(ks[3], (d, dkv), dtype=jnp.float32) * sc
        Wo = jax.random.normal(ks[4], (d, d), dtype=jnp.float32) * sc
        b_out = jax.random.normal(ks[5], (d,), dtype=jnp.float32) * 0.01
        return {'x': x, 'Wq': Wq, 'Wk': Wk, 'Wv': Wv, 'Wo': Wo, 'b_out': b_out}
    _L0_attn_a_in = _L0_attn_a_setup()

    def _L0_attn_b_setup():
        import jax, jax.numpy as jnp
        import numpy as np
        ROPE_THETA = 10000.0

        def rope(t, rot_dim):
            S = t.shape[-2]
            half = rot_dim // 2
            inv_freq = 1.0 / ROPE_THETA ** (jnp.arange(0, rot_dim, 2, dtype=jnp.float32) / rot_dim)
            freqs = jnp.arange(S, dtype=jnp.float32)[:, None] * inv_freq[None, :]
            freqs = jnp.repeat(freqs, 2, axis=-1)
            cos, sin = (jnp.cos(freqs), jnp.sin(freqs))
            t_rot, t_pass = (t[..., :rot_dim], t[..., rot_dim:])
            x = t_rot.reshape(*t_rot.shape[:-1], half, 2)
            rh = jnp.stack([-x[..., 1], x[..., 0]], axis=-1).reshape(t_rot.shape)
            t_rot = t_rot * cos + rh * sin
            return jnp.concatenate([t_rot, t_pass], axis=-1)

        def feature_map(x):
            norm = jnp.sqrt(jnp.sum(x * x, axis=-1, keepdims=True))
            return x / jnp.maximum(norm, 1e-12)
        key = jax.random.key(seed)
        kx, kwi, kwo = jax.random.split(key, 3)
        B, S, D = (8, 512, 256)
        scale = 0.02
        return {'X': jax.random.normal(kx, (B, S, D), dtype=jnp.float32), 'W_in': jax.random.normal(kwi, (3 * D, D), dtype=jnp.float32) * scale, 'b_in': jnp.zeros((3 * D,), dtype=jnp.float32), 'W_out': jax.random.normal(kwo, (D, D), dtype=jnp.float32) * scale, 'b_out': jnp.zeros((D,), dtype=jnp.float32)}
    _L0_attn_b_in = _L0_attn_b_setup()

    def _L0_ffn_setup():
        import jax, jax.numpy as jnp
        import numpy as np
        D_MODEL = 256
        D_FF = 1024
        N_EXPERTS = 4
        B, S = (2, 256)
        key = jax.random.key(seed)
        ks = jax.random.split(key, 6)
        scale = 0.02
        return {'hidden_states': jax.random.normal(ks[0], (B, S, D_MODEL), dtype=jnp.float32), 'Wr': jax.random.normal(ks[1], (D_MODEL, N_EXPERTS), dtype=jnp.float32) * scale, 'br': jnp.zeros((N_EXPERTS,), dtype=jnp.float32), 'Wg': jax.random.normal(ks[2], (N_EXPERTS, D_MODEL, D_FF), dtype=jnp.float32) * scale, 'Wu': jax.random.normal(ks[3], (N_EXPERTS, D_MODEL, D_FF), dtype=jnp.float32) * scale, 'Wd': jax.random.normal(ks[4], (N_EXPERTS, D_FF, D_MODEL), dtype=jnp.float32) * scale}
    _L0_ffn_in = _L0_ffn_setup()

    def _L1_attn_a_setup():
        import jax, jax.numpy as jnp
        import numpy as np
        D_MODEL = 256
        N_HEADS = 16
        D_K = D_MODEL // N_HEADS
        EPS = 1e-06
        key = jax.random.key(seed)
        ks = jax.random.split(key, 9)
        s = 1.0 / np.sqrt(D_MODEL)
        return {'x': jax.random.normal(ks[0], (4, 512, D_MODEL), dtype=jnp.float32), 'Wq': jax.random.normal(ks[1], (D_MODEL, D_MODEL), dtype=jnp.float32) * s, 'bq': jnp.zeros((D_MODEL,), dtype=jnp.float32), 'Wk': jax.random.normal(ks[2], (D_MODEL, D_MODEL), dtype=jnp.float32) * s, 'bk': jnp.zeros((D_MODEL,), dtype=jnp.float32), 'Wv': jax.random.normal(ks[3], (D_MODEL, D_MODEL), dtype=jnp.float32) * s, 'bv': jnp.zeros((D_MODEL,), dtype=jnp.float32), 'Wo': jax.random.normal(ks[4], (D_MODEL, D_MODEL), dtype=jnp.float32) * s, 'bo': jnp.zeros((D_MODEL,), dtype=jnp.float32)}
    _L1_attn_a_in = _L1_attn_a_setup()

    def _L1_attn_b_setup():
        import jax, jax.numpy as jnp
        import numpy as np
        N_EMBD = 256
        Q_HEAD = 16
        KV_HEAD = 4
        HEAD_DIM = N_EMBD // Q_HEAD
        ROPE_BASE = 10000.0

        def _rope(Y, d_rope, base=ROPE_BASE):
            b, h, t, d = Y.shape
            mid = d_rope // 2
            Y1 = Y[:, :mid]
            Y2 = Y[:, mid:]
            Ym1 = jnp.concatenate([Y1, Y2], axis=1)
            Ym2 = jnp.concatenate([-Y2, Y1], axis=1)
            inv = base ** (-2.0 * jnp.arange(d // 2, dtype=jnp.float32) / d)
            theta = jnp.arange(t, dtype=jnp.float32)[:, None] * inv[None, :]
            cos2 = jnp.concatenate([jnp.cos(theta), jnp.cos(theta)], axis=1)
            sin2 = jnp.concatenate([jnp.sin(theta), jnp.sin(theta)], axis=1)
            return Ym1 * cos2 + Ym2 * sin2

        def _attention(x, Wq, bq, Wk, bk, Wv, bv, Wo, bo):
            b, t, n = x.shape
            hd = n // Q_HEAD
            q = x @ Wq.T + bq
            k = x @ Wk.T + bk
            v = x @ Wv.T + bv
            q = q.reshape(b, t, Q_HEAD, hd).transpose(0, 2, 1, 3)
            k = k.reshape(b, t, KV_HEAD, hd).transpose(0, 2, 1, 3)
            v = v.reshape(b, t, KV_HEAD, hd).transpose(0, 2, 1, 3)
            q = _rope(q, N_EMBD)
            k = _rope(k, N_EMBD)
            rep = Q_HEAD // KV_HEAD
            k = jnp.repeat(k, rep, axis=1)
            v = jnp.repeat(v, rep, axis=1)
            scale = jnp.sqrt(jnp.float32(hd))
            att = jnp.einsum('bhqd,bhkd->bhqk', q, k) / scale
            causal = jnp.tril(jnp.ones((t, t), dtype=bool))
            att = jnp.where(causal[None, None], att, -jnp.inf)
            att = jax.nn.softmax(att, axis=-1)
            y = jnp.einsum('bhqt,bhtd->bhqd', att, v)
            y = y.transpose(0, 2, 1, 3).reshape(b, t, n)
            return y @ Wo.T + bo
        key = jax.random.key(seed)
        ks = jax.random.split(key, 9)
        kv_dim = HEAD_DIM * KV_HEAD
        s = 1.0 / np.sqrt(N_EMBD)
        return {'x': jax.random.normal(ks[0], (4, 128, N_EMBD), jnp.float32), 'Wq': jax.random.normal(ks[1], (N_EMBD, N_EMBD), jnp.float32) * s, 'bq': jax.random.normal(ks[2], (N_EMBD,), jnp.float32) * 0.01, 'Wk': jax.random.normal(ks[3], (kv_dim, N_EMBD), jnp.float32) * s, 'bk': jax.random.normal(ks[4], (kv_dim,), jnp.float32) * 0.01, 'Wv': jax.random.normal(ks[5], (kv_dim, N_EMBD), jnp.float32) * s, 'bv': jax.random.normal(ks[6], (kv_dim,), jnp.float32) * 0.01, 'Wo': jax.random.normal(ks[7], (N_EMBD, N_EMBD), jnp.float32) * s, 'bo': jax.random.normal(ks[8], (N_EMBD,), jnp.float32) * 0.01}
    _L1_attn_b_in = _L1_attn_b_setup()

    def _L1_ffn_setup():
        import jax, jax.numpy as jnp
        import numpy as np
        B, S, D = (4, 64, 256)
        E, K, H = (8, 2, 176)
        HS = 2 * 176
        ALPHA = 0.001
        W_SCALE = 0.02

        def _moe_forward(hidden_states, gate_w, w_gate, w_up, w_down, sw_gate, sw_up, sw_down):
            b, s, d = hidden_states.shape
            x = hidden_states.reshape(-1, d)
            T = x.shape[0]
            logits = x @ gate_w
            scores = jax.nn.softmax(logits, axis=-1)
            topk_w, topk_idx = jax.lax.top_k(scores, K)
            mask = jax.nn.one_hot(topk_idx, E, dtype=scores.dtype).sum(axis=1)
            ce = mask.mean(axis=0)
            Pi = scores.mean(axis=0)
            aux_loss = (Pi * ce * E).sum() * ALPHA
            comb = jnp.zeros((T, E), dtype=x.dtype)
            comb = comb.at[jnp.arange(T)[:, None], topk_idx].add(topk_w)
            g = jax.nn.silu(jnp.einsum('td,edh->teh', x, w_gate)) * jnp.einsum('td,edh->teh', x, w_up)
            routed = jnp.einsum('teh,ehd,te->td', g, w_down, comb)
            shared = jax.nn.silu(x @ sw_gate) * (x @ sw_up) @ sw_down
            out = (routed + shared).reshape(b, s, d)
            return (out, aux_loss)
        key = jax.random.key(seed)
        ks = jax.random.split(key, 8)
        rn = lambda k, sh: jax.random.normal(k, sh, dtype=jnp.float32)
        return {'hidden_states': rn(ks[0], (B, S, D)), 'gate_w': rn(ks[1], (D, E)) * W_SCALE, 'w_gate': rn(ks[2], (E, D, H)) * W_SCALE, 'w_up': rn(ks[3], (E, D, H)) * W_SCALE, 'w_down': rn(ks[4], (E, H, D)) * W_SCALE, 'sw_gate': rn(ks[5], (D, HS)) * W_SCALE, 'sw_up': rn(ks[6], (D, HS)) * W_SCALE, 'sw_down': rn(ks[7], (HS, D)) * W_SCALE}
    _L1_ffn_in = _L1_ffn_setup()
    _d = {'L0_attn_a_x': _L0_attn_a_in['x'], 'L0_attn_a_Wq': _L0_attn_a_in['Wq'], 'L0_attn_a_Wk': _L0_attn_a_in['Wk'], 'L0_attn_a_Wv': _L0_attn_a_in['Wv'], 'L0_attn_a_Wo': _L0_attn_a_in['Wo'], 'L0_attn_a_b_out': _L0_attn_a_in['b_out'], 'L0_attn_b_W_in': _L0_attn_b_in['W_in'], 'L0_attn_b_b_in': _L0_attn_b_in['b_in'], 'L0_attn_b_W_out': _L0_attn_b_in['W_out'], 'L0_attn_b_b_out': _L0_attn_b_in['b_out'], 'L0_ffn_Wr': _L0_ffn_in['Wr'], 'L0_ffn_br': _L0_ffn_in['br'], 'L0_ffn_Wg': _L0_ffn_in['Wg'], 'L0_ffn_Wu': _L0_ffn_in['Wu'], 'L0_ffn_Wd': _L0_ffn_in['Wd'], 'L1_attn_a_Wq': _L1_attn_a_in['Wq'], 'L1_attn_a_bq': _L1_attn_a_in['bq'], 'L1_attn_a_Wk': _L1_attn_a_in['Wk'], 'L1_attn_a_bk': _L1_attn_a_in['bk'], 'L1_attn_a_Wv': _L1_attn_a_in['Wv'], 'L1_attn_a_bv': _L1_attn_a_in['bv'], 'L1_attn_a_Wo': _L1_attn_a_in['Wo'], 'L1_attn_a_bo': _L1_attn_a_in['bo'], 'L1_attn_b_Wq': _L1_attn_b_in['Wq'], 'L1_attn_b_bq': _L1_attn_b_in['bq'], 'L1_attn_b_Wk': _L1_attn_b_in['Wk'], 'L1_attn_b_bk': _L1_attn_b_in['bk'], 'L1_attn_b_Wv': _L1_attn_b_in['Wv'], 'L1_attn_b_bv': _L1_attn_b_in['bv'], 'L1_attn_b_Wo': _L1_attn_b_in['Wo'], 'L1_attn_b_bo': _L1_attn_b_in['bo'], 'L1_ffn_gate_w': _L1_ffn_in['gate_w'], 'L1_ffn_w_gate': _L1_ffn_in['w_gate'], 'L1_ffn_w_up': _L1_ffn_in['w_up'], 'L1_ffn_w_down': _L1_ffn_in['w_down'], 'L1_ffn_sw_gate': _L1_ffn_in['sw_gate'], 'L1_ffn_sw_up': _L1_ffn_in['sw_up'], 'L1_ffn_sw_down': _L1_ffn_in['sw_down']}
    _x0 = _d['L0_attn_a_x']
    _d['L0_attn_a_x'] = jax.random.normal(jax.random.fold_in(jax.random.key(seed), 1), (2, 1024, 256), dtype=_x0.dtype)
    del _x0
    return _d

def reference(L0_attn_a_x, L0_attn_a_Wq, L0_attn_a_Wk, L0_attn_a_Wv, L0_attn_a_Wo, L0_attn_a_b_out, L0_attn_b_W_in, L0_attn_b_b_in, L0_attn_b_W_out, L0_attn_b_b_out, L0_ffn_Wr, L0_ffn_br, L0_ffn_Wg, L0_ffn_Wu, L0_ffn_Wd, L1_attn_a_Wq, L1_attn_a_bq, L1_attn_a_Wk, L1_attn_a_bk, L1_attn_a_Wv, L1_attn_a_bv, L1_attn_a_Wo, L1_attn_a_bo, L1_attn_b_Wq, L1_attn_b_bq, L1_attn_b_Wk, L1_attn_b_bk, L1_attn_b_Wv, L1_attn_b_bv, L1_attn_b_Wo, L1_attn_b_bo, L1_ffn_gate_w, L1_ffn_w_gate, L1_ffn_w_up, L1_ffn_w_down, L1_ffn_sw_gate, L1_ffn_sw_up, L1_ffn_sw_down):

    def _L0_attn_a_ref(x, Wq, Wk, Wv, Wo, b_out):
        import jax, jax.numpy as jnp
        import numpy as np
        D_MODEL = 256
        N_HEADS = 32
        N_KV_HEADS = 8
        HEAD_DIM = D_MODEL // N_HEADS
        N_GROUPS = N_HEADS // N_KV_HEADS
        THETA = 10000.0

        def _rope_tables(T, dim):
            inv_freq = 1.0 / THETA ** (jnp.arange(0, dim, 2, dtype=jnp.float32) / dim)
            t = jnp.arange(T, dtype=jnp.float32)
            freqs = jnp.outer(t, inv_freq)
            return (jnp.cos(freqs), jnp.sin(freqs))

        def _apply_rope(x, cos, sin):
            half = x.shape[-1] // 2
            x1, x2 = (x[..., :half], x[..., half:])
            c = cos[None, None, :, :]
            s = sin[None, None, :, :]
            return jnp.concatenate([x1 * c - x2 * s, x2 * c + x1 * s], axis=-1)
        b, T, d = x.shape
        hd = HEAD_DIM
        q = (x @ Wq).reshape(b, T, N_HEADS, hd).transpose(0, 2, 1, 3)
        k = (x @ Wk).reshape(b, T, N_KV_HEADS, hd).transpose(0, 2, 1, 3)
        v = (x @ Wv).reshape(b, T, N_KV_HEADS, hd).transpose(0, 2, 1, 3)
        cos, sin = _rope_tables(T, hd)
        q = _apply_rope(q, cos, sin)
        k = _apply_rope(k, cos, sin)
        qg = q.reshape(b, N_KV_HEADS, N_GROUPS, T, hd)
        scores = jnp.einsum('bkgtd,bksd->bkgts', qg, k) / jnp.sqrt(jnp.asarray(hd, x.dtype))
        causal = jnp.tril(jnp.ones((T, T), dtype=bool))
        scores = jnp.where(causal[None, None, None, :, :], scores, jnp.asarray(-jnp.inf, x.dtype))
        attn = jax.nn.softmax(scores, axis=-1)
        ctx = jnp.einsum('bkgts,bksd->bkgtd', attn, v)
        ctx = ctx.reshape(b, N_HEADS, T, hd).transpose(0, 2, 1, 3).reshape(b, T, d)
        return ctx @ Wo + b_out

    def _L0_attn_b_ref(X, W_in, b_in, W_out, b_out):
        import jax, jax.numpy as jnp
        import numpy as np
        ROPE_THETA = 10000.0

        def rope(t, rot_dim):
            S = t.shape[-2]
            half = rot_dim // 2
            inv_freq = 1.0 / ROPE_THETA ** (jnp.arange(0, rot_dim, 2, dtype=jnp.float32) / rot_dim)
            freqs = jnp.arange(S, dtype=jnp.float32)[:, None] * inv_freq[None, :]
            freqs = jnp.repeat(freqs, 2, axis=-1)
            cos, sin = (jnp.cos(freqs), jnp.sin(freqs))
            t_rot, t_pass = (t[..., :rot_dim], t[..., rot_dim:])
            x = t_rot.reshape(*t_rot.shape[:-1], half, 2)
            rh = jnp.stack([-x[..., 1], x[..., 0]], axis=-1).reshape(t_rot.shape)
            t_rot = t_rot * cos + rh * sin
            return jnp.concatenate([t_rot, t_pass], axis=-1)

        def feature_map(x):
            norm = jnp.sqrt(jnp.sum(x * x, axis=-1, keepdims=True))
            return x / jnp.maximum(norm, 1e-12)
        D = X.shape[-1]
        QKV = jnp.einsum('bsd,ed->bse', X, W_in) + b_in
        Q, K, V = jnp.split(QKV, 3, axis=-1)
        rot_dim = D // 2
        Q = rope(Q, rot_dim)
        K = rope(K, rot_dim)
        A = jnp.sum(feature_map(K) * V, axis=-2)
        Y = A[:, None, :] * Q
        Y = jnp.einsum('bsd,ed->bse', Y, W_out) + b_out
        return Y + X

    def _L0_ffn_ref(hidden_states, Wr, br, Wg, Wu, Wd):
        import jax, jax.numpy as jnp
        import numpy as np
        D_MODEL = 256
        D_FF = 1024
        N_EXPERTS = 4
        B, S = (2, 256)
        b, s, d = hidden_states.shape
        x = hidden_states.reshape(-1, d)
        logits = x @ Wr + br
        probs = jax.nn.softmax(logits, axis=-1)
        top_w, top_idx = jax.lax.top_k(probs, 1)
        g = jnp.einsum('td,edf->tef', x, Wg)
        u = jnp.einsum('td,edf->tef', x, Wu)
        h = jax.nn.silu(g) * u
        y = jnp.einsum('tef,efd->ted', h, Wd)
        sel = jnp.take_along_axis(y, top_idx[:, :, None], axis=1)[:, 0]
        out = sel * top_w
        return out.reshape(b, s, d)

    def _L1_attn_a_ref(x, Wq, bq, Wk, bk, Wv, bv, Wo, bo):
        import jax, jax.numpy as jnp
        import numpy as np
        D_MODEL = 256
        N_HEADS = 16
        D_K = D_MODEL // N_HEADS
        EPS = 1e-06
        b, n, _ = x.shape
        h, d = (N_HEADS, D_K)

        def proj(W, bias):
            y = jnp.einsum('bnm,dm->bnd', x, W) + bias
            return y.reshape(b, n, h, d).transpose(0, 2, 1, 3)
        Q = jax.nn.relu(proj(Wq, bq))
        K = jax.nn.relu(proj(Wk, bk))
        V = proj(Wv, bv)
        pos = jnp.arange(n, dtype=x.dtype)
        decay = jnp.exp(-pos / n)[None, None, :, None]
        Q = Q * decay
        K = K * decay
        KV = jnp.einsum('bhnd,bhne->bhde', K, V)
        Ksum = K.sum(axis=2)
        Z = 1.0 / (jnp.einsum('bhnd,bhd->bhn', Q, Ksum)[..., None] + EPS)
        out = jnp.einsum('bhnd,bhde->bhne', Q, KV) * Z
        out = out.transpose(0, 2, 1, 3).reshape(b, n, h * d)
        return jnp.einsum('bnm,dm->bnd', out, Wo) + bo

    def _L1_attn_b_ref(x, Wq, bq, Wk, bk, Wv, bv, Wo, bo):
        import jax, jax.numpy as jnp
        import numpy as np
        N_EMBD = 256
        Q_HEAD = 16
        KV_HEAD = 4
        HEAD_DIM = N_EMBD // Q_HEAD
        ROPE_BASE = 10000.0

        def _rope(Y, d_rope, base=ROPE_BASE):
            b, h, t, d = Y.shape
            mid = d_rope // 2
            Y1 = Y[:, :mid]
            Y2 = Y[:, mid:]
            Ym1 = jnp.concatenate([Y1, Y2], axis=1)
            Ym2 = jnp.concatenate([-Y2, Y1], axis=1)
            inv = base ** (-2.0 * jnp.arange(d // 2, dtype=jnp.float32) / d)
            theta = jnp.arange(t, dtype=jnp.float32)[:, None] * inv[None, :]
            cos2 = jnp.concatenate([jnp.cos(theta), jnp.cos(theta)], axis=1)
            sin2 = jnp.concatenate([jnp.sin(theta), jnp.sin(theta)], axis=1)
            return Ym1 * cos2 + Ym2 * sin2

        def _attention(x, Wq, bq, Wk, bk, Wv, bv, Wo, bo):
            b, t, n = x.shape
            hd = n // Q_HEAD
            q = x @ Wq.T + bq
            k = x @ Wk.T + bk
            v = x @ Wv.T + bv
            q = q.reshape(b, t, Q_HEAD, hd).transpose(0, 2, 1, 3)
            k = k.reshape(b, t, KV_HEAD, hd).transpose(0, 2, 1, 3)
            v = v.reshape(b, t, KV_HEAD, hd).transpose(0, 2, 1, 3)
            q = _rope(q, N_EMBD)
            k = _rope(k, N_EMBD)
            rep = Q_HEAD // KV_HEAD
            k = jnp.repeat(k, rep, axis=1)
            v = jnp.repeat(v, rep, axis=1)
            scale = jnp.sqrt(jnp.float32(hd))
            att = jnp.einsum('bhqd,bhkd->bhqk', q, k) / scale
            causal = jnp.tril(jnp.ones((t, t), dtype=bool))
            att = jnp.where(causal[None, None], att, -jnp.inf)
            att = jax.nn.softmax(att, axis=-1)
            y = jnp.einsum('bhqt,bhtd->bhqd', att, v)
            y = y.transpose(0, 2, 1, 3).reshape(b, t, n)
            return y @ Wo.T + bo
        return _attention(x, Wq, bq, Wk, bk, Wv, bv, Wo, bo)

    def _L1_ffn_ref(hidden_states, gate_w, w_gate, w_up, w_down, sw_gate, sw_up, sw_down):
        import jax, jax.numpy as jnp
        import numpy as np
        B, S, D = (4, 64, 256)
        E, K, H = (8, 2, 176)
        HS = 2 * 176
        ALPHA = 0.001
        W_SCALE = 0.02

        def _moe_forward(hidden_states, gate_w, w_gate, w_up, w_down, sw_gate, sw_up, sw_down):
            b, s, d = hidden_states.shape
            x = hidden_states.reshape(-1, d)
            T = x.shape[0]
            logits = x @ gate_w
            scores = jax.nn.softmax(logits, axis=-1)
            topk_w, topk_idx = jax.lax.top_k(scores, K)
            mask = jax.nn.one_hot(topk_idx, E, dtype=scores.dtype).sum(axis=1)
            ce = mask.mean(axis=0)
            Pi = scores.mean(axis=0)
            aux_loss = (Pi * ce * E).sum() * ALPHA
            comb = jnp.zeros((T, E), dtype=x.dtype)
            comb = comb.at[jnp.arange(T)[:, None], topk_idx].add(topk_w)
            g = jax.nn.silu(jnp.einsum('td,edh->teh', x, w_gate)) * jnp.einsum('td,edh->teh', x, w_up)
            routed = jnp.einsum('teh,ehd,te->td', g, w_down, comb)
            shared = jax.nn.silu(x @ sw_gate) * (x @ sw_up) @ sw_down
            out = (routed + shared).reshape(b, s, d)
            return (out, aux_loss)
        out, _aux = _moe_forward(hidden_states, gate_w, w_gate, w_up, w_down, sw_gate, sw_up, sw_down)
        return out
    x = L0_attn_a_x
    x = x + _L0_attn_a_ref(_layernorm(x, axis=-1), L0_attn_a_Wq, L0_attn_a_Wk, L0_attn_a_Wv, L0_attn_a_Wo, L0_attn_a_b_out)
    x = x + _L0_ffn_ref(_layernorm(x, axis=-1), L0_ffn_Wr, L0_ffn_br, L0_ffn_Wg, L0_ffn_Wu, L0_ffn_Wd)
    x = x + _L0_attn_b_ref(_layernorm(x, axis=-1), L0_attn_b_W_in, L0_attn_b_b_in, L0_attn_b_W_out, L0_attn_b_b_out)
    x = x + _L0_ffn_ref(_layernorm(x, axis=-1), L0_ffn_Wr, L0_ffn_br, L0_ffn_Wg, L0_ffn_Wu, L0_ffn_Wd)
    x = x + _L1_attn_a_ref(_layernorm(x, axis=-1), L1_attn_a_Wq, L1_attn_a_bq, L1_attn_a_Wk, L1_attn_a_bk, L1_attn_a_Wv, L1_attn_a_bv, L1_attn_a_Wo, L1_attn_a_bo)
    x = x + _L1_ffn_ref(_layernorm(x, axis=-1), L1_ffn_gate_w, L1_ffn_w_gate, L1_ffn_w_up, L1_ffn_w_down, L1_ffn_sw_gate, L1_ffn_sw_up, L1_ffn_sw_down)
    x = x + _L1_attn_b_ref(_layernorm(x, axis=-1), L1_attn_b_Wq, L1_attn_b_bq, L1_attn_b_Wk, L1_attn_b_bk, L1_attn_b_Wv, L1_attn_b_bv, L1_attn_b_Wo, L1_attn_b_bo)
    x = x + _L1_ffn_ref(_layernorm(x, axis=-1), L1_ffn_gate_w, L1_ffn_w_gate, L1_ffn_w_up, L1_ffn_w_down, L1_ffn_sw_gate, L1_ffn_sw_up, L1_ffn_sw_down)
    return x

_drawn_inputs = setup_inputs


def setup_inputs(seed=0):
    import zlib

    import numpy as np

    out = dict(_drawn_inputs(seed))
    spreads = {'L0_attn_b_b_in': (0.0, 0.1),
     'L0_attn_b_b_out': (0.0, 0.1),
     'L0_ffn_br': (0.0, 0.755),
     'L1_attn_a_bq': (0.0, 0.8),
     'L1_attn_a_bk': (0.0, 0.8),
     'L1_attn_a_bv': (0.0, 0.1),
     'L1_attn_a_bo': (0.0, 0.1)}
    factors = {'L0_attn_a_b_out': 3.724,
     'L0_ffn_Wr': 3.902,
     'L0_ffn_Wg': 3.26,
     'L0_ffn_Wu': 3.225,
     'L0_ffn_Wd': 3.227,
     'L1_attn_a_Wq': 3.292,
     'L1_attn_b_bq': 54.079,
     'L1_attn_b_bk': 56.366,
     'L1_attn_b_bv': 8.0,
     'L1_attn_b_bo': 8.0,
     'L1_ffn_gate_w': 8.0,
     'L1_ffn_w_gate': 8.0,
     'L1_ffn_w_up': 8.0,
     'L1_ffn_w_down': 8.0,
     'L1_ffn_sw_gate': 2.934,
     'L1_ffn_sw_up': 2.899,
     'L1_ffn_sw_down': 2.897}
    for name, (base, spread) in spreads.items():
        noise = np.random.default_rng([zlib.crc32(name.encode()), seed]).standard_normal(out[name].shape)
        drawn = base * np.exp(spread * noise) if base else spread * noise
        out[name] = jnp.asarray(drawn.astype(out[name].dtype))
    for name, factor in factors.items():
        out[name] = (out[name] * factor).astype(out[name].dtype)
    return out
```

```python
from contextlib import ExitStack

import concourse.bass as bass
from concourse import mybir

ALU = mybir.AluOpType
ACT = mybir.ActivationFunctionType
AX_X = mybir.AxisListType.X
F32 = mybir.dt.float32
BF16 = mybir.dt.bfloat16

P = 128
D = 256
FT = D // P
NB, SEQ = 2, 1024
NTOK = NB * SEQ
NT = NTOK // P
BT = SEQ // P
NG = NT // 4
LN_EPS = 1e-5
GQ = 4
QK_COLS = D + D // GQ
NEG = -1e30
KROWS = 96
SROWS = KROWS + 3
STEPS = [(i, j) for i in range(BT) for j in range(i + 1)]
MAX_STEPS = [(0, i, h) for i in range(4) for h in (0, 2)] + [(1, i, h) for i in range(4, 8) for h in range(GQ)]
SLOTS = 3
ST_BANK, ACC_BANK, TURN_BANK = 4, 6, 7


class Core:

    def __init__(self, nc, ctx):
        self.nc, self.ctx, self.shared, self.counted = nc, ctx, {}, {}
        self.x = self.sb("x_res", [P, NT, D], F32)
        self.yn = self.sb("y_norm", [P, NT, D], F32)
        self.yt = self.sb("y_t", [P, FT, NTOK], F32)
        self.cx_pad = self.sb("ctx", [P, NT * D + D], F32)
        self.cx = self.cx_pad[:, 0:NT * D]
        self.stats = self.sb("ln_stats", [P, NT, 6], F32)
        self.mv = self.sb("ln_mv", [P, NT, 2], F32)
        self.rstd = self.sb("ln_rstd", [P, NT], F32)
        self.vareps = self.sb("ln_vareps", [P, NT], F32)
        self.mhalf = self.sb("minus_half", [P, NT], F32)
        self.half = self.sb("plus_half", [P, NT], F32)
        self.identf = self.sb("identf", [P, P], F32)
        self.identb = self.sb("identb", [P, P], BF16)
        self.region = {"w": self.sb("region_w", [P, 24576], F32), "a": self.sb("region_a", [P, 11450], F32)}
        self.psum = ctx.enter_context(nc.psum_tensor("psum", [P, 8, 512], F32))
        self.bank = [self.psum[:, i, :] for i in range(8)]

    def sb(self, name, shape, dt):
        return self.ctx.enter_context(self.nc.sbuf_tensor(name, shape, dt))

    def sem(self, name):
        return self.ctx.enter_context(self.nc.semaphore(name))

    def shared_sem(self, name):
        if name not in self.shared:
            self.shared[name] = self.sem(name)
        return self.shared[name]


class Carve:

    def __init__(self, region, at=0):
        self.region, self.at = region, at

    def take(self, free, dt=F32, parts=P):
        n = 1
        for f in free:
            n *= f
        words = n if dt == F32 else (n + 1) // 2
        v = self.region[0:parts, self.at:self.at + words]
        self.at += words
        assert self.at <= self.region.shape[1], self.at
        if dt != F32:
            v = v.bitcast(dt)
        if len(free) == 2:
            v = v.rearrange("p (a b) -> p a b", a=free[0])
        if len(free) == 3:
            v = v.rearrange("p (a b c) -> p a b c", a=free[0], b=free[1])
        return v


def over(ap, axis, n):
    shape = list(ap.shape)
    return ap.unsqueeze(axis).to_broadcast(shape[:axis] + [n] + shape[axis:])


class Counted:

    def __init__(self, sem, base):
        self.sem, self.base = sem, base

    def at(self, n):
        return n + self.base if self.base else n


class Stage:

    def count(self, c, kind, **totals):
        counted = []
        for name, total in totals.items():
            key = f"{kind}_{name}"
            sem, base = c.counted.get(key) or (c.sem(key), 0)
            counted.append(Counted(sem, base))
            c.counted[key] = (sem, base + total)
        return counted

    def sync(self, sp): pass
    def gpsimd(self, pool): pass
    def scalar(self, act): pass
    def tensor(self, pe): pass
    def vector(self, dve): pass


class Start(Stage):

    def __init__(self, c, x, identf, identb):
        self.c, self.x_dram, self.identf, self.identb = c, x, identf, identb
        self.x_in = c.sem("x_in")
        self.const_in = c.sem("const_in")
        self.consts = c.sem("consts_set")

    def sync(self, sp):
        c = self.c
        sp.dma_start(c.identf[:, :], self.identf).then_inc(self.const_in, 16)
        sp.dma_start(c.identb[:, :], self.identb).then_inc(self.const_in, 16)
        x = self.x_dram.rearrange("b (t p) d -> p (b t) d", p=P)
        for g in range(NG):
            sp.dma_start(c.x[:, 4 * g:4 * g + 4, :], x[:, 4 * g:4 * g + 4, :]).then_inc(self.x_in, 16)

    def gpsimd(self, pool):
        c = self.c
        pool.memset(c.mhalf[:, :], -0.5).then_inc(self.consts, 1)
        pool.memset(c.half[:, :], 0.5).then_inc(self.consts, 1)
        pool.wait_ge(self.consts, 2)

    def vector(self, dve):
        dve.wait_ge(self.x_in, 16 * NG)

    def tensor(self, pe):
        pe.wait_ge(self.const_in, 32)


class LayerNorm(Stage):


    def __init__(self, c, k):
        self.c, self.k = c, k
        self.stat = c.shared_sem("ln_stat")
        self.aggr = c.shared_sem("ln_aggr")
        self.veps = c.shared_sem("ln_veps")
        self.rstd = c.shared_sem("ln_rstd")
        self.norm = c.shared_sem("ln_norm")
        self.turned = c.shared_sem("ln_turned")
        self.yt0 = c.shared_sem("ln_yt0")
        self.yt1 = c.shared_sem("ln_yt1")

    def ready(self, eng, g):
        eng.wait_ge(self.yt0, NG * self.k + g + 1)
        eng.wait_ge(self.yt1, NG * self.k + g + 1)

    def normed(self, eng, t):
        eng.wait_ge(self.norm, NT * self.k + t + 1)

    def vector(self, dve):
        c, k = self.c, self.k
        for t in range(NT):
            dve.bn_stats(c.stats[:, t, :], c.x[:, t, :]).then_inc(self.stat, 1)
        for t in range(NT):
            dve.wait_ge(self.stat, NT * k + t + 1)
            dve.bn_aggr(c.mv[:, t, :], c.stats[:, t, :]).then_inc(self.aggr, 1)

        def copies(g):
            dve.wait_ge(self.turned, FT * (NG * k + g + 1))
            dve.tensor_copy(c.yt[:, 1, 512 * g:512 * g + 512], c.bank[5 + 2 * (g % 2)][:, :]).then_inc(self.yt1, 1)

        for g in range(NG):
            dve.wait_ge(self.rstd, NG * k + g + 1)
            for t in range(4 * g, 4 * g + 4):
                dve.tensor_scalar(c.yn[:, t, :], c.x[:, t, :], c.mv[:, t, 0:1], c.rstd[:, t:t + 1],
                                  ALU.subtract, ALU.mult).then_inc(self.norm, 1)
            if g:
                copies(g - 1)
        copies(NG - 1)

    def gpsimd(self, pool):
        c, k = self.c, self.k
        for g in range(NG):
            s = slice(4 * g, 4 * g + 4)
            pool.wait_ge(self.aggr, NT * k + 4 * g + 4)
            pool.tensor_scalar(c.vareps[:, s], c.mv[:, s, 1], LN_EPS, None, ALU.add).then_inc(self.veps, 1)
            pool.wait_ge(self.veps, NG * k + g + 1)
            pool.tensor_tensor(c.rstd[:, s], c.vareps[:, s], c.mhalf[:, s], ALU.pow).then_inc(self.rstd, 1)

    def tensor(self, pe):
        c, k = self.c, self.k
        for g in range(NG):
            self.normed(pe, 4 * g + 3)
            for f in range(FT):
                if g >= 2:
                    pe.wait_ge([self.yt0, self.yt1][f], NG * k + g - 1)
                for q in range(4):
                    mm = pe.transpose(c.bank[4 + 2 * (g % 2) + f][:, P * q:P * q + P],
                                      c.yn[:, 4 * g + q, P * f:P * f + P], c.identf[:, :])
                mm.then_inc(self.turned, 1)

    def scalar(self, act):
        c, k = self.c, self.k
        for g in range(NG):
            act.wait_ge(self.turned, FT * (NG * k + g) + 1)
            act.activation(c.yt[:, 0, 512 * g:512 * g + 512], c.bank[4 + 2 * (g % 2)][:, :],
                           ACT.Copy).then_inc(self.yt0, 1)


class Project(Stage):


    def __init__(self, c, k, source, w, before):
        self.c, self.k, self.source, self.w, self.before = c, k, source, w, before
        self.turned = c.shared_sem("project_turned")
        self.ot0 = c.shared_sem("project_ot0")
        self.ot1 = c.shared_sem("project_ot1")
        self.prod = c.shared_sem("project_prod")
        self.added = c.shared_sem("project_added")

    def tensor(self, pe):
        c, k = self.c, self.k

        def turn(g):
            self.before(pe, g)
            for f in range(FT):
                if g >= 2:
                    pe.wait_ge([self.ot0, self.ot1][f], NG * k + g - 1)
                for q in range(4):
                    mm = pe.transpose(c.bank[4 + 2 * (g % 2) + f][:, P * q:P * q + P],
                                      self.source(4 * g + q, f), c.identf[:, :])
                mm.then_inc(self.turned, 1)

        def multiply(g):
            pe.wait_ge(self.ot0, NG * k + g + 1)
            pe.wait_ge(self.ot1, NG * k + g + 1)
            for q in range(4):
                t = 4 * g + q
                if t >= 4:
                    pe.wait_ge(self.added, NT * k + t - 3)
                for f in range(FT):
                    mm = pe.matmul(c.bank[q][:, 0:D], c.yt[:, f, P * t:P * t + P], self.w(t, f),
                                   start=(f == 0), stop=(f == FT - 1))
                mm.then_inc(self.prod, 1)

        for g in range(NG):
            turn(g)
            if g:
                multiply(g - 1)
        multiply(NG - 1)

    def scalar(self, act):
        c, k = self.c, self.k
        for g in range(NG):
            act.wait_ge(self.turned, FT * (NG * k + g) + 1)
            act.activation(c.yt[:, 0, 512 * g:512 * g + 512], c.bank[4 + 2 * (g % 2)][:, :],
                           ACT.Copy).then_inc(self.ot0, 1)

    def vector(self, dve):
        c, k = self.c, self.k

        def adds(g):
            for t in range(4 * g, 4 * g + 4):
                dve.wait_ge(self.prod, NT * k + t + 1)
                dve.tensor_tensor(c.x[:, t, :], c.bank[t % 4][:, 0:D], c.x[:, t, :], ALU.add).then_inc(self.added, 1)

        for g in range(NG):
            dve.wait_ge(self.turned, FT * (NG * k + g + 1))
            dve.tensor_copy(c.yt[:, 1, 512 * g:512 * g + 512], c.bank[5 + 2 * (g % 2)][:, :]).then_inc(self.ot1, 1)
            if g:
                adds(g - 1)
        adds(NG - 1)
        dve.wait_ge(self.added, NT * (k + 1))


class Attention(Stage):

    def __init__(self, c, name, ln, hd, w, wo, tables, bias, bias_out, mask_q, mask_k):
        self.c, self.ln, self.hd = c, ln, hd
        self.nkv = D // GQ // hd
        self.units = NB * self.nkv
        self.scale = float(hd) ** -0.5
        self.dram = dict(w=w, wo=wo, tables=tables, bias=bias, bias_out=bias_out, mq=mask_q, mk=mask_k)
        pairs = [(a, b) for a in range(3) for b in range(3)]
        self.terms = pairs if hd == 8 else [(a, b) for a, b in pairs if a + b <= 2]
        assert len(self.terms) * hd <= KROWS
        nc = c.nc
        self.q_dram = nc.dram_tensor(name + "_q", [3, NB * D, SEQ], BF16, kind="Internal").ap()
        self.k_dram = nc.dram_tensor(name + "_k", [3, NB * D // GQ, SEQ], BF16, kind="Internal").ap()
        r = Carve(c.region["a"])
        self.wo = r.take([FT, D])
        self.v = r.take([self.units, BT, hd])
        self.bias_out = r.take([D])
        self.mq = r.take([P], BF16)
        self.mk = r.take([P], BF16)
        self.kp = [r.take([SEQ], BF16) for _ in range(SLOTS)]
        self.vp = [r.take([BT, 32]) for _ in range(SLOTS)]
        self.mparts = [r.take([4, P], BF16) for _ in range(2)]
        yn, yt = Carve(c.yn.rearrange("p t d -> p (t d)")), Carve(c.yt[:, 0, :])
        self.qp = [at.take([GQ, SEQ], BF16) for at in (yn, yn, yt)]
        both = r.at
        self.w = r.take([FT, 3 * P])
        self.cos = r.take([BT, hd])
        self.sin = r.take([BT, hd])
        self.bias = r.take([3 * P])
        self.rot = [r.take([QK_COLS]) for _ in range(2)]
        self.rotb = [r.take([QK_COLS]) for _ in range(2)]
        self.qk = [r.take([QK_COLS]) for _ in range(4)]
        self.parts = [r.take([3, 512], BF16) for _ in range(2)]
        self.rest = [r.take([512]) for _ in range(2)]
        r = Carve(c.region["a"], both)
        self.p = [r.take([GQ, P]) for _ in range(3)]
        self.acc = r.take([512])
        self.mx = [r.take([4, GQ]) for _ in range(2)]
        self.mneg = [r.take([4, GQ]) for _ in range(2)]
        self.mrest = [r.take([4, GQ]) for _ in range(2)]
        self.mrows = [r.take([512], BF16) for _ in range(2)]
        self.rden = r.take([4, GQ])
        u, n = self.units, len(self.terms)
        (self.w_in, self.wo_in, self.q_in, self.k_in, self.prod, self.rotm, self.qk_done, self.v_done,
         self.turned, self.part1, self.rest_done, self.part2, self.part3, self.parts_out0, self.parts_out1,
         self.pads, self.vp_in, self.max_prod, self.max_done, self.m_neg, self.m_chain, self.m_in0, self.m_in1,
         self.st, self.exp, self.pv, self.acc_out, self.tb, self.den, self.drained, self.biased) = \
            self.count(c, "attn", w_in=64, wo_in=64, q_in=16 * n * u, k_in=48 * u, prod=NT, rotm=3 * NT if hd == 8 else NT + 1,
            qk_done=NT, v_done=NT, turned=3 * NG, part1=3 * NG, rest_done=3 * NG, part2=3 * NG, part3=3 * NG,
            parts_out0=24 * NG, parts_out1=24 * NG, pads=2 + 5 * SLOTS, vp_in=u, max_prod=len(MAX_STEPS) * u,
            max_done=len(MAX_STEPS) * u, m_neg=10 * u, m_chain=2 * u, m_in0=16 * u, m_in1=16 * u,
            st=len(STEPS) * u, exp=len(STEPS) * u, pv=len(STEPS) * u, acc_out=2 * u, tb=4 * u, den=2 * u,
            drained=2 * u, biased=NT)
        self.parts_out = [self.parts_out0, self.parts_out1]
        self.m_in = [self.m_in0, self.m_in1]

    def all_parts_out(self, eng):
        for s in self.parts_out:
            eng.wait_ge(s.sem, s.at(16 * 3 * NG // 2))

    def first_parts_out(self, eng):
        for s in self.parts_out:
            eng.wait_ge(s.sem, s.at(16 * 3 * NG // 2 // NB))

    def every_unit(self, eng, unit, ahead=1):
        unit(0, 0, left=self.units - 1)
        rounds = (self.units - 1 - ahead) // SLOTS
        with eng.Fori(0, rounds) as k:
            for i in range(1, SLOTS + 1):
                unit(k * SLOTS + i, i % SLOTS, left=ahead)
        for u in range(1 + rounds * SLOTS, self.units):
            unit(u, u % SLOTS, left=self.units - 1 - u)


    def turned_max(self, u, half):
        if half == 1:
            return u * 4 + 2
        return 1 if isinstance(u, int) and u == 0 else u * 4

    def turned_out(self, u, half):
        if half == 0:
            return u * 4 + 3
        return u * 4 + (4 if isinstance(u, int) and u == self.units - 1 else 5)

    def sync(self, sp):
        d, hd = self.dram, self.hd
        for dst, src in ((self.w, d["w"].rearrange("(f p) n -> p f n", p=P)),
                         (self.cos, d["tables"][0].rearrange("(t p) n -> p t n", p=P)),
                         (self.sin, d["tables"][1].rearrange("(t p) n -> p t n", p=P)),
                         (self.bias, d["bias"].partition_broadcast(P))):
            sp.dma_start(dst, src).then_inc(self.w_in.sem, 16)
        for dst, src in ((self.wo, d["wo"].rearrange("(f p) n -> p f n", p=P)),
                         (self.bias_out, d["bias_out"].partition_broadcast(P)),
                         (self.mq, d["mq"]), (self.mk, d["mk"])):
            sp.dma_start(dst, src).then_inc(self.wo_in.sem, 16)
        def load(u, slot):
            for n, (a, b) in enumerate(self.terms):
                src = self.q_dram[a, bass.ds(u * (GQ * hd), GQ * hd), :].rearrange("(h d) t -> d h t", d=hd)
                sp.dma_start(self.qp[slot][hd * n:hd * n + hd, :, :], src).then_inc(self.q_in.sem, 16)
            row = 0
            for a in range(3):
                n = sum(1 for term in self.terms if term[0] == a)
                sp.dma_start(self.kp[slot][row:row + hd * n, :], self.k_dram[0:n, bass.ds(u * hd, hd), :])\
                    .then_inc(self.k_in.sem, 16)
                row += hd * n

        def load_max(u, half, slot):
            sp.wait_ge(self.m_chain.sem, self.m_chain.at(u * 2 + half + 1))
            sp.dma_start(self.qp[slot][KROWS:SROWS, :, 512 * half:512 * half + 512],
                         self.mrows[half][0:3 * GQ, :]).then_inc(self.m_in[half].sem, 16)

        for n in range(3 * NG):
            g, f = divmod(n, 3)
            b, at = divmod(512 * g, SEQ)
            rows = P if f < FT else QK_COLS - D
            if f < FT:
                dst = self.q_dram[:, b * D + P * f:b * D + P * f + P, at:at + 512]
            else:
                dst = self.k_dram[:, b * rows:b * rows + rows, at:at + 512]
            sp.wait_ge(self.part1.sem, self.part1.at(n + 1))
            sp.wait_ge(self.part2.sem, self.part2.at(n + 1))
            sp.wait_ge(self.part3.sem, self.part3.at(n + 1))
            sp.dma_start(dst.rearrange("a f t -> f a t"), self.parts[n % 2][0:rows, :, :]).then_inc(self.parts_out[n % 2].sem, 16)
            if n == 3 * NG - 4:
                self.first_parts_out(sp)
                sp.wait_ge(self.pads.sem, self.pads.at(2 + 5 * 2))
                load(0, 0)
        sp.wait_ge(self.q_in.sem, self.q_in.at(16 * len(self.terms)))
        sp.wait_ge(self.k_in.sem, self.k_in.at(48))
        load(1, 1)
        load_max(0, 0, 0)
        self.all_parts_out(sp)
        sp.wait_ge(self.pads.sem, self.pads.at(2 + 5 * SLOTS))

        def unit(u, slot, left):
            if left > 1:
                sp.wait_ge(self.max_prod.sem, self.max_prod.at((u + 1) * len(MAX_STEPS) + 1))
                load(u + 2, (slot + 2) % SLOTS)
            load_max(u, 1, slot)
            if left:
                load_max(u + 1, 0, (slot + 1) % SLOTS)

        self.every_unit(sp, unit, ahead=2)

    def gpsimd(self, pool):
        c, hd = self.c, self.hd
        self.ln.ready(pool, NG - 1)
        pads = [(parts, 0.0) for parts in self.mparts]
        for slot in range(SLOTS):
            pads += [(self.vp[slot], 0.0), (self.vp[slot][:, :, hd:hd + 1], 1.0),
                     (self.kp[slot][64:KROWS, :], 0.0), (self.kp[slot][KROWS:SROWS, :], 1.0),
                     (self.qp[slot][64:SROWS, :, :], 0.0)]
        for n, (rows, value) in enumerate(pads):
            if n == 12:
                pool.wait_ge(self.prod.sem, self.prod.at(NT))
            if n:
                pool.wait_ge(self.pads.sem, self.pads.at(n))
            pool.memset(rows, value).then_inc(self.pads.sem, 1)
        pool.wait_ge(self.pads.sem, self.pads.at(len(pads)))
        pool.wait_ge(self.wo_in.sem, self.wo_in.at(64))
        for t in range(NT):
            self.ln.normed(pool, t)
            pool.tensor_tensor(c.x[:, t, :], c.x[:, t, :], self.bias_out, ALU.add).then_inc(self.biased.sem, 1)
        v_flat = self.v.rearrange("p u b d -> p (u b d)")

        def copy_v(u, slot):
            pool.tensor_copy(self.vp[slot][:, :, 0:hd],
                             v_flat[:, bass.ds(u * (BT * hd), BT * hd)].rearrange("p (b d) -> p b d", d=hd))\
                .then_inc(self.vp_in.sem, 1)

        def unit(u, slot, left):
            if left:
                if not (isinstance(u, int) and u == 0):
                    pool.wait_ge(self.pv.sem, self.pv.at(u * len(STEPS)))
                copy_v(u + 1, (slot + 1) % SLOTS)

        pool.wait_ge(self.v_done.sem, self.v_done.at(NT))
        pool.wait_ge(self.pads.sem, self.pads.at(2 + 5 * SLOTS))
        copy_v(0, 0)
        self.every_unit(pool, unit)

    def vector(self, dve):
        c, hd = self.c, self.hd
        heads = QK_COLS // hd
        by_head = lambda z: z.rearrange("p (n d) -> p n d", d=hd)
        dve.wait_ge(self.w_in.sem, self.w_in.at(64))
        if hd != 8:
            dve.tensor_tensor(self.cos, self.cos, self.sin, ALU.add).then_inc(self.rotm.sem, 1)

        def rotate(t):
            bt = t % BT
            z = by_head(c.bank[t % 4][:, 0:QK_COLS])
            zv = by_head(c.bank[t % 4][:, QK_COLS:3 * P])
            a, b, out = self.rot[t % 2], self.rotb[t % 2], by_head(self.qk[t % 4])
            aa, bb = by_head(a), by_head(b)
            cos = over(self.cos[:, bt, :], 1, heads)
            v = self.v[:, (t // BT) * self.nkv:(t // BT + 1) * self.nkv, bt, :]
            dve.wait_ge(self.prod.sem, self.prod.at(t + 1))
            if t >= 4:
                dve.wait_ge(self.turned.sem, self.turned.at(3 * (t // 4)))
            if t >= 2:
                dve.wait_ge(self.qk_done.sem, self.qk_done.at(t - 1))
            if hd == 8:
                h = hd // 2
                dve.tensor_tensor(aa, z, cos, ALU.mult).then_inc(self.rotm.sem, 1)
                dve.tensor_tensor(bb[:, :, 0:h], z[:, :, h:hd], over(self.sin[:, bt, 0:h], 1, heads),
                                  ALU.mult).then_inc(self.rotm.sem, 1)
                dve.tensor_tensor(bb[:, :, h:hd], z[:, :, 0:h], over(self.sin[:, bt, h:hd], 1, heads),
                                  ALU.mult).then_inc(self.rotm.sem, 1)
                dve.tensor_copy(v, zv).then_inc(self.v_done.sem, 1)
                dve.wait_ge(self.rotm.sem, self.rotm.at(3 * t + 3))
                dve.tensor_tensor(out, aa, bb, ALU.add).then_inc(self.qk_done.sem, 1)
            else:
                dve.tensor_tensor(aa, z, by_head(self.bias[:, 0:QK_COLS]), ALU.add).then_inc(self.rotm.sem, 1)
                dve.tensor_tensor(v, zv, by_head(self.bias[:, QK_COLS:3 * P]), ALU.add).then_inc(self.v_done.sem, 1)
                dve.wait_ge(self.rotm.sem, self.rotm.at(t + 2))
                dve.tensor_tensor(out, aa, cos, ALU.mult).then_inc(self.qk_done.sem, 1)

        def cut(n):
            rows = P if n % 3 < FT else QK_COLS - D
            z, parts, rest = c.bank[4 + n % 4][0:rows, :], self.parts[n % 2][0:rows], self.rest[n % 2][0:rows]
            dve.wait_ge(self.part1.sem, self.part1.at(n + 1))
            if n >= 2:
                dve.wait_ge(self.part3.sem, self.part3.at(n - 1))
            dve.tensor_tensor(rest, z, parts[:, 0, :], ALU.subtract).then_inc(self.rest_done.sem, 1)
            dve.wait_ge(self.part2.sem, self.part2.at(n + 1))
            dve.tensor_tensor(parts[:, 2, :], rest, parts[:, 1, :], ALU.subtract).then_inc(self.part3.sem, 1)

        for g in range(NG + 1):
            if g < NG:
                for t in range(4 * g, 4 * g + 4):
                    rotate(t)
            if g:
                for f in range(3):
                    cut(3 * (g - 1) + f)
        self.all_parts_out(dve)

        def maxima(u, k0, k1):
            for k in range(k0, k1):
                half, i, h = MAX_STEPS[k]
                n = (i + 1) * P
                both = c.psum[:, 2 * (k % 2):2 * (k % 2) + 2, :]
                if half == 0:
                    src, dst = both[:, :, 0:n], self.mx[0][:, i, h:h + 2]
                else:
                    src, dst = both.rearrange("p a b -> p (a b)")[:, 0:n], self.mx[1][:, i - 4, h:h + 1]
                dve.wait_ge(self.max_prod.sem, self.max_prod.at(u * len(MAX_STEPS) + k + 1))
                dve.tensor_reduce(dst, src, AX_X, ALU.max).then_inc(self.max_done.sem, 1)

        def split_max(u, half):
            neg, rest = self.mneg[half], self.mrest[half]
            part = [self.mparts[half][:, :, GQ * i:GQ * i + GQ] for i in range(3)]
            done = u * 10 + 5 * half
            dve.wait_ge(self.max_done.sem, self.max_done.at(u * len(MAX_STEPS) + (8 if half == 0 else len(MAX_STEPS))))
            dve.tensor_scalar(neg, self.mx[half], -1.0, None, ALU.mult).then_inc(self.m_neg.sem, 1)
            dve.wait_ge(self.m_neg.sem, self.m_neg.at(done + 1))
            dve.tensor_copy(part[0], neg).then_inc(self.m_neg.sem, 1)
            dve.wait_ge(self.m_neg.sem, self.m_neg.at(done + 2))
            dve.tensor_tensor(rest, neg, part[0], ALU.subtract).then_inc(self.m_neg.sem, 1)
            dve.wait_ge(self.m_neg.sem, self.m_neg.at(done + 3))
            dve.tensor_copy(part[1], rest).then_inc(self.m_neg.sem, 1)
            dve.wait_ge(self.m_neg.sem, self.m_neg.at(done + 4))
            dve.tensor_tensor(part[2], rest, part[1], ALU.subtract).then_inc(self.m_neg.sem, 1)

        def rows_out(u, half):
            dve.wait_ge(self.tb.sem, self.tb.at(self.turned_max(u, half)))
            if not (isinstance(u, int) and u == 0):
                dve.wait_ge(self.m_in[half].sem, self.m_in[half].at(u * 16))
            dve.tensor_copy(self.mrows[half][0:3 * GQ, :],
                            c.bank[TURN_BANK][0:3 * GQ, 0:256].bitcast(BF16)).then_inc(self.m_chain.sem, 1)

        def normalize(u, half):
            z = c.bank[TURN_BANK].rearrange("p (i h e) -> p i h e", i=4, e=32)
            at = u * (GQ * hd) + (u // self.nkv) * (BT * D - D) + 4 * half * D
            dst = c.cx_pad[:, bass.ds(at, 4 * D)].rearrange("p (i n) -> p i n", i=4)[:, :, 0:GQ * hd]
            dve.wait_ge(self.tb.sem, self.tb.at(self.turned_out(u, half)))
            dve.reciprocal(self.rden, z[:, :, :, hd]).then_inc(self.den.sem, 1)
            dve.wait_ge(self.den.sem, self.den.at(u * 2 + half + 1))
            dve.tensor_tensor(dst.rearrange("p i (h d) -> p i h d", d=hd), z[:, :, :, 0:hd],
                              over(self.rden, 3, hd), ALU.mult).then_inc(self.drained.sem, 1)

        def unit(u, slot, left):
            if left:
                maxima(u + 1, 0, 2)
            if not (isinstance(u, int) and u == 0):
                normalize(u - 1, 1)
            rows_out(u, 1)
            if left:
                maxima(u + 1, 2, 8)
                split_max(u + 1, 0)
                maxima(u + 1, 8, 10)
            normalize(u, 0)
            if left:
                maxima(u + 1, 10, 11)
                rows_out(u + 1, 0)
                maxima(u + 1, 11, len(MAX_STEPS))
                split_max(u + 1, 1)

        maxima(0, 0, 8)
        split_max(0, 0)
        rows_out(0, 0)
        maxima(0, 8, len(MAX_STEPS))
        split_max(0, 1)
        self.every_unit(dve, unit)
        normalize(self.units - 1, 1)
        dve.wait_ge(self.biased.sem, self.biased.at(NT))

    def scalar(self, act):
        c = self.c
        for n in range(3 * NG):
            rows = P if n % 3 < FT else QK_COLS - D
            parts, rest = self.parts[n % 2][0:rows], self.rest[n % 2][0:rows]
            act.wait_ge(self.turned.sem, self.turned.at(n + 1))
            if n >= 2:
                act.wait_ge(self.parts_out[n % 2].sem, self.parts_out[n % 2].at(16 * (n // 2)))
            act.activation(parts[:, 0, :], c.bank[4 + n % 4][0:rows, :], ACT.Copy).then_inc(self.part1.sem, 1)
            act.wait_ge(self.rest_done.sem, self.rest_done.at(n + 1))
            act.activation(parts[:, 1, :], rest, ACT.Copy).then_inc(self.part2.sem, 1)
        act.wait_ge(self.pads.sem, self.pads.at(2 + 5 * SLOTS))

        def unit(u, slot, left):
            first = isinstance(u, int) and u == 0
            for s in range(len(STEPS)):
                act.wait_ge(self.st.sem, self.st.at(u * len(STEPS) + s + 1))
                if not (first and s < 3):
                    act.wait_ge(self.pv.sem, self.pv.at(u * len(STEPS) + (s - 2)))
                act.activation(self.p[s % 3].rearrange("p h t -> p (h t)"), c.bank[ST_BANK + s % 2][:, :], ACT.Exp,
                               scale=self.scale).then_inc(self.exp.sem, 1)
                for half, after, steps in ((0, 11, 10), (1, 35, 36)):
                    if s == after:
                        act.wait_ge(self.pv.sem, self.pv.at(u * len(STEPS) + steps))
                        if not (first and half == 0):
                            act.wait_ge(self.tb.sem, self.tb.at(self.turned_out(u, 0) if half else self.turned_out(u - 1, 1)))
                        act.activation(self.acc, c.bank[ACC_BANK][:, :], ACT.Copy).then_inc(self.acc_out.sem, 1)

        self.every_unit(act, unit)

    def tensor(self, pe):
        c, hd = self.c, self.hd
        pe.wait_ge(self.w_in.sem, self.w_in.at(64))

        def turn(g):
            pe.wait_ge(self.qk_done.sem, self.qk_done.at(4 * g + 4))
            self.ln.ready(pe, NG - 1)
            for f in range(3):
                n = 3 * g + f
                rows = P if f < FT else QK_COLS - D
                if n >= 4:
                    pe.wait_ge(self.rest_done.sem, self.rest_done.at(n - 3))
                for q in range(4):
                    mm = pe.transpose(c.bank[4 + n % 4][0:rows, P * q:P * q + P],
                                      self.qk[q][:, P * f:P * f + rows], c.identf[:, :])
                mm.then_inc(self.turned.sem, 1)

        for g in range(NG):
            self.ln.ready(pe, g)
            for t in range(4 * g, 4 * g + 4):
                if t >= 4:
                    pe.wait_ge(self.rotm.sem, self.rotm.at(3 * (t - 3) if hd == 8 else t - 2))
                    pe.wait_ge(self.v_done.sem, self.v_done.at(t - 3))
                for f in range(FT):
                    mm = pe.matmul(c.bank[t % 4][:, 0:3 * P], c.yt[:, f, P * t:P * t + P], self.w[:, f, :],
                                   start=(f == 0), stop=(f == FT - 1))
                mm.then_inc(self.prod.sem, 1)
            if g:
                turn(g - 1)
        turn(NG - 1)

        pe.wait_ge(self.rest_done.sem, self.rest_done.at(3 * NG))
        pe.wait_ge(self.v_done.sem, self.v_done.at(NT))
        pe.wait_ge(self.rotm.sem, self.rotm.at(3 * NT if hd == 8 else NT + 1))
        pe.wait_ge(self.wo_in.sem, self.wo_in.at(64))

        def max_scores(u, k, slot):
            half, i, h = MAX_STEPS[k]
            qp, kp = self.qp[slot], self.kp[slot]
            if k == 0:
                pe.wait_ge(self.q_in.sem, self.q_in.at((u + 1) * (16 * len(self.terms))))
                pe.wait_ge(self.k_in.sem, self.k_in.at((u + 1) * 48))
            if not (isinstance(u, int) and u == 0 and k < 2):
                pe.wait_ge(self.max_done.sem, self.max_done.at(u * len(MAX_STEPS) + (k - 1)))
            for b in range(2):
                bank = c.bank[2 * (k % 2) + b]
                head = h + b if half == 0 else h
                q = qp[0:KROWS, head, P * i:P * i + P]
                lo = 512 * b * half
                n = min(512, (i + 1) * P - lo)
                diag = half == 0 or b == 1
                mm = pe.matmul(bank[:, 0:n], q, kp[0:KROWS, lo:lo + n], start=True, stop=not diag,
                               skip_group_check=True)
                if diag:
                    mm = pe.matmul(bank[:, n - P:n], c.identb[:, :], self.mq, start=False, stop=True,
                                   skip_group_check=True)
            mm.then_inc(self.max_prod.sem, 1)

        def turn_max(u, half):
            pe.wait_ge(self.m_neg.sem, self.m_neg.at(u * 10 + (5 * half + 5)))
            if isinstance(u, int) and u == 0:
                if half == 1:
                    pe.wait_ge(self.m_chain.sem, self.m_chain.at(1))
            else:
                pe.wait_ge(self.drained.sem, self.drained.at(u * 2 if half else u * 2 - 1))
            for i in range(4):
                mm = pe.transpose(c.bank[TURN_BANK].bitcast(BF16)[:, P * i:P * i + P], self.mparts[half][:, i, :],
                                  c.identb[:, :])
            mm.then_inc(self.tb.sem, 1)

        def turn_out(u, half):
            pe.wait_ge(self.acc_out.sem, self.acc_out.at(u * 2 + half + 1))
            if half == 1 and isinstance(u, int) and u == self.units - 1:
                pe.wait_ge(self.drained.sem, self.drained.at(u * 2 + 1))
            else:
                pe.wait_ge(self.m_chain.sem, self.m_chain.at(u * 2 + half + 2))
            for i in range(4):
                mm = pe.transpose(c.bank[TURN_BANK][:, P * i:P * i + P], self.acc[:, P * i:P * i + P],
                                  c.identf[:, :])
            mm.then_inc(self.tb.sem, 1)

        def scores(u, s, slot, first):
            i, j = STEPS[s]
            if s == 0 or s == 10:
                rows_in = self.m_in[0 if s == 0 else 1]
                pe.wait_ge(rows_in.sem, rows_in.at((u + 1) * 16))
            if not (first and s < 2):
                pe.wait_ge(self.exp.sem, self.exp.at(u * len(STEPS) + (s - 1)))
            bank = c.bank[ST_BANK + s % 2]
            mm = pe.matmul(bank[:, :], self.kp[slot][0:SROWS, P * j:P * j + P],
                           self.qp[slot][0:SROWS, :, P * i:P * i + P],
                           start=True, stop=(j < i))
            if i == j:
                mm = pe.matmul(bank[:, :], c.identb[:, :], over(self.mk, 1, GQ), start=False, stop=True)
            mm.then_inc(self.st.sem, 1)

        def values(u, s, slot, first):
            i, j = STEPS[s]
            if s == 0:
                pe.wait_ge(self.vp_in.sem, self.vp_in.at(u + 1))
            if s == 10 or (s == 0 and not first):
                pe.wait_ge(self.acc_out.sem, self.acc_out.at(u * 2 + (1 if s else 0)))
            pe.wait_ge(self.exp.sem, self.exp.at(u * len(STEPS) + (s + 1)))
            for h in range(GQ):
                mm = pe.matmul(c.bank[ACC_BANK][32 * h:32 * h + 32, P * (i % 4):P * (i % 4) + P],
                               self.vp[slot][:, j, :], self.p[s % 3][:, h, :], start=(j == 0), stop=(j == i))
            mm.then_inc(self.pv.sem, 1)

        def unit(u, slot, left):
            first = isinstance(u, int) and u == 0
            for s in range(len(STEPS) + 2):
                if s < len(STEPS):
                    scores(u, s, slot, first)
                if s == 2 and not first:
                    turn_out(u - 1, 1)
                if s == 3:
                    turn_max(u, 1)
                if s == 14:
                    turn_out(u, 0)
                if s == 16 and left:
                    turn_max(u + 1, 0)
                if left and s < len(STEPS) and s % 3 < 2:
                    max_scores(u + 1, s - s // 3, (slot + 1) % SLOTS)
                if s >= 2:
                    values(u, s - 2, slot, first)

        for k in range(8):
            max_scores(0, k, 0)
        turn_max(0, 0)
        for k in range(8, len(MAX_STEPS)):
            max_scores(0, k, 0)
        self.every_unit(pe, unit)
        turn_out(self.units - 1, 1)

    def source(self, t, f):
        return self.c.cx[:, D * t + P * f:D * t + P * f + P]

    def finished(self, pe, g):
        if g == 0:
            pe.wait_ge(self.drained.sem, self.drained.at(2 * self.units))


class Gate(Stage):

    def __init__(self, c, name, ln, experts, top, shared, w, bias, carve):
        self.c, self.ln, self.e, self.top, self.shared, self.dram_w, self.dram_b = c, ln, experts, top, shared, w, bias
        self.n = experts + shared
        r = carve
        self.w = r.take([FT, experts])
        self.b = r.take([experts])
        self.order = r.take([experts])
        t = lambda: r.take([NT, experts])
        self.z, self.pr, self.left, self.hit, self.comb, self.eq = t(), t(), t(), t(), t(), t()
        self.s = r.take([NT])
        self.rs = r.take([NT])
        self.cut = r.take([NT, 3, self.n], BF16)
        self.rest = r.take([NT, self.n])
        self.rows = r.take([NTOK], BF16)
        (self.w_in, self.prod, self.step, self.shifted, self.exp, self.ready_cut, self.turned, self.rows_set,
         self.orders) = \
            self.count(c, "gate", w_in=16 * (1 + (bias is not None)), prod=1, step=14 + (top > 1) + 7 * (top - 1) + 2 * shared, shifted=1,
            exp=1, ready_cut=1, turned=1, rows_set=2, orders=experts + 1)

    def sync(self, sp):
        sp.dma_start(self.w, self.dram_w.rearrange("(f p) e -> p f e", p=P)).then_inc(self.w_in.sem, 16)
        if self.dram_b is not None:
            sp.dma_start(self.b, self.dram_b.partition_broadcast(P)).then_inc(self.w_in.sem, 16)

    def w_loaded(self, eng):
        eng.wait_ge(self.w_in.sem, self.w_in.at(32 if self.dram_b is not None else 16))

    def gpsimd(self, pool):
        for e in range(self.e):
            pool.memset(self.order[:, e:e + 1], float(self.e - e)).then_inc(self.orders.sem, 1)
        pool.memset(self.rows, 0.0).then_inc(self.orders.sem, 1)

    def tensor(self, pe):
        c, e = self.c, self.e
        self.w_loaded(pe)
        for g in range(NG):
            self.ln.ready(pe, g)
            for t in range(4 * g, 4 * g + 4):
                for f in range(FT):
                    mm = pe.matmul(c.bank[2][:, e * t:e * t + e], c.yt[:, f, P * t:P * t + P], self.w[:, f, :],
                                   start=(f == 0), stop=(f == FT - 1))
        mm.then_inc(self.prod.sem, 1)

    def turn(self, pe):
        c = self.c
        pe.wait_ge(self.ready_cut.sem, self.ready_cut.at(1))
        for t in range(NT):
            bank = c.bank[4 + t // 8].bitcast(BF16)
            mm = pe.transpose(bank[0:3 * self.n, P * (t % 8):P * (t % 8) + P],
                              self.cut[:, t, :, :].rearrange("p a e -> p (a e)"), c.identb[:, :])
        mm.then_inc(self.turned.sem, 1)

    def scalar(self, act):
        act.wait_ge(self.shifted.sem, self.shifted.at(1))
        act.activation(self.pr, self.z, ACT.Exp).then_inc(self.exp.sem, 1)
        act.wait_ge(self.turned.sem, self.turned.at(1))
        act.wait_ge(self.orders.sem, self.orders.at(self.e + 1))
        for h in range(2):
            act.activation(self.rows[0:3 * self.n, 1024 * h:1024 * h + 1024],
                           self.c.bank[4 + h].bitcast(BF16)[0:3 * self.n, :], ACT.Copy).then_inc(self.rows_set.sem, 1)

    def vector(self, dve):
        c, e = self.c, self.e
        count = [0]

        def then(ins):
            count[0] += 1
            ins.then_inc(self.step.sem, 1)
            dve.wait_ge(self.step.sem, self.step.at(count[0]))

        wide = lambda v: over(v, 2, e)
        by_token = lambda v: over(v, 1, NT)
        logits = c.bank[2][:, 0:NT * e].rearrange("p (t e) -> p t e", e=e)
        dve.wait_ge(self.prod.sem, self.prod.at(1))
        self.w_loaded(dve)
        if self.dram_b is not None:
            then(dve.tensor_tensor(self.z, logits, by_token(self.b), ALU.add))
        else:
            then(dve.tensor_copy(self.z, logits))
        then(dve.tensor_reduce(self.s, self.z, AX_X, ALU.max))
        dve.tensor_tensor(self.z, self.z, wide(self.s), ALU.subtract).then_inc(self.shifted.sem, 1)
        dve.wait_ge(self.exp.sem, self.exp.at(1))
        then(dve.tensor_reduce(self.s, self.pr, AX_X, ALU.add))
        then(dve.reciprocal(self.rs, self.s))
        then(dve.tensor_tensor(self.pr, self.pr, wide(self.rs), ALU.mult))
        dve.wait_ge(self.orders.sem, self.orders.at(e + 1))
        left = self.pr
        for k in range(self.top):
            then(dve.tensor_reduce(self.s, left, AX_X, ALU.max))
            then(dve.tensor_tensor(self.eq, left, wide(self.s), ALU.is_equal))
            then(dve.tensor_tensor(self.eq, self.eq, by_token(self.order), ALU.mult))
            then(dve.tensor_reduce(self.s, self.eq, AX_X, ALU.max))
            then(dve.tensor_tensor(self.hit, self.eq, wide(self.s), ALU.is_equal))
            if k == 0:
                then(dve.tensor_tensor(self.comb, self.pr, self.hit, ALU.mult))
            if k + 1 < self.top:
                then(dve.scalar_tensor_tensor(out=self.left.rearrange("p t e -> p (t e)"),
                                              in0=self.hit.rearrange("p t e -> p (t e)"), scalar=-2.0,
                                              in1=self.pr.rearrange("p t e -> p (t e)"), op0=ALU.mult, op1=ALU.add))
                left = self.left
            if k:
                then(dve.tensor_tensor(self.eq, self.pr, self.hit, ALU.mult))
                then(dve.tensor_tensor(self.comb, self.comb, self.eq, ALU.add))
        if self.shared:
            then(dve.memset(self.cut, 0.0))
            then(dve.memset(self.cut[:, :, 0, e:e + 1], 1.0))
        rest = self.rest[:, :, 0:e]
        then(dve.tensor_copy(self.cut[:, :, 0, 0:e], self.comb))
        then(dve.tensor_tensor(rest, self.comb, self.cut[:, :, 0, 0:e], ALU.subtract))
        then(dve.tensor_copy(self.cut[:, :, 1, 0:e], rest))
        dve.tensor_tensor(self.cut[:, :, 2, 0:e], rest, self.cut[:, :, 1, 0:e], ALU.subtract)\
            .then_inc(self.ready_cut.sem, 1)


class Experts(Stage):

    def __init__(self, c, name, ln, gate, hidden, weights, weights_in, spread, carve):
        self.c, self.ln, self.gate, self.hidden = c, ln, gate, hidden
        self.wg, self.wu, self.wd = weights
        self.weights_in = weights_in
        self.nj = -(-hidden // P)
        r = carve
        self.spread_dram = spread
        self.spread = r.take([hidden], BF16)
        self.act_g = [r.take([512]) for _ in range(2)]
        self.gu = [r.take([512]) for _ in range(2)]
        self.h = [r.take([512]) for _ in range(3)]
        n = self.nj * NG
        (self.spread_in, self.gprod, self.silu, self.mul, self.cprod, self.h_done, self.down, self.added) = \
            self.count(c, "experts", spread_in=16, gprod=n, silu=n, mul=n, cprod=n, h_done=n, down=n, added=NT)

    def sync(self, sp):
        sp.dma_start(self.spread[0:96, :], self.spread_dram).then_inc(self.spread_in.sem, 16)

    def rows(self, j):
        return min(P, self.hidden - P * j)


    def tensor(self, pe):
        c, nj = self.c, self.nj
        self.weights_in(pe)
        pe.wait_ge(self.spread_in.sem, self.spread_in.at(16))

        def up(g, j):
            n, m = g * nj + j, self.rows(j)
            if isinstance(n, int) and n < 2:
                pass
            else:
                pe.wait_ge(self.mul.sem, self.mul.at(n - 1))
            for k, w in enumerate((self.wg, self.wu)):
                bank = c.bank[2 * (j % 2) + k][0:m, :]
                for f in range(FT):
                    mm = pe.matmul(bank, w[:, f, P * j:P * j + m], c.yt[:, f, bass.ds(g * 512, 512)],
                                   start=(f == 0), stop=(f == FT - 1))
            mm.then_inc(self.gprod.sem, 1)

        def weigh(g, j, first):
            n, m = g * nj + j, self.rows(j)
            if not (first and j < 2):
                pe.wait_ge(self.h_done.sem, self.h_done.at(n - 1))
            pe.matmul(c.bank[4 + j % 2][0:m, :], self.spread[0:96, P * j:P * j + m],
                      self.gate.rows[0:96, bass.ds(g * 512, 512)], start=True, stop=True).then_inc(self.cprod.sem, 1)

        def down(g, j):
            n, m = g * nj + j, self.rows(j)
            pe.wait_ge(self.h_done.sem, self.h_done.at(n + 1))
            for q in range(4):
                mm = pe.matmul(c.bank[6 + q // 2][:, D * (q % 2):D * (q % 2) + D],
                               self.h[j % 3][0:m, P * q:P * q + P], self.wd[0:m, j, :],
                               start=(j == 0 and q % 2 == 0), stop=(j == nj - 1), skip_group_check=True)
            mm.then_inc(self.down.sem, 1)

        def group(g, first=False):
            for j in range(nj + 2):
                if j < nj:
                    up(g, j)
                if first and j == 0:
                    self.gate.turn(pe)
                    pe.wait_ge(self.gate.rows_set.sem, self.gate.rows_set.at(2))
                if j < nj:
                    weigh(g, j, first)
                if j == 2 and not first:
                    pe.wait_ge(self.added.sem, self.added.at(g * 4))
                if j >= 2:
                    down(g, j - 2)

        group(0, first=True)
        with pe.Fori(1, NG) as g:
            group(g)

    def scalar(self, act):
        c, nj = self.c, self.nj

        def group(g, first=False):
            for j in range(nj):
                n, m = g * nj + j, self.rows(j)
                act.wait_ge(self.gprod.sem, self.gprod.at(n + 1))
                if not (first and j < 2):
                    act.wait_ge(self.mul.sem, self.mul.at(n - 1))
                act.activation(self.act_g[j % 2][0:m, :], c.bank[2 * (j % 2)][0:m, :], ACT.Silu).then_inc(self.silu.sem, 1)

        group(0, first=True)
        with act.Fori(1, NG) as g:
            group(g)

    def vector(self, dve):
        c, nj = self.c, self.nj

        def group(g, first=False):
            for j in range(nj):
                n, m = g * nj + j, self.rows(j)
                dve.wait_ge(self.silu.sem, self.silu.at(n + 1))
                if not (first and j < 2):
                    dve.wait_ge(self.h_done.sem, self.h_done.at(n - 1))
                dve.tensor_tensor(self.gu[j % 2][0:m, :], c.bank[2 * (j % 2) + 1][0:m, :], self.act_g[j % 2][0:m, :],
                                  ALU.mult).then_inc(self.mul.sem, 1)
                dve.wait_ge(self.mul.sem, self.mul.at(n + 1))
                dve.wait_ge(self.cprod.sem, self.cprod.at(n + 1))
                if j >= 3:
                    dve.wait_ge(self.down.sem, self.down.at(n - 2))
                elif not first:
                    dve.wait_ge(self.down.sem, self.down.at(g * nj))
                dve.tensor_tensor(self.h[j % 3][0:m, :], c.bank[4 + j % 2][0:m, :], self.gu[j % 2][0:m, :],
                                  ALU.mult).then_inc(self.h_done.sem, 1)
            dve.wait_ge(self.down.sem, self.down.at(g * nj + nj))
            xf = c.x[:, :, :].rearrange("p t d -> p (t d)")
            for half in range(2):
                xs = xf[:, bass.ds(g * (4 * D) + 2 * D * half, 2 * D)]
                dve.tensor_tensor(xs, c.bank[6 + half][:, :], xs, ALU.add).then_inc(self.added.sem, 2)

        group(0, first=True)
        with dve.Fori(1, NG) as g:
            group(g)
        dve.wait_ge(self.added.sem, self.added.at(NT))


class KeyedSum(Stage):

    def __init__(self, c, name, ln, w, bias, cos, sin, wo, bias_out):
        self.c, self.ln = c, ln
        self.dram = (w, bias, cos, sin, wo, bias_out)
        r = Carve(c.region["a"])
        self.w = r.take([FT, 3 * D])
        self.bias = r.take([3 * D])
        self.cos = r.take([BT, P])
        self.sin = r.take([BT, P])
        self.wo = r.take([FT, D])
        self.bias_out = r.take([D])
        self.k = r.take([NT, D])
        self.ta = [r.take([2, P]) for _ in range(2)]
        self.tb = [r.take([2, P]) for _ in range(2)]
        self.ws = [r.take([FT, D]) for _ in range(NB)]
        self.ones = r.take([1])
        self.ss = r.take([NT])
        self.norm = r.take([NT])
        self.rnorm = r.take([NT])
        (self.w_in, self.prod, self.lin, self.v_done, self.cosm, self.sinm, self.rot, self.square, self.root,
         self.floor, self.rec, self.kv, self.sums, self.scaled, self.xy, self.biased, self.one) = (
            c.sem(f"{name}_{n}") for n in
            "w_in prod lin v_done cosm sinm rot square root floor rec kv sums scaled xy biased one".split())

    def sync(self, sp):
        w, bias, cos, sin, wo, bias_out = self.dram
        for dst, src in ((self.w, w.rearrange("(f p) n -> p f n", p=P)), (self.bias, bias.partition_broadcast(P)),
                         (self.cos, cos.rearrange("(t p) n -> p t n", p=P)),
                         (self.sin, sin.rearrange("(t p) n -> p t n", p=P)),
                         (self.wo, wo.rearrange("(f p) n -> p f n", p=P)),
                         (self.bias_out, bias_out.partition_broadcast(P))):
            sp.dma_start(dst, src).then_inc(self.w_in, 16)

    def gpsimd(self, pool):
        c = self.c
        pool.wait_ge(self.w_in, 96)
        pool.memset(self.ones, 1.0).then_inc(self.one, 1)
        for t in range(NT):
            self.ln.normed(pool, t)
            pool.tensor_tensor(c.x[:, t, :], c.x[:, t, :], c.yn[:, t, :], ALU.add).then_inc(self.xy, 1)
            pool.wait_ge(self.xy, t + 1)
            pool.tensor_tensor(c.x[:, t, :], c.x[:, t, :], self.bias_out, ALU.add).then_inc(self.biased, 1)
        for b in range(NB):
            s = slice(b * BT, b * BT + BT)
            pool.wait_ge(self.square, (b + 1) * BT)
            pool.tensor_tensor(self.norm[:, s], self.ss[:, s], c.half[:, s], ALU.pow).then_inc(self.root, 1)

    def tensor(self, pe):
        c = self.c
        pe.wait_ge(self.w_in, 96)
        for g in range(NG):
            self.ln.ready(pe, g)
            for t in range(4 * g, 4 * g + 4):
                if t >= 2:
                    pe.wait_ge(self.lin, 2 * (t - 1))
                    pe.wait_ge(self.v_done, t - 1)
                for bank, lo, n in ((2 * (t % 2), D, 2 * D), (2 * (t % 2) + 1, 0, D)):
                    for f in range(FT):
                        mm = pe.matmul(c.bank[bank][:, 0:n], c.yt[:, f, P * t:P * t + P], self.w[:, f, lo:lo + n],
                                       start=(f == 0), stop=(f == FT - 1))
                mm.then_inc(self.prod, 1)
        pe.wait_ge(self.one, 1)
        for b in range(NB):
            pe.wait_ge(self.kv, (b + 1) * BT)
            for f in range(FT):
                for t in range(b * BT, b * BT + BT):
                    mm = pe.matmul(c.bank[4 + b][:, f:f + 1], self.k[:, t, P * f:P * f + P], self.ones,
                                   start=(t == b * BT), stop=(t == b * BT + BT - 1))
            mm.then_inc(self.sums, 1)

    def scalar(self, act):
        c = self.c
        self.ln.ready(act, NG - 1)
        for t in range(NT):
            act.wait_ge(self.rot, 2 * t + 2)
            if t:
                act.wait_ge(self.square, t)
            act.activation(c.bank[6][:, 0:D], self.k[:, t, :], ACT.Square,
                           accum_out=self.ss[:, t:t + 1]).then_inc(self.square, 1)

    def vector(self, dve):
        c = self.c
        dve.wait_ge(self.w_in, 96)
        cx = c.cx[:, :].rearrange("p (t d) -> p t d", d=D)

        def product(b):
            s = slice(b * BT, b * BT + BT)
            dve.wait_ge(self.root, b + 1)
            dve.tensor_scalar(self.norm[:, s], self.norm[:, s], 1e-12, None, ALU.max).then_inc(self.floor, 1)
            dve.wait_ge(self.floor, b + 1)
            dve.reciprocal(self.rnorm[:, s], self.norm[:, s]).then_inc(self.rec, 1)
            dve.wait_ge(self.rec, b + 1)
            for t in range(b * BT, b * BT + BT):
                dve.scalar_tensor_tensor(out=self.k[:, t, :], in0=self.k[:, t, :], scalar=self.rnorm[:, t:t + 1],
                                         in1=c.yn[:, t, :], op0=ALU.mult, op1=ALU.mult).then_inc(self.kv, 1)

        for t in range(NT):
            kv, q = c.bank[2 * (t % 2)], c.bank[2 * (t % 2) + 1]
            bt = t % BT
            dve.wait_ge(self.prod, t + 1)
            dve.tensor_tensor(cx[:, t, :], q[:, 0:D], self.bias[:, 0:D], ALU.add).then_inc(self.lin, 1)
            dve.tensor_tensor(self.k[:, t, :], kv[:, 0:D], self.bias[:, D:2 * D], ALU.add).then_inc(self.lin, 1)
            dve.wait_ge(self.xy, t + 1)
            self.ln.ready(dve, t // 4)
            dve.tensor_tensor(c.yn[:, t, :], kv[:, D:2 * D], self.bias[:, 2 * D:3 * D], ALU.add).then_inc(self.v_done, 1)
            dve.wait_ge(self.lin, 2 * t + 2)
            if t >= 2:
                dve.wait_ge(self.rot, 2 * t - 2)
            a, b = self.ta[t % 2], self.tb[t % 2]
            sin = self.sin[:, bt, :].rearrange("p (n e) -> p n e", e=2)
            for n, z in enumerate((cx[:, t, 0:P], self.k[:, t, 0:P])):
                pair = z.rearrange("p (n e) -> p n e", e=2)
                bp = b[:, n, :].rearrange("p (n e) -> p n e", e=2)
                dve.tensor_tensor(a[:, n, :], z, self.cos[:, bt, :], ALU.mult).then_inc(self.cosm, 1)
                for e in range(2):
                    dve.tensor_tensor(bp[:, :, e], pair[:, :, 1 - e], sin[:, :, e], ALU.mult).then_inc(self.sinm, 1)
            dve.wait_ge(self.cosm, 2 * t + 2)
            dve.wait_ge(self.sinm, 4 * t + 4)
            for n, z in enumerate((cx[:, t, 0:P], self.k[:, t, 0:P])):
                dve.tensor_tensor(z, a[:, n, :], b[:, n, :], ALU.add).then_inc(self.rot, 1)
            if t == BT + 1:
                dve.wait_ge(self.v_done, BT)
                product(0)
        dve.wait_ge(self.v_done, NT)
        product(1)
        for b in range(NB):
            dve.wait_ge(self.sums, b + 1)
            for f in range(FT):
                dve.tensor_scalar(self.ws[b][:, f, :], self.wo[:, f, :], c.bank[4 + b][:, f:f + 1], None,
                                  ALU.mult).then_inc(self.scaled, 1)
        dve.wait_ge(self.biased, NT)

    def source(self, t, f):
        return self.c.cx[:, D * t + P * f:D * t + P * f + P]

    def out_weights(self, t, f):
        return self.ws[t // BT][:, f, :]

    def finished(self, pe, g):
        if g == 0:
            pe.wait_ge(self.rot, 2 * NT)
            pe.wait_ge(self.scaled, NB * FT)


class LinearAttention(Stage):

    HEAD = 16
    EPS = 1e-6

    def __init__(self, c, name, ln, wq, wkv, bq, bkv, wo, bo, decay, block, member, at):
        self.c, self.ln = c, ln
        self.dram = (wq, wkv, bq, bkv, wo, bo, decay, block, member)
        r = Carve(c.region["a"])
        self.wq = r.take([FT, D])
        self.wkv = r.take([FT, 2 * D])
        self.wo = r.take([FT, D])
        self.bq = r.take([FT])
        self.bkv = r.take([2 * D])
        self.bo = r.take([D])
        self.decay = r.take([BT])
        self.block = r.take([P])
        self.member = r.take([P // self.HEAD])
        self.kt = [r.take([D]) for _ in range(2)]
        self.nh = P // self.HEAD
        self.bd = [r.take([FT, P + self.nh]) for _ in range(NB)]
        self.den = [r.take([FT, self.nh]) for _ in range(2)]
        self.rden = [r.take([FT, self.nh]) for _ in range(2)]
        self.k = r.take([NT, D])
        r = Carve(c.region["w"], at)
        self.v = r.take([NT, FT, P + 1])
        self.qt = r.take([FT, NTOK])
        (self.w_in, self.qprod, self.q_done, self.kvprod, self.k_lin, self.v_done, self.k_done, self.one,
         self.sums, self.bd_done, self.outp, self.dn, self.rc, self.rd, self.o_done, self.biased) = (
            c.sem(f"{name}_{n}") for n in
            "w_in qprod q_done kvprod k_lin v_done k_done one sums bd_done outp dn rc rd o_done biased".split())

    def sync(self, sp):
        wq, wkv, bq, bkv, wo, bo, decay, block, member = self.dram
        for dst, src in ((self.wq, wq.rearrange("(f p) n -> p f n", p=P)),
                         (self.wkv, wkv.rearrange("(f p) n -> p f n", p=P)),
                         (self.wo, wo.rearrange("(f p) n -> p f n", p=P)), (self.bq, bq),
                         (self.bkv, bkv.partition_broadcast(P)), (self.bo, bo.partition_broadcast(P)),
                         (self.decay, decay), (self.block, block), (self.member, member)):
            sp.dma_start(dst, src).then_inc(self.w_in, 16)

    W_IN = 9 * 16

    def gpsimd(self, pool):
        c = self.c
        pool.wait_ge(self.w_in, self.W_IN)
        pool.memset(self.v[:, :, :, P:P + 1], 1.0).then_inc(self.one, 1)
        for t in range(NT):
            self.ln.normed(pool, t)
            pool.tensor_tensor(c.x[:, t, :], c.x[:, t, :], self.bo, ALU.add).then_inc(self.biased, 1)

    def tensor(self, pe):
        c, nh = self.c, self.nh
        pe.wait_ge(self.w_in, self.W_IN)
        for g in range(NG):
            self.ln.ready(pe, g)
            for o in range(FT):
                if g:
                    pe.wait_ge(self.q_done, FT * (g - 1) + o + 1)
                for f in range(FT):
                    mm = pe.matmul(c.bank[o][:, :], self.wq[:, f, P * o:P * o + P], c.yt[:, f, 512 * g:512 * g + 512],
                                   start=(f == 0), stop=(f == FT - 1))
                mm.then_inc(self.qprod, 1)
            for t in range(4 * g, 4 * g + 4):
                if t >= 2:
                    pe.wait_ge(self.k_lin, t - 1)
                    pe.wait_ge(self.v_done, t - 1)
                for f in range(FT):
                    mm = pe.matmul(c.bank[2 + t % 2][:, :], c.yt[:, f, P * t:P * t + P], self.wkv[:, f, :],
                                   start=(f == 0), stop=(f == FT - 1))
                mm.then_inc(self.kvprod, 1)
        pe.wait_ge(self.one, 1)
        for b in range(NB):
            pe.wait_ge(self.k_done, (b + 1) * BT)
            pe.wait_ge(self.v_done, (b + 1) * BT)
            for f in range(FT):
                for t in range(b * BT, b * BT + BT):
                    mm = pe.matmul(c.bank[4 + b][:, D * f:D * f + P + 1], self.k[:, t, P * f:P * f + P],
                                   self.v[:, t, f, :], start=(t == b * BT), stop=(t == b * BT + BT - 1))
            mm.then_inc(self.sums, 1)
        pe.wait_ge(self.q_done, FT * NG)
        for t in range(NT):
            pe.wait_ge(self.bd_done, 2 * FT * (t // BT + 1))
            if t >= 4:
                pe.wait_ge(self.o_done, t - 3)
            for f in range(FT):
                mm = pe.matmul(c.bank[t % 4][:, (P + nh) * f:(P + nh) * (f + 1)], self.qt[:, f, P * t:P * t + P],
                               self.bd[t // BT][:, f, :], start=True, stop=True)
            mm.then_inc(self.outp, 1)

    def scalar(self, act):
        c = self.c
        act.wait_ge(self.w_in, self.W_IN)
        for g in range(NG):
            for o in range(FT):
                act.wait_ge(self.qprod, FT * g + o + 1)
                act.activation(self.qt[:, o, 512 * g:512 * g + 512], c.bank[o][:, :], ACT.Relu,
                               bias=self.bq[:, o:o + 1]).then_inc(self.q_done, 1)

    def vector(self, dve):
        c, nh = self.c, self.nh
        dve.wait_ge(self.w_in, self.W_IN)
        halves = lambda z: z.rearrange("p (f e) -> p f e", f=FT)
        for t in range(NT):
            z = c.bank[2 + t % 2]
            dve.wait_ge(self.kvprod, t + 1)
            if t >= 2:
                dve.wait_ge(self.k_done, t - 1)
            dve.tensor_tensor(self.kt[t % 2], z[:, 0:D], self.bkv[:, 0:D], ALU.add).then_inc(self.k_lin, 1)
            dve.tensor_tensor(self.v[:, t, :, 0:P], halves(z[:, D:2 * D]), halves(self.bkv[:, D:2 * D]),
                              ALU.add).then_inc(self.v_done, 1)
            dve.wait_ge(self.k_lin, t + 1)
            dve.tensor_scalar(self.k[:, t, :], self.kt[t % 2], 0.0, self.decay[:, t % BT:t % BT + 1], ALU.max,
                              ALU.mult).then_inc(self.k_done, 1)
        for b in range(NB):
            dve.wait_ge(self.sums, b + 1)
            for f in range(FT):
                z = c.bank[4 + b][:, D * f:D * f + P + 1]
                dve.tensor_tensor(self.bd[b][:, f, 0:P], z[:, 0:P], self.block, ALU.mult).then_inc(self.bd_done, 1)
                dve.tensor_scalar(self.bd[b][:, f, P:P + nh], self.member, z[:, P:P + 1], None,
                                  ALU.mult).then_inc(self.bd_done, 1)
        for t in range(NT):
            z = c.bank[t % 4][:, 0:FT * (P + nh)].rearrange("p (f e) -> p f e", f=FT)
            den, rden = self.den[t % 2], self.rden[t % 2]
            decay = self.decay[:, t % BT:t % BT + 1]
            dve.wait_ge(self.outp, t + 1)
            dve.tensor_scalar(den, z[:, :, P:P + nh], decay, self.EPS, ALU.mult, ALU.add).then_inc(self.dn, 1)
            dve.wait_ge(self.dn, t + 1)
            dve.reciprocal(rden, den).then_inc(self.rc, 1)
            dve.wait_ge(self.rc, t + 1)
            dve.tensor_scalar(den, rden, decay, None, ALU.mult).then_inc(self.rd, 1)
            dve.wait_ge(self.rd, t + 1)
            dve.tensor_tensor(c.cx[:, D * t:D * t + D].rearrange("p (f h e) -> p f h e", f=FT, h=nh),
                              z[:, :, 0:P].rearrange("p f (h e) -> p f h e", h=nh), over(den, 3, self.HEAD),
                              ALU.mult).then_inc(self.o_done, 1)
        dve.wait_ge(self.biased, NT)

    def source(self, t, f):
        return self.c.cx[:, D * t + P * f:D * t + P * f + P]

    def finished(self, pe, g):
        pe.wait_ge(self.o_done, 4 * g + 4 if g else NT)


class Weights(Stage):

    def __init__(self, c, name, wg, wu, wd, hidden):
        self.c, self.hidden, self.dram = c, hidden, (wg, wu, wd)
        r = Carve(c.region["w"])
        self.nj = -(-hidden // P)
        self.wg, self.wu, self.wd = r.take([FT, hidden]), r.take([FT, hidden]), r.take([self.nj, D])
        self.end = r.at
        self.loaded = c.sem(name + "_loaded")

    def sync(self, sp):
        wg, wu, wd = self.dram
        full = self.hidden // P
        sp.dma_start(self.wg, wg.rearrange("(f p) n -> p f n", p=P)).then_inc(self.loaded, 16)
        sp.dma_start(self.wu, wu.rearrange("(f p) n -> p f n", p=P)).then_inc(self.loaded, 16)
        sp.dma_start(self.wd[:, 0:full, :], wd[0:full * P, :].rearrange("(j p) n -> p j n", p=P)).then_inc(self.loaded, 16)
        if full < self.nj:
            sp.dma_start(self.wd[0:self.hidden - full * P, full, :], wd[full * P:, :]).then_inc(self.loaded, 16)

    def wait(self, eng):
        eng.wait_ge(self.loaded, 16 * (3 + (self.hidden % P > 0)))


class After(Stage):

    def __init__(self, sem, count):
        self.sem, self.count = sem, count

    def sync(self, sp):
        sp.wait_ge(self.sem, self.count)

    gpsimd = sync


class Finish(Stage):
    def __init__(self, c, out, added, count):
        self.c, self.out, self.added, self.count, self.out_done = c, out, added, count, c.sem("out_done")

    def sync(self, sp):
        out = self.out.rearrange("b (t p) d -> p (b t) d", p=P)
        sp.wait_ge(self.added, self.count)
        for g in range(NG):
            sp.dma_start(out[:, 4 * g:4 * g + 4, :], self.c.x[:, 4 * g:4 * g + 4, :]).then_inc(self.out_done, 16)
        sp.wait_ge(self.out_done, 16 * NG)


def build(nc, t, out):
    with ExitStack() as ctx:
        c = Core(nc, ctx)
        stages = [Start(c, t["x"], t["identf"], t["identb"])]
        w0 = Weights(c, "w0", t["f0_wg"], t["f0_wu"], t["f0_wd"], t["f0_wg"].shape[1])
        w1 = Weights(c, "w1", t["f1_wg"], t["f1_wu"], t["f1_wd"], t["f1_wg"].shape[1])
        last = [None]
        counts = {"ln": 0, "project": 0}

        def begin(name):
            if last[0] is not None:
                stages.append(After(*last[0]))
            ln = LayerNorm(c, counts["ln"])
            counts["ln"] += 1
            stages.append(ln)
            return ln

        def project(name, mixer, w):
            p = Project(c, counts["project"], mixer.source, w, mixer.finished)
            counts["project"] += 1
            stages.append(p)
            last[0] = (p.added, NT * counts["project"])

        def attention(name, hd, w, wo, tables, bias, bias_out):
            ln = begin(name)
            a = Attention(c, name, ln, hd, t[w], t[wo], (t[tables + "_cos"], t[tables + "_sin"]), t[bias], t[bias_out],
                          t["mask_q"], t["mask_k"])
            stages.append(a)
            project(name, a, lambda tt, f: a.wo[:, f, :])

        def experts(name, weights, n, top, shared, w, bias, spread):
            ln = begin(name)
            r = Carve(c.region["a"])
            gate = Gate(c, name + "_gate", ln, n, top, shared, t[w], t[bias] if bias else None, r)
            e = Experts(c, name, ln, gate, weights.hidden, (weights.wg, weights.wu, weights.wd), weights.wait,
                        t[spread], r)
            stages.extend([gate, e])
            last[0] = (e.added.sem, e.added.at(NT))

        def s1():
            attention("a0", 8, "a0_w", "a0_wo", "a0", "a0_bias", "a0_bo")

        def s2():
            experts("f0", w0, 4, 1, False, "f0_wr", "f0_br", "spread0")

        def s3():
            ln = begin("b0")
            m = KeyedSum(c, "b0", ln, t["b0_w"], t["b0_bias"], t["b0_cos"], t["b0_sin"], t["b0_wo"], t["b0_bo"])
            stages.append(m)
            project("b0", m, m.out_weights)

        def s4():
            experts("f0b", w0, 4, 1, False, "f0_wr", "f0_br", "spread0")

        def s5():
            ln = begin("a1")
            stages.append(w1)
            m = LinearAttention(c, "a1", ln, t["a1_wq"], t["a1_wkv"], t["a1_bq"], t["a1_bkv"], t["a1_wo"], t["a1_bo"],
                                t["decay"], t["block"], t["member"], w1.end)
            stages.append(m)
            project("a1", m, lambda tt, f: m.wo[:, f, :])

        def s6():
            experts("f1", w1, 8, 2, True, "f1_gate", None, "spread1")

        def s7():
            attention("b1", 16, "b1_w", "b1_wo", "b1", "b1_bias", "b1_bo")

        def s8():
            experts("f1b", w1, 8, 2, True, "f1_gate", None, "spread1")

        stages.append(w0)
        for stage in (s1, s2, s3, s4, s5, s6, s7, s8):
            stage()
        stages.append(Finish(c, out, *last[0]))

        block = ctx.enter_context(nc.Block())

        @block.sync
        def _(sp):
            for s in stages:
                s.sync(sp)

        @block.gpsimd
        def _(pool):
            for s in stages:
                s.gpsimd(pool)

        @block.scalar
        def _(act):
            for s in stages:
                s.scalar(act)

        @block.tensor
        def _(pe):
            for s in stages:
                s.tensor(pe)

        @block.vector
        def _(dve):
            for s in stages:
                s.vector(dve)



def constants():
    import numpy as np

    f = np.float32
    bf = mybir.dt.np(BF16)
    pos = np.arange(SEQ, dtype=f)
    out = {}

    inv = (f(1) / np.power(f(10000), np.arange(0, 8, 2, dtype=f) / f(8))).astype(f)
    th = np.outer(pos, inv).astype(f)
    out["a0_cos"] = np.concatenate([np.cos(th), np.cos(th)], 1)
    out["a0_sin"] = np.concatenate([-np.sin(th), np.sin(th)], 1)

    inv = (f(1) / np.power(f(10000), np.arange(0, P, 2, dtype=f) / f(P))).astype(f)
    th = np.repeat(pos[:, None] * inv[None, :], 2, 1).astype(f)
    sign = np.tile(np.array([-1, 1], f), P // 2)
    out["b0_cos"], out["b0_sin"] = np.cos(th), np.sin(th) * sign

    inv = np.power(f(10000), f(-2) * np.arange(8, dtype=f) / f(16)).astype(f)
    th = (pos[:, None] * inv[None, :]).astype(f)
    out["b1_cos"], out["b1_sin"] = np.tile(np.cos(th), (1, 2)), np.tile(np.sin(th), (1, 2))

    out["decay"] = np.exp(-pos / f(SEQ)).reshape(BT, P).T
    q = np.arange(P)
    out["mask_q"] = np.where(q[None, :] > q[:, None], f(NEG), f(0)).astype(bf)
    out["mask_k"] = out["mask_q"].T
    out["block"] = (q[:, None] // 16 == q[None, :] // 16).astype(f)
    out["member"] = (q[:, None] // 16 == np.arange(8)[None, :]).astype(f)
    out["identf"] = np.eye(P, dtype=f)
    out["identb"] = np.eye(P, dtype=f).astype(bf)
    owner0 = np.repeat(np.arange(4), 1024)
    owner1 = np.concatenate([np.repeat(np.arange(8), 176), np.full(352, 8)])
    for name, owner, n in (("spread0", owner0, 4), ("spread1", owner1, 9)):
        s = np.zeros((96, len(owner)), f)
        for part in range(3):
            s[part * n + owner, np.arange(len(owner))] = 1
        out[name] = s.astype(bf)
    out["a0_bias"] = np.zeros(3 * P, f)
    return {k: np.ascontiguousarray(v) for k, v in out.items()}


def kernel(**i):
    import numpy as np
    import concourse.bacc as bacc
    from concourse.bass_utils import run_bass_kernel_spmd

    i = {k: np.asarray(v) for k, v in i.items()}
    cat = lambda *a: np.concatenate(a, -1)
    by_feature = lambda w: np.transpose(w, (1, 0, 2)).reshape(w.shape[1], -1)
    arrays = {
        "x": i["L0_attn_a_x"],
        "a0_w": cat(i["L0_attn_a_Wq"], i["L0_attn_a_Wk"], i["L0_attn_a_Wv"]),
        "a0_wo": i["L0_attn_a_Wo"], "a0_bo": i["L0_attn_a_b_out"],
        "f0_wr": i["L0_ffn_Wr"], "f0_br": i["L0_ffn_br"],
        "f0_wg": by_feature(i["L0_ffn_Wg"]), "f0_wu": by_feature(i["L0_ffn_Wu"]),
        "f0_wd": i["L0_ffn_Wd"].reshape(-1, D),
        "b0_w": i["L0_attn_b_W_in"].T, "b0_bias": i["L0_attn_b_b_in"],
        "b0_wo": i["L0_attn_b_W_out"].T, "b0_bo": i["L0_attn_b_b_out"],
        "a1_wq": i["L1_attn_a_Wq"].T, "a1_wkv": cat(i["L1_attn_a_Wk"].T, i["L1_attn_a_Wv"].T),
        "a1_bq": i["L1_attn_a_bq"].reshape(FT, P).T, "a1_bkv": cat(i["L1_attn_a_bk"], i["L1_attn_a_bv"]),
        "a1_wo": i["L1_attn_a_Wo"].T, "a1_bo": i["L1_attn_a_bo"],
        "f1_gate": i["L1_ffn_gate_w"],
        "f1_wg": cat(by_feature(i["L1_ffn_w_gate"]), i["L1_ffn_sw_gate"]),
        "f1_wu": cat(by_feature(i["L1_ffn_w_up"]), i["L1_ffn_sw_up"]),
        "f1_wd": np.concatenate([i["L1_ffn_w_down"].reshape(-1, D), i["L1_ffn_sw_down"]], 0),
        "b1_w": cat(i["L1_attn_b_Wq"].T, i["L1_attn_b_Wk"].T, i["L1_attn_b_Wv"].T),
        "b1_bias": cat(i["L1_attn_b_bq"], i["L1_attn_b_bk"], i["L1_attn_b_bv"]),
        "b1_wo": i["L1_attn_b_Wo"].T, "b1_bo": i["L1_attn_b_bo"],
        **constants(),
    }
    arrays = {"in_" + k: np.ascontiguousarray(v) for k, v in arrays.items()}
    nc = bacc.Bacc("TRN2", target_bir_lowering=False, num_devices=1)
    tensors = {k[3:]: nc.dram_tensor(k, v.shape, mybir.dt.from_np(v.dtype), kind="ExternalInput").ap()
               for k, v in arrays.items()}
    out = nc.dram_tensor("out", [NB, SEQ, D], F32, kind="ExternalOutput").ap()
    build(nc, tensors, out)
    r = run_bass_kernel_spmd(nc, [arrays], core_ids=[0])
    return r.results[0]["out"]
```

```python
from contextlib import ExitStack

import concourse.bass as bass
from concourse import mybir

ALU = mybir.AluOpType
ACT = mybir.ActivationFunctionType
AX_X = mybir.AxisListType.X
F32 = mybir.dt.float32
BF16 = mybir.dt.bfloat16
U32 = mybir.dt.uint32

P = 128
D = 256
FT = D // P
NB, SEQ = 2, 1024
NTOK = NB * SEQ
NT = NTOK // P
BT = SEQ // P
NG = NT // 4
LN_EPS = 1e-5
L0_EXPERTS = 4
GQ = 4
QK_COLS = D + D // GQ
NEG = -1e30
KROWS = 96
SROWS = KROWS + 3
STEPS = [(i, j) for i in range(BT) for j in range(i + 1)]
MAX_STEPS = [(0, i, h) for i in range(4) for h in (0, 2)] + [(1, i, h) for i in range(4, 8) for h in range(GQ)]
SLOTS = 3
ST_BANK, ACC_BANK, TURN_BANK = 4, 6, 7


class Core:

    def __init__(self, nc, ctx):
        self.nc, self.ctx, self.shared, self.counted = nc, ctx, {}, {}
        self.x = self.sb("x_res", [P, NT, D], F32)
        self.yn = self.sb("y_norm", [P, NT, D], F32)
        self.yt = self.sb("y_t", [P, FT, NTOK], F32)
        self.cx_pad = self.sb("ctx", [P, NT * D + D], F32)
        self.cx = self.cx_pad[:, 0:NT * D]
        self.stats = self.sb("ln_stats", [P, NT, 6], F32)
        self.mv = self.sb("ln_mv", [P, NT, 2], F32)
        self.rstd = self.sb("ln_rstd", [P, NT], F32)
        self.vareps = self.sb("ln_vareps", [P, NT], F32)
        self.mhalf = self.sb("minus_half", [P, NT], F32)
        self.half = self.sb("plus_half", [P, NT], F32)
        self.identf = self.sb("identf", [P, P], F32)
        self.identb = self.sb("identb", [P, P], BF16)
        self.region = {"w": self.sb("region_w", [P, 24576], F32), "a": self.sb("region_a", [P, 11450], F32)}
        self.psum = ctx.enter_context(nc.psum_tensor("psum", [P, 8, 512], F32))
        self.bank = [self.psum[:, i, :] for i in range(8)]
        self.sorted = nc.dram_tensor("sorted_rows", [(NT + L0_EXPERTS - 1) * P, D], F32, kind="Internal").ap()
        self.results = nc.dram_tensor("result_rows", [(NT + L0_EXPERTS - 1) * P, D], F32, kind="Internal").ap()
        self.zeros_out = self.sem("zeros_out")

    def sb(self, name, shape, dt):
        return self.ctx.enter_context(self.nc.sbuf_tensor(name, shape, dt))

    def sem(self, name):
        return self.ctx.enter_context(self.nc.semaphore(name))

    def shared_sem(self, name):
        if name not in self.shared:
            self.shared[name] = self.sem(name)
        return self.shared[name]


class Carve:

    def __init__(self, region, at=0):
        self.region, self.at = region, at

    def take(self, free, dt=F32, parts=P):
        n = 1
        for f in free:
            n *= f
        words = n if dt == F32 else (n + 1) // 2
        v = self.region[0:parts, self.at:self.at + words]
        self.at += words
        assert self.at <= self.region.shape[1], self.at
        if dt != F32:
            v = v.bitcast(dt)
        if len(free) == 2:
            v = v.rearrange("p (a b) -> p a b", a=free[0])
        if len(free) == 3:
            v = v.rearrange("p (a b c) -> p a b c", a=free[0], b=free[1])
        return v


def over(ap, axis, n):
    shape = list(ap.shape)
    return ap.unsqueeze(axis).to_broadcast(shape[:axis] + [n] + shape[axis:])


class Counted:

    def __init__(self, sem, base):
        self.sem, self.base = sem, base

    def at(self, n):
        return n + self.base if self.base else n


class Stage:

    def count(self, c, kind, **totals):
        counted = []
        for name, total in totals.items():
            key = f"{kind}_{name}"
            sem, base = c.counted.get(key) or (c.sem(key), 0)
            counted.append(Counted(sem, base))
            c.counted[key] = (sem, base + total)
        return counted

    def sync(self, sp): pass
    def gpsimd(self, pool): pass
    def scalar(self, act): pass
    def tensor(self, pe): pass
    def vector(self, dve): pass


class Start(Stage):

    def __init__(self, c, x, identf, identb):
        self.c, self.x_dram, self.identf, self.identb = c, x, identf, identb
        self.x_in = c.sem("x_in")
        self.const_in = c.sem("const_in")
        self.consts = c.sem("consts_set")
        self.zeros = c.cx_pad[:, NT * D:NT * D + D]

    def sync(self, sp):
        c = self.c
        sp.dma_start(c.identf[:, :], self.identf).then_inc(self.const_in, 16)
        sp.dma_start(c.identb[:, :], self.identb).then_inc(self.const_in, 16)
        x = self.x_dram.rearrange("b (t p) d -> p (b t) d", p=P)
        for g in range(NG):
            sp.dma_start(c.x[:, 4 * g:4 * g + 4, :], x[:, 4 * g:4 * g + 4, :]).then_inc(self.x_in, 16)
        sp.wait_ge(self.consts, 3)
        sp.dma_start(c.sorted.rearrange("(n p) d -> p n d", p=P), over(self.zeros, 1, c.sorted.shape[0] // P))\
            .then_inc(c.zeros_out, 16)

    def gpsimd(self, pool):
        c = self.c
        pool.memset(c.mhalf[:, :], -0.5).then_inc(self.consts, 1)
        pool.memset(c.half[:, :], 0.5).then_inc(self.consts, 1)
        pool.memset(self.zeros, 0.0).then_inc(self.consts, 1)
        pool.wait_ge(self.consts, 3)

    def vector(self, dve):
        dve.wait_ge(self.x_in, 16 * NG)

    def tensor(self, pe):
        pe.wait_ge(self.const_in, 32)


class LayerNorm(Stage):


    def __init__(self, c, k):
        self.c, self.k = c, k
        self.stat = c.shared_sem("ln_stat")
        self.aggr = c.shared_sem("ln_aggr")
        self.veps = c.shared_sem("ln_veps")
        self.rstd = c.shared_sem("ln_rstd")
        self.norm = c.shared_sem("ln_norm")
        self.turned = c.shared_sem("ln_turned")
        self.yt0 = c.shared_sem("ln_yt0")
        self.yt1 = c.shared_sem("ln_yt1")

    def ready(self, eng, g):
        eng.wait_ge(self.yt0, NG * self.k + g + 1)
        eng.wait_ge(self.yt1, NG * self.k + g + 1)

    def normed(self, eng, t):
        eng.wait_ge(self.norm, NT * self.k + t + 1)

    def vector(self, dve):
        c, k = self.c, self.k
        for t in range(NT):
            dve.bn_stats(c.stats[:, t, :], c.x[:, t, :]).then_inc(self.stat, 1)
        for t in range(NT):
            dve.wait_ge(self.stat, NT * k + t + 1)
            dve.bn_aggr(c.mv[:, t, :], c.stats[:, t, :]).then_inc(self.aggr, 1)

        def copies(g):
            dve.wait_ge(self.turned, FT * (NG * k + g + 1))
            dve.tensor_copy(c.yt[:, 1, 512 * g:512 * g + 512], c.bank[5 + 2 * (g % 2)][:, :]).then_inc(self.yt1, 1)

        for g in range(NG):
            dve.wait_ge(self.rstd, NG * k + g + 1)
            for t in range(4 * g, 4 * g + 4):
                dve.tensor_scalar(c.yn[:, t, :], c.x[:, t, :], c.mv[:, t, 0:1], c.rstd[:, t:t + 1],
                                  ALU.subtract, ALU.mult).then_inc(self.norm, 1)
            if g:
                copies(g - 1)
        copies(NG - 1)

    def gpsimd(self, pool):
        c, k = self.c, self.k
        for g in range(NG):
            s = slice(4 * g, 4 * g + 4)
            pool.wait_ge(self.aggr, NT * k + 4 * g + 4)
            pool.tensor_scalar(c.vareps[:, s], c.mv[:, s, 1], LN_EPS, None, ALU.add).then_inc(self.veps, 1)
            pool.wait_ge(self.veps, NG * k + g + 1)
            pool.tensor_tensor(c.rstd[:, s], c.vareps[:, s], c.mhalf[:, s], ALU.pow).then_inc(self.rstd, 1)

    def tensor(self, pe):
        c, k = self.c, self.k
        for g in range(NG):
            self.normed(pe, 4 * g + 3)
            for f in range(FT):
                if g >= 2:
                    pe.wait_ge([self.yt0, self.yt1][f], NG * k + g - 1)
                for q in range(4):
                    mm = pe.transpose(c.bank[4 + 2 * (g % 2) + f][:, P * q:P * q + P],
                                      c.yn[:, 4 * g + q, P * f:P * f + P], c.identf[:, :])
                mm.then_inc(self.turned, 1)

    def scalar(self, act):
        c, k = self.c, self.k
        for g in range(NG):
            act.wait_ge(self.turned, FT * (NG * k + g) + 1)
            act.activation(c.yt[:, 0, 512 * g:512 * g + 512], c.bank[4 + 2 * (g % 2)][:, :],
                           ACT.Copy).then_inc(self.yt0, 1)


class Project(Stage):


    def __init__(self, c, k, source, w, before):
        self.c, self.k, self.source, self.w, self.before = c, k, source, w, before
        self.turned = c.shared_sem("project_turned")
        self.ot0 = c.shared_sem("project_ot0")
        self.ot1 = c.shared_sem("project_ot1")
        self.prod = c.shared_sem("project_prod")
        self.added = c.shared_sem("project_added")

    def tensor(self, pe):
        c, k = self.c, self.k

        def turn(g):
            self.before(pe, g)
            for f in range(FT):
                if g >= 2:
                    pe.wait_ge([self.ot0, self.ot1][f], NG * k + g - 1)
                for q in range(4):
                    mm = pe.transpose(c.bank[4 + 2 * (g % 2) + f][:, P * q:P * q + P],
                                      self.source(4 * g + q, f), c.identf[:, :])
                mm.then_inc(self.turned, 1)

        def multiply(g):
            pe.wait_ge(self.ot0, NG * k + g + 1)
            pe.wait_ge(self.ot1, NG * k + g + 1)
            for q in range(4):
                t = 4 * g + q
                if t >= 4:
                    pe.wait_ge(self.added, NT * k + t - 3)
                for f in range(FT):
                    mm = pe.matmul(c.bank[q][:, 0:D], c.yt[:, f, P * t:P * t + P], self.w(t, f),
                                   start=(f == 0), stop=(f == FT - 1))
                mm.then_inc(self.prod, 1)

        for g in range(NG):
            turn(g)
            if g:
                multiply(g - 1)
        multiply(NG - 1)

    def scalar(self, act):
        c, k = self.c, self.k
        for g in range(NG):
            act.wait_ge(self.turned, FT * (NG * k + g) + 1)
            act.activation(c.yt[:, 0, 512 * g:512 * g + 512], c.bank[4 + 2 * (g % 2)][:, :],
                           ACT.Copy).then_inc(self.ot0, 1)

    def vector(self, dve):
        c, k = self.c, self.k

        def adds(g):
            for t in range(4 * g, 4 * g + 4):
                dve.wait_ge(self.prod, NT * k + t + 1)
                dve.tensor_tensor(c.x[:, t, :], c.bank[t % 4][:, 0:D], c.x[:, t, :], ALU.add).then_inc(self.added, 1)

        for g in range(NG):
            dve.wait_ge(self.turned, FT * (NG * k + g + 1))
            dve.tensor_copy(c.yt[:, 1, 512 * g:512 * g + 512], c.bank[5 + 2 * (g % 2)][:, :]).then_inc(self.ot1, 1)
            if g:
                adds(g - 1)
        adds(NG - 1)
        dve.wait_ge(self.added, NT * (k + 1))


class Attention(Stage):

    def __init__(self, c, name, ln, hd, w, wo, tables, bias, bias_out, mask_q, mask_k):
        self.c, self.ln, self.hd = c, ln, hd
        self.nkv = D // GQ // hd
        self.units = NB * self.nkv
        self.scale = float(hd) ** -0.5
        self.dram = dict(w=w, wo=wo, tables=tables, bias=bias, bias_out=bias_out, mq=mask_q, mk=mask_k)
        pairs = [(a, b) for a in range(3) for b in range(3)]
        self.terms = pairs if hd == 8 else [(a, b) for a, b in pairs if a + b <= 2]
        assert len(self.terms) * hd <= KROWS
        nc = c.nc
        self.q_dram = nc.dram_tensor(name + "_q", [3, NB * D, SEQ], BF16, kind="Internal").ap()
        self.k_dram = nc.dram_tensor(name + "_k", [3, NB * D // GQ, SEQ], BF16, kind="Internal").ap()
        r = Carve(c.region["a"])
        self.wo = r.take([FT, D])
        self.v = r.take([self.units, BT, hd])
        self.bias_out = r.take([D])
        self.mq = r.take([P], BF16)
        self.mk = r.take([P], BF16)
        self.kp = [r.take([SEQ], BF16) for _ in range(SLOTS)]
        self.vp = [r.take([BT, 32]) for _ in range(SLOTS)]
        self.mparts = [r.take([4, P], BF16) for _ in range(2)]
        yn, yt = Carve(c.yn.rearrange("p t d -> p (t d)")), Carve(c.yt[:, 0, :])
        self.qp = [at.take([GQ, SEQ], BF16) for at in (yn, yn, yt)]
        both = r.at
        self.w = r.take([FT, 3 * P])
        self.cos = r.take([BT, hd])
        self.sin = r.take([BT, hd])
        self.bias = r.take([3 * P])
        self.rot = [r.take([QK_COLS]) for _ in range(2)]
        self.rotb = [r.take([QK_COLS]) for _ in range(2)]
        self.qk = [r.take([QK_COLS]) for _ in range(4)]
        self.parts = [r.take([3, 512], BF16) for _ in range(2)]
        self.rest = [r.take([512]) for _ in range(2)]
        r = Carve(c.region["a"], both)
        self.p = [r.take([GQ, P]) for _ in range(3)]
        self.acc = r.take([512])
        self.mx = [r.take([4, GQ]) for _ in range(2)]
        self.mneg = [r.take([4, GQ]) for _ in range(2)]
        self.mrest = [r.take([4, GQ]) for _ in range(2)]
        self.mrows = [r.take([512], BF16) for _ in range(2)]
        self.rden = r.take([4, GQ])
        u, n = self.units, len(self.terms)
        (self.w_in, self.wo_in, self.q_in, self.k_in, self.prod, self.rotm, self.qk_done, self.v_done,
         self.turned, self.part1, self.rest_done, self.part2, self.part3, self.parts_out0, self.parts_out1,
         self.pads, self.vp_in, self.max_prod, self.max_done, self.m_neg, self.m_chain, self.m_in0, self.m_in1,
         self.st, self.exp, self.pv, self.acc_out, self.tb, self.den, self.drained, self.biased) = \
            self.count(c, "attn", w_in=64, wo_in=64, q_in=16 * n * u, k_in=48 * u, prod=NT, rotm=3 * NT if hd == 8 else NT + 1,
            qk_done=NT, v_done=NT, turned=3 * NG, part1=3 * NG, rest_done=3 * NG, part2=3 * NG, part3=3 * NG,
            parts_out0=24 * NG, parts_out1=24 * NG, pads=2 + 5 * SLOTS, vp_in=u, max_prod=len(MAX_STEPS) * u,
            max_done=len(MAX_STEPS) * u, m_neg=10 * u, m_chain=2 * u, m_in0=16 * u, m_in1=16 * u,
            st=len(STEPS) * u, exp=len(STEPS) * u, pv=len(STEPS) * u, acc_out=2 * u, tb=4 * u, den=2 * u,
            drained=2 * u, biased=NT)
        self.parts_out = [self.parts_out0, self.parts_out1]
        self.m_in = [self.m_in0, self.m_in1]

    def all_parts_out(self, eng):
        for s in self.parts_out:
            eng.wait_ge(s.sem, s.at(16 * 3 * NG // 2))

    def first_parts_out(self, eng):
        for s in self.parts_out:
            eng.wait_ge(s.sem, s.at(16 * 3 * NG // 2 // NB))

    def every_unit(self, eng, unit, ahead=1):
        unit(0, 0, left=self.units - 1)
        rounds = (self.units - 1 - ahead) // SLOTS
        with eng.Fori(0, rounds) as k:
            for i in range(1, SLOTS + 1):
                unit(k * SLOTS + i, i % SLOTS, left=ahead)
        for u in range(1 + rounds * SLOTS, self.units):
            unit(u, u % SLOTS, left=self.units - 1 - u)


    def turned_max(self, u, half):
        if half == 1:
            return u * 4 + 2
        return 1 if isinstance(u, int) and u == 0 else u * 4

    def turned_out(self, u, half):
        if half == 0:
            return u * 4 + 3
        return u * 4 + (4 if isinstance(u, int) and u == self.units - 1 else 5)

    def sync(self, sp):
        d, hd = self.dram, self.hd
        for dst, src in ((self.w, d["w"].rearrange("(f p) n -> p f n", p=P)),
                         (self.cos, d["tables"][0].rearrange("(t p) n -> p t n", p=P)),
                         (self.sin, d["tables"][1].rearrange("(t p) n -> p t n", p=P)),
                         (self.bias, d["bias"].partition_broadcast(P))):
            sp.dma_start(dst, src).then_inc(self.w_in.sem, 16)
        for dst, src in ((self.wo, d["wo"].rearrange("(f p) n -> p f n", p=P)),
                         (self.bias_out, d["bias_out"].partition_broadcast(P)),
                         (self.mq, d["mq"]), (self.mk, d["mk"])):
            sp.dma_start(dst, src).then_inc(self.wo_in.sem, 16)
        def load(u, slot):
            for n, (a, b) in enumerate(self.terms):
                src = self.q_dram[a, bass.ds(u * (GQ * hd), GQ * hd), :].rearrange("(h d) t -> d h t", d=hd)
                sp.dma_start(self.qp[slot][hd * n:hd * n + hd, :, :], src).then_inc(self.q_in.sem, 16)
            row = 0
            for a in range(3):
                n = sum(1 for term in self.terms if term[0] == a)
                sp.dma_start(self.kp[slot][row:row + hd * n, :], self.k_dram[0:n, bass.ds(u * hd, hd), :])\
                    .then_inc(self.k_in.sem, 16)
                row += hd * n

        def load_max(u, half, slot):
            sp.wait_ge(self.m_chain.sem, self.m_chain.at(u * 2 + half + 1))
            sp.dma_start(self.qp[slot][KROWS:SROWS, :, 512 * half:512 * half + 512],
                         self.mrows[half][0:3 * GQ, :]).then_inc(self.m_in[half].sem, 16)

        for n in range(3 * NG):
            g, f = divmod(n, 3)
            b, at = divmod(512 * g, SEQ)
            rows = P if f < FT else QK_COLS - D
            if f < FT:
                dst = self.q_dram[:, b * D + P * f:b * D + P * f + P, at:at + 512]
            else:
                dst = self.k_dram[:, b * rows:b * rows + rows, at:at + 512]
            sp.wait_ge(self.part1.sem, self.part1.at(n + 1))
            sp.wait_ge(self.part2.sem, self.part2.at(n + 1))
            sp.wait_ge(self.part3.sem, self.part3.at(n + 1))
            sp.dma_start(dst.rearrange("a f t -> f a t"), self.parts[n % 2][0:rows, :, :]).then_inc(self.parts_out[n % 2].sem, 16)
            if n == 3 * NG - 4:
                self.first_parts_out(sp)
                sp.wait_ge(self.pads.sem, self.pads.at(2 + 5 * 2))
                load(0, 0)
        sp.wait_ge(self.q_in.sem, self.q_in.at(16 * len(self.terms)))
        sp.wait_ge(self.k_in.sem, self.k_in.at(48))
        load(1, 1)
        load_max(0, 0, 0)
        self.all_parts_out(sp)
        sp.wait_ge(self.pads.sem, self.pads.at(2 + 5 * SLOTS))

        def unit(u, slot, left):
            if left > 1:
                sp.wait_ge(self.max_prod.sem, self.max_prod.at((u + 1) * len(MAX_STEPS) + 1))
                load(u + 2, (slot + 2) % SLOTS)
            load_max(u, 1, slot)
            if left:
                load_max(u + 1, 0, (slot + 1) % SLOTS)

        self.every_unit(sp, unit, ahead=2)

    def gpsimd(self, pool):
        c, hd = self.c, self.hd
        self.ln.ready(pool, NG - 1)
        pads = [(parts, 0.0) for parts in self.mparts]
        for slot in range(SLOTS):
            pads += [(self.vp[slot], 0.0), (self.vp[slot][:, :, hd:hd + 1], 1.0),
                     (self.kp[slot][64:KROWS, :], 0.0), (self.kp[slot][KROWS:SROWS, :], 1.0),
                     (self.qp[slot][64:SROWS, :, :], 0.0)]
        for n, (rows, value) in enumerate(pads):
            if n == 12:
                pool.wait_ge(self.prod.sem, self.prod.at(NT))
            if n:
                pool.wait_ge(self.pads.sem, self.pads.at(n))
            pool.memset(rows, value).then_inc(self.pads.sem, 1)
        pool.wait_ge(self.pads.sem, self.pads.at(len(pads)))
        pool.wait_ge(self.wo_in.sem, self.wo_in.at(64))
        for t in range(NT):
            self.ln.normed(pool, t)
            pool.tensor_tensor(c.x[:, t, :], c.x[:, t, :], self.bias_out, ALU.add).then_inc(self.biased.sem, 1)
        v_flat = self.v.rearrange("p u b d -> p (u b d)")

        def copy_v(u, slot):
            pool.tensor_copy(self.vp[slot][:, :, 0:hd],
                             v_flat[:, bass.ds(u * (BT * hd), BT * hd)].rearrange("p (b d) -> p b d", d=hd))\
                .then_inc(self.vp_in.sem, 1)

        def unit(u, slot, left):
            if left:
                if not (isinstance(u, int) and u == 0):
                    pool.wait_ge(self.pv.sem, self.pv.at(u * len(STEPS)))
                copy_v(u + 1, (slot + 1) % SLOTS)

        pool.wait_ge(self.v_done.sem, self.v_done.at(NT))
        pool.wait_ge(self.pads.sem, self.pads.at(2 + 5 * SLOTS))
        copy_v(0, 0)
        self.every_unit(pool, unit)

    def vector(self, dve):
        c, hd = self.c, self.hd
        heads = QK_COLS // hd
        by_head = lambda z: z.rearrange("p (n d) -> p n d", d=hd)
        dve.wait_ge(self.w_in.sem, self.w_in.at(64))
        if hd != 8:
            dve.tensor_tensor(self.cos, self.cos, self.sin, ALU.add).then_inc(self.rotm.sem, 1)

        def rotate(t):
            bt = t % BT
            z = by_head(c.bank[t % 4][:, 0:QK_COLS])
            zv = by_head(c.bank[t % 4][:, QK_COLS:3 * P])
            a, b, out = self.rot[t % 2], self.rotb[t % 2], by_head(self.qk[t % 4])
            aa, bb = by_head(a), by_head(b)
            cos = over(self.cos[:, bt, :], 1, heads)
            v = self.v[:, (t // BT) * self.nkv:(t // BT + 1) * self.nkv, bt, :]
            dve.wait_ge(self.prod.sem, self.prod.at(t + 1))
            if t >= 4:
                dve.wait_ge(self.turned.sem, self.turned.at(3 * (t // 4)))
            if t >= 2:
                dve.wait_ge(self.qk_done.sem, self.qk_done.at(t - 1))
            if hd == 8:
                h = hd // 2
                dve.tensor_tensor(aa, z, cos, ALU.mult).then_inc(self.rotm.sem, 1)
                dve.tensor_tensor(bb[:, :, 0:h], z[:, :, h:hd], over(self.sin[:, bt, 0:h], 1, heads),
                                  ALU.mult).then_inc(self.rotm.sem, 1)
                dve.tensor_tensor(bb[:, :, h:hd], z[:, :, 0:h], over(self.sin[:, bt, h:hd], 1, heads),
                                  ALU.mult).then_inc(self.rotm.sem, 1)
                dve.tensor_copy(v, zv).then_inc(self.v_done.sem, 1)
                dve.wait_ge(self.rotm.sem, self.rotm.at(3 * t + 3))
                dve.tensor_tensor(out, aa, bb, ALU.add).then_inc(self.qk_done.sem, 1)
            else:
                dve.tensor_tensor(aa, z, by_head(self.bias[:, 0:QK_COLS]), ALU.add).then_inc(self.rotm.sem, 1)
                dve.tensor_tensor(v, zv, by_head(self.bias[:, QK_COLS:3 * P]), ALU.add).then_inc(self.v_done.sem, 1)
                dve.wait_ge(self.rotm.sem, self.rotm.at(t + 2))
                dve.tensor_tensor(out, aa, cos, ALU.mult).then_inc(self.qk_done.sem, 1)

        def cut(n):
            rows = P if n % 3 < FT else QK_COLS - D
            z, parts, rest = c.bank[4 + n % 4][0:rows, :], self.parts[n % 2][0:rows], self.rest[n % 2][0:rows]
            dve.wait_ge(self.part1.sem, self.part1.at(n + 1))
            if n >= 2:
                dve.wait_ge(self.part3.sem, self.part3.at(n - 1))
            dve.tensor_tensor(rest, z, parts[:, 0, :], ALU.subtract).then_inc(self.rest_done.sem, 1)
            dve.wait_ge(self.part2.sem, self.part2.at(n + 1))
            dve.tensor_tensor(parts[:, 2, :], rest, parts[:, 1, :], ALU.subtract).then_inc(self.part3.sem, 1)

        for g in range(NG + 1):
            if g < NG:
                for t in range(4 * g, 4 * g + 4):
                    rotate(t)
            if g:
                for f in range(3):
                    cut(3 * (g - 1) + f)
        self.all_parts_out(dve)

        def maxima(u, k0, k1):
            for k in range(k0, k1):
                half, i, h = MAX_STEPS[k]
                n = (i + 1) * P
                both = c.psum[:, 2 * (k % 2):2 * (k % 2) + 2, :]
                if half == 0:
                    src, dst = both[:, :, 0:n], self.mx[0][:, i, h:h + 2]
                else:
                    src, dst = both.rearrange("p a b -> p (a b)")[:, 0:n], self.mx[1][:, i - 4, h:h + 1]
                dve.wait_ge(self.max_prod.sem, self.max_prod.at(u * len(MAX_STEPS) + k + 1))
                dve.tensor_reduce(dst, src, AX_X, ALU.max).then_inc(self.max_done.sem, 1)

        def split_max(u, half):
            neg, rest = self.mneg[half], self.mrest[half]
            part = [self.mparts[half][:, :, GQ * i:GQ * i + GQ] for i in range(3)]
            done = u * 10 + 5 * half
            dve.wait_ge(self.max_done.sem, self.max_done.at(u * len(MAX_STEPS) + (8 if half == 0 else len(MAX_STEPS))))
            dve.tensor_scalar(neg, self.mx[half], -1.0, None, ALU.mult).then_inc(self.m_neg.sem, 1)
            dve.wait_ge(self.m_neg.sem, self.m_neg.at(done + 1))
            dve.tensor_copy(part[0], neg).then_inc(self.m_neg.sem, 1)
            dve.wait_ge(self.m_neg.sem, self.m_neg.at(done + 2))
            dve.tensor_tensor(rest, neg, part[0], ALU.subtract).then_inc(self.m_neg.sem, 1)
            dve.wait_ge(self.m_neg.sem, self.m_neg.at(done + 3))
            dve.tensor_copy(part[1], rest).then_inc(self.m_neg.sem, 1)
            dve.wait_ge(self.m_neg.sem, self.m_neg.at(done + 4))
            dve.tensor_tensor(part[2], rest, part[1], ALU.subtract).then_inc(self.m_neg.sem, 1)

        def rows_out(u, half):
            dve.wait_ge(self.tb.sem, self.tb.at(self.turned_max(u, half)))
            if not (isinstance(u, int) and u == 0):
                dve.wait_ge(self.m_in[half].sem, self.m_in[half].at(u * 16))
            dve.tensor_copy(self.mrows[half][0:3 * GQ, :],
                            c.bank[TURN_BANK][0:3 * GQ, 0:256].bitcast(BF16)).then_inc(self.m_chain.sem, 1)

        def normalize(u, half):
            z = c.bank[TURN_BANK].rearrange("p (i h e) -> p i h e", i=4, e=32)
            at = u * (GQ * hd) + (u // self.nkv) * (BT * D - D) + 4 * half * D
            dst = c.cx_pad[:, bass.ds(at, 4 * D)].rearrange("p (i n) -> p i n", i=4)[:, :, 0:GQ * hd]
            dve.wait_ge(self.tb.sem, self.tb.at(self.turned_out(u, half)))
            dve.reciprocal(self.rden, z[:, :, :, hd]).then_inc(self.den.sem, 1)
            dve.wait_ge(self.den.sem, self.den.at(u * 2 + half + 1))
            dve.tensor_tensor(dst.rearrange("p i (h d) -> p i h d", d=hd), z[:, :, :, 0:hd],
                              over(self.rden, 3, hd), ALU.mult).then_inc(self.drained.sem, 1)

        def unit(u, slot, left):
            if left:
                maxima(u + 1, 0, 2)
            if not (isinstance(u, int) and u == 0):
                normalize(u - 1, 1)
            rows_out(u, 1)
            if left:
                maxima(u + 1, 2, 8)
                split_max(u + 1, 0)
                maxima(u + 1, 8, 10)
            normalize(u, 0)
            if left:
                maxima(u + 1, 10, 11)
                rows_out(u + 1, 0)
                maxima(u + 1, 11, len(MAX_STEPS))
                split_max(u + 1, 1)

        maxima(0, 0, 8)
        split_max(0, 0)
        rows_out(0, 0)
        maxima(0, 8, len(MAX_STEPS))
        split_max(0, 1)
        self.every_unit(dve, unit)
        normalize(self.units - 1, 1)
        dve.wait_ge(self.biased.sem, self.biased.at(NT))

    def scalar(self, act):
        c = self.c
        for n in range(3 * NG):
            rows = P if n % 3 < FT else QK_COLS - D
            parts, rest = self.parts[n % 2][0:rows], self.rest[n % 2][0:rows]
            act.wait_ge(self.turned.sem, self.turned.at(n + 1))
            if n >= 2:
                act.wait_ge(self.parts_out[n % 2].sem, self.parts_out[n % 2].at(16 * (n // 2)))
            act.activation(parts[:, 0, :], c.bank[4 + n % 4][0:rows, :], ACT.Copy).then_inc(self.part1.sem, 1)
            act.wait_ge(self.rest_done.sem, self.rest_done.at(n + 1))
            act.activation(parts[:, 1, :], rest, ACT.Copy).then_inc(self.part2.sem, 1)
        act.wait_ge(self.pads.sem, self.pads.at(2 + 5 * SLOTS))

        def unit(u, slot, left):
            first = isinstance(u, int) and u == 0
            for s in range(len(STEPS)):
                act.wait_ge(self.st.sem, self.st.at(u * len(STEPS) + s + 1))
                if not (first and s < 3):
                    act.wait_ge(self.pv.sem, self.pv.at(u * len(STEPS) + (s - 2)))
                act.activation(self.p[s % 3].rearrange("p h t -> p (h t)"), c.bank[ST_BANK + s % 2][:, :], ACT.Exp,
                               scale=self.scale).then_inc(self.exp.sem, 1)
                for half, after, steps in ((0, 11, 10), (1, 35, 36)):
                    if s == after:
                        act.wait_ge(self.pv.sem, self.pv.at(u * len(STEPS) + steps))
                        if not (first and half == 0):
                            act.wait_ge(self.tb.sem, self.tb.at(self.turned_out(u, 0) if half else self.turned_out(u - 1, 1)))
                        act.activation(self.acc, c.bank[ACC_BANK][:, :], ACT.Copy).then_inc(self.acc_out.sem, 1)

        self.every_unit(act, unit)

    def tensor(self, pe):
        c, hd = self.c, self.hd
        pe.wait_ge(self.w_in.sem, self.w_in.at(64))

        def turn(g):
            pe.wait_ge(self.qk_done.sem, self.qk_done.at(4 * g + 4))
            self.ln.ready(pe, NG - 1)
            for f in range(3):
                n = 3 * g + f
                rows = P if f < FT else QK_COLS - D
                if n >= 4:
                    pe.wait_ge(self.rest_done.sem, self.rest_done.at(n - 3))
                for q in range(4):
                    mm = pe.transpose(c.bank[4 + n % 4][0:rows, P * q:P * q + P],
                                      self.qk[q][:, P * f:P * f + rows], c.identf[:, :])
                mm.then_inc(self.turned.sem, 1)

        for g in range(NG):
            self.ln.ready(pe, g)
            for t in range(4 * g, 4 * g + 4):
                if t >= 4:
                    pe.wait_ge(self.rotm.sem, self.rotm.at(3 * (t - 3) if hd == 8 else t - 2))
                    pe.wait_ge(self.v_done.sem, self.v_done.at(t - 3))
                for f in range(FT):
                    mm = pe.matmul(c.bank[t % 4][:, 0:3 * P], c.yt[:, f, P * t:P * t + P], self.w[:, f, :],
                                   start=(f == 0), stop=(f == FT - 1))
                mm.then_inc(self.prod.sem, 1)
            if g:
                turn(g - 1)
        turn(NG - 1)

        pe.wait_ge(self.rest_done.sem, self.rest_done.at(3 * NG))
        pe.wait_ge(self.v_done.sem, self.v_done.at(NT))
        pe.wait_ge(self.rotm.sem, self.rotm.at(3 * NT if hd == 8 else NT + 1))
        pe.wait_ge(self.wo_in.sem, self.wo_in.at(64))

        def max_scores(u, k, slot):
            half, i, h = MAX_STEPS[k]
            qp, kp = self.qp[slot], self.kp[slot]
            if k == 0:
                pe.wait_ge(self.q_in.sem, self.q_in.at((u + 1) * (16 * len(self.terms))))
                pe.wait_ge(self.k_in.sem, self.k_in.at((u + 1) * 48))
            if not (isinstance(u, int) and u == 0 and k < 2):
                pe.wait_ge(self.max_done.sem, self.max_done.at(u * len(MAX_STEPS) + (k - 1)))
            for b in range(2):
                bank = c.bank[2 * (k % 2) + b]
                head = h + b if half == 0 else h
                q = qp[0:KROWS, head, P * i:P * i + P]
                lo = 512 * b * half
                n = min(512, (i + 1) * P - lo)
                diag = half == 0 or b == 1
                mm = pe.matmul(bank[:, 0:n], q, kp[0:KROWS, lo:lo + n], start=True, stop=not diag,
                               skip_group_check=True)
                if diag:
                    mm = pe.matmul(bank[:, n - P:n], c.identb[:, :], self.mq, start=False, stop=True,
                                   skip_group_check=True)
            mm.then_inc(self.max_prod.sem, 1)

        def turn_max(u, half):
            pe.wait_ge(self.m_neg.sem, self.m_neg.at(u * 10 + (5 * half + 5)))
            if isinstance(u, int) and u == 0:
                if half == 1:
                    pe.wait_ge(self.m_chain.sem, self.m_chain.at(1))
            else:
                pe.wait_ge(self.drained.sem, self.drained.at(u * 2 if half else u * 2 - 1))
            for i in range(4):
                mm = pe.transpose(c.bank[TURN_BANK].bitcast(BF16)[:, P * i:P * i + P], self.mparts[half][:, i, :],
                                  c.identb[:, :])
            mm.then_inc(self.tb.sem, 1)

        def turn_out(u, half):
            pe.wait_ge(self.acc_out.sem, self.acc_out.at(u * 2 + half + 1))
            if half == 1 and isinstance(u, int) and u == self.units - 1:
                pe.wait_ge(self.drained.sem, self.drained.at(u * 2 + 1))
            else:
                pe.wait_ge(self.m_chain.sem, self.m_chain.at(u * 2 + half + 2))
            for i in range(4):
                mm = pe.transpose(c.bank[TURN_BANK][:, P * i:P * i + P], self.acc[:, P * i:P * i + P],
                                  c.identf[:, :])
            mm.then_inc(self.tb.sem, 1)

        def scores(u, s, slot, first):
            i, j = STEPS[s]
            if s == 0 or s == 10:
                rows_in = self.m_in[0 if s == 0 else 1]
                pe.wait_ge(rows_in.sem, rows_in.at((u + 1) * 16))
            if not (first and s < 2):
                pe.wait_ge(self.exp.sem, self.exp.at(u * len(STEPS) + (s - 1)))
            bank = c.bank[ST_BANK + s % 2]
            mm = pe.matmul(bank[:, :], self.kp[slot][0:SROWS, P * j:P * j + P],
                           self.qp[slot][0:SROWS, :, P * i:P * i + P],
                           start=True, stop=(j < i))
            if i == j:
                mm = pe.matmul(bank[:, :], c.identb[:, :], over(self.mk, 1, GQ), start=False, stop=True)
            mm.then_inc(self.st.sem, 1)

        def values(u, s, slot, first):
            i, j = STEPS[s]
            if s == 0:
                pe.wait_ge(self.vp_in.sem, self.vp_in.at(u + 1))
            if s == 10 or (s == 0 and not first):
                pe.wait_ge(self.acc_out.sem, self.acc_out.at(u * 2 + (1 if s else 0)))
            pe.wait_ge(self.exp.sem, self.exp.at(u * len(STEPS) + (s + 1)))
            for h in range(GQ):
                mm = pe.matmul(c.bank[ACC_BANK][32 * h:32 * h + 32, P * (i % 4):P * (i % 4) + P],
                               self.vp[slot][:, j, :], self.p[s % 3][:, h, :], start=(j == 0), stop=(j == i))
            mm.then_inc(self.pv.sem, 1)

        def unit(u, slot, left):
            first = isinstance(u, int) and u == 0
            for s in range(len(STEPS) + 2):
                if s < len(STEPS):
                    scores(u, s, slot, first)
                if s == 2 and not first:
                    turn_out(u - 1, 1)
                if s == 3:
                    turn_max(u, 1)
                if s == 14:
                    turn_out(u, 0)
                if s == 16 and left:
                    turn_max(u + 1, 0)
                if left and s < len(STEPS) and s % 3 < 2:
                    max_scores(u + 1, s - s // 3, (slot + 1) % SLOTS)
                if s >= 2:
                    values(u, s - 2, slot, first)

        for k in range(8):
            max_scores(0, k, 0)
        turn_max(0, 0)
        for k in range(8, len(MAX_STEPS)):
            max_scores(0, k, 0)
        self.every_unit(pe, unit)
        turn_out(self.units - 1, 1)

    def source(self, t, f):
        return self.c.cx[:, D * t + P * f:D * t + P * f + P]

    def finished(self, pe, g):
        if g == 0:
            pe.wait_ge(self.drained.sem, self.drained.at(2 * self.units))


class Choice(Stage):

    def __init__(self, c, kind, ln, experts, top, w, bias, carve, steps, **more):
        self.c, self.ln, self.e, self.top, self.dram_w, self.dram_b = c, ln, experts, top, w, bias
        r = carve
        self.w = r.take([FT, experts])
        self.b = r.take([experts])
        self.order = r.take([experts])
        t = lambda: r.take([NT, experts])
        self.z, self.pr, self.left, self.hit, self.comb, self.eq = t(), t(), t(), t(), t(), t()
        self.s = r.take([NT])
        self.rs = r.take([NT])
        self.steps = 0
        (self.w_in, self.prod, self.step, self.shifted, self.exp, self.orders, *self.more) = self.count(
            c, kind, w_in=16 * (1 + (bias is not None)), prod=1, step=6 + 5 * top + 3 * (top - 1) + steps, shifted=1,
            exp=1, orders=experts, **more)

    def sync(self, sp):
        sp.dma_start(self.w, self.dram_w.rearrange("(f p) e -> p f e", p=P)).then_inc(self.w_in.sem, 16)
        if self.dram_b is not None:
            sp.dma_start(self.b, self.dram_b.partition_broadcast(P)).then_inc(self.w_in.sem, 16)

    def w_loaded(self, eng):
        eng.wait_ge(self.w_in.sem, self.w_in.at(32 if self.dram_b is not None else 16))

    def gpsimd(self, pool):
        for e in range(self.e):
            pool.memset(self.order[:, e:e + 1], float(self.e - e)).then_inc(self.orders.sem, 1)

    def tensor(self, pe):
        c, e = self.c, self.e
        self.w_loaded(pe)
        for g in range(NG):
            self.ln.ready(pe, g)
            for t in range(4 * g, 4 * g + 4):
                for f in range(FT):
                    mm = pe.matmul(c.bank[2][:, e * t:e * t + e], c.yt[:, f, P * t:P * t + P], self.w[:, f, :],
                                   start=(f == 0), stop=(f == FT - 1))
        mm.then_inc(self.prod.sem, 1)

    def scalar(self, act):
        act.wait_ge(self.shifted.sem, self.shifted.at(1))
        act.activation(self.pr, self.z, ACT.Exp).then_inc(self.exp.sem, 1)

    def then(self, dve, ins):
        self.steps += 1
        ins.then_inc(self.step.sem, 1)
        dve.wait_ge(self.step.sem, self.step.at(self.steps))

    def choose(self, dve):
        c, e = self.c, self.e
        wide = lambda v: over(v, 2, e)
        by_token = lambda v: over(v, 1, NT)
        logits = c.bank[2][:, 0:NT * e].rearrange("p (t e) -> p t e", e=e)
        dve.wait_ge(self.prod.sem, self.prod.at(1))
        self.w_loaded(dve)
        if self.dram_b is not None:
            self.then(dve, dve.tensor_tensor(self.z, logits, by_token(self.b), ALU.add))
        else:
            self.then(dve, dve.tensor_copy(self.z, logits))
        self.then(dve, dve.tensor_reduce(self.s, self.z, AX_X, ALU.max))
        dve.tensor_tensor(self.z, self.z, wide(self.s), ALU.subtract).then_inc(self.shifted.sem, 1)
        dve.wait_ge(self.exp.sem, self.exp.at(1))
        self.then(dve, dve.tensor_reduce(self.s, self.pr, AX_X, ALU.add))
        self.then(dve, dve.reciprocal(self.rs, self.s))
        self.then(dve, dve.tensor_tensor(self.pr, self.pr, wide(self.rs), ALU.mult))
        dve.wait_ge(self.orders.sem, self.orders.at(e))
        left = self.pr
        for k in range(self.top):
            self.then(dve, dve.tensor_reduce(self.s, left, AX_X, ALU.max))
            self.then(dve, dve.tensor_tensor(self.eq, left, wide(self.s), ALU.is_equal))
            self.then(dve, dve.tensor_tensor(self.eq, self.eq, by_token(self.order), ALU.mult))
            self.then(dve, dve.tensor_reduce(self.s, self.eq, AX_X, ALU.max))
            self.then(dve, dve.tensor_tensor(self.hit, self.eq, wide(self.s), ALU.is_equal))
            if k == 0:
                self.then(dve, dve.tensor_tensor(self.comb, self.pr, self.hit, ALU.mult))
            if k + 1 < self.top:
                self.then(dve, dve.scalar_tensor_tensor(out=self.left.rearrange("p t e -> p (t e)"),
                                              in0=self.hit.rearrange("p t e -> p (t e)"), scalar=-2.0,
                                              in1=self.pr.rearrange("p t e -> p (t e)"), op0=ALU.mult, op1=ALU.add))
                left = self.left
            if k:
                self.then(dve, dve.tensor_tensor(self.eq, self.pr, self.hit, ALU.mult))
                self.then(dve, dve.tensor_tensor(self.comb, self.comb, self.eq, ALU.add))


class Gate(Choice):

    def __init__(self, c, ln, experts, top, shared, w, bias, carve):
        super().__init__(c, "gate", ln, experts, top, w, bias, carve, 3 + 2 * shared, ready_cut=1, turned=1, rows_set=2,
                         rows_clear=1)
        self.ready_cut, self.turned, self.rows_set, self.rows_clear = self.more
        self.n, self.shared = experts + shared, shared
        r = carve
        self.cut = r.take([NT, 3, self.n], BF16)
        self.rest = r.take([NT, self.n])
        self.rows = r.take([NTOK], BF16)

    def gpsimd(self, pool):
        super().gpsimd(pool)
        pool.memset(self.rows, 0.0).then_inc(self.rows_clear.sem, 1)

    def turn(self, pe):
        c = self.c
        pe.wait_ge(self.ready_cut.sem, self.ready_cut.at(1))
        for t in range(NT):
            bank = c.bank[4 + t // 8].bitcast(BF16)
            mm = pe.transpose(bank[0:3 * self.n, P * (t % 8):P * (t % 8) + P],
                              self.cut[:, t, :, :].rearrange("p a e -> p (a e)"), c.identb[:, :])
        mm.then_inc(self.turned.sem, 1)

    def scalar(self, act):
        super().scalar(act)
        act.wait_ge(self.turned.sem, self.turned.at(1))
        act.wait_ge(self.rows_clear.sem, self.rows_clear.at(1))
        for h in range(2):
            act.activation(self.rows[0:3 * self.n, 1024 * h:1024 * h + 1024],
                           self.c.bank[4 + h].bitcast(BF16)[0:3 * self.n, :], ACT.Copy).then_inc(self.rows_set.sem, 1)

    def vector(self, dve):
        self.choose(dve)
        e, then = self.e, self.then
        if self.shared:
            then(dve, dve.memset(self.cut, 0.0))
            then(dve, dve.memset(self.cut[:, :, 0, e:e + 1], 1.0))
        rest = self.rest[:, :, 0:e]
        then(dve, dve.tensor_copy(self.cut[:, :, 0, 0:e], self.comb))
        then(dve, dve.tensor_tensor(rest, self.comb, self.cut[:, :, 0, 0:e], ALU.subtract))
        then(dve, dve.tensor_copy(self.cut[:, :, 1, 0:e], rest))
        dve.tensor_tensor(self.cut[:, :, 2, 0:e], rest, self.cut[:, :, 1, 0:e], ALU.subtract)\
            .then_inc(self.ready_cut.sem, 1)


class Routed(Choice):

    def __init__(self, c, ln, experts, weights, w, bias, const, carve):
        tiles = NT + experts - 1
        super().__init__(
            c, "routed", ln, experts, 1, w, bias, carve, 10 + experts - 1, const_in=64, hits=1, before=1, places=1, owners=1,
            scattered=16 * NT, y_in=16 * tiles, y_turned=tiles, y_set=tiles, gprod=2 * tiles, uprod=2 * tiles,
            silu=2 * tiles, h_done=2 * tiles, h_turned=2 * tiles, ht0=tiles, ht1=tiles, down=tiles, o_set=tiles,
            o_out=16 * tiles, gathered0=64, gathered1=64, gathered2=64, gathered3=64, added=NT)
        (self.const_in, self.hits, self.before, self.places, self.owners, self.scattered, self.y_in, self.y_turned,
         self.y_set, self.gprod, self.uprod, self.silu, self.h_done, self.h_turned, self.ht0, self.ht1, self.down,
         self.o_set, self.o_out, *gathered, self.added) = self.more
        self.gathered = gathered
        self.tiles, self.weights, self.const, self.hidden = tiles, weights, const, weights.hidden // experts
        self.wg, self.wu = weights.wg, weights.wu
        self.wd = weights.wd.rearrange("p j d -> p (j d)")
        assert self.hidden == 1024 and experts * (NT + 1) <= 512
        r = carve
        e = experts
        self.hitb = r.take([NT, e], BF16)
        self.lower = r.take([P], BF16)
        self.ones = r.take([P], BF16)
        self.edges = r.take([NT])
        self.numbers = r.take([tiles])
        self.over_edge = r.take([e, NT])
        self.shares = r.take([e])
        self.starts = r.take([e])
        self.start_rows = r.take([e])
        self.place = r.take([NT, e])
        self.placef = r.take([NT])
        self.placei = r.take([NT]).bitcast(U32)
        self.past = r.take([tiles, e - 1])
        self.ownerf = r.take([tiles])
        self.owner = r.take([tiles]).bitcast(U32)
        self.weight = r.take([NT])
        self.y = r.take([D])
        self.yt = r.take([FT, P])
        self.g = r.take([self.hidden])
        self.h = r.take([self.hidden])
        self.ht = r.take([self.hidden // P, P])
        self.o = r.take([D])


    def every_tile(self, eng, step):
        step(0, True, False)
        with eng.Fori(1, self.tiles - 1) as k:
            step(k, False, False)
        step(self.tiles - 1, False, True)

    def sync(self, sp):
        super().sync(sp)
        c, q = self.c, self.const
        for dst, src in ((self.lower, q["lower"]), (self.ones, q["ones"]),
                         (self.edges, q["edges"].partition_broadcast(P)),
                         (self.numbers, q["numbers"].partition_broadcast(P))):
            sp.dma_start(dst, src).then_inc(self.const_in.sem, 16)
        sp.wait_ge(self.scattered.sem, self.scattered.at(16 * NT))

        def load(k):
            sp.dma_start(self.y, c.sorted[bass.ds(k * P, P), :]).then_inc(self.y_in.sem, 16)

        def store(k):
            sp.wait_ge(self.o_set.sem, self.o_set.at(k + 1))
            sp.dma_start(c.results[bass.ds(k * P, P), :], self.o).then_inc(self.o_out.sem, 16)

        def step(k, first, last):
            if not last:
                sp.wait_ge(self.y_turned.sem, self.y_turned.at(k + 1))
                load(k + 1)
            if not first:
                store(k - 1)

        load(0)
        self.every_tile(sp, step)
        store(self.tiles - 1)

    def gpsimd(self, pool):
        super().gpsimd(pool)
        c = self.c
        pool.wait_ge(self.places.sem, self.places.at(1))
        pool.wait_ge(c.zeros_out, 16)
        for t in range(NT):
            self.ln.normed(pool, t)
            pool.indirect_dma_start(c.sorted[:, :], bass.IndirectOffsetOnAxis(ap=self.placei[:, t:t + 1], axis=0),
                                    c.yn[:, t, :], None).then_inc(self.scattered.sem, 16)
        pool.wait_ge(self.o_out.sem, self.o_out.at(16 * self.tiles))
        for t in range(NT):
            pool.indirect_dma_start(c.yn[:, t, :], None, c.results[:, :],
                                    bass.IndirectOffsetOnAxis(ap=self.placei[:, t:t + 1], axis=0))\
                .then_inc(self.gathered[t // 4].sem, 16)

    def tensor(self, pe):
        super().tensor(pe)
        c, e = self.c, self.e
        before = c.bank[3]
        pe.wait_ge(self.const_in.sem, self.const_in.at(64))
        pe.wait_ge(self.hits.sem, self.hits.at(1))
        pe.matmul(before[:, 0:NT * e], self.lower, self.hitb.rearrange("p t e -> p (t e)"), start=True, stop=False,
                  skip_group_check=True)
        pe.matmul(before[:, NT * e:NT * e + e], self.ones, self.hitb[:, NT - 1, :], start=False, stop=False,
                  skip_group_check=True)
        for t in range(NT - 1):
            mm = pe.matmul(before[:, e * (t + 1):e * (NT + 1)], self.ones, over(self.hitb[:, t, :], 1, NT - t),
                           start=False, stop=(t == NT - 2), skip_group_check=True)
        mm.then_inc(self.before.sem, 1)
        self.weights.wait(pe)
        pe.wait_ge(self.owners.sem, self.owners.at(1))

        def owner(k):
            return pe.value_load(self.owner[0:1, bass.ds(k, 1)], min_val=0, max_val=e - 1)

        def turn_y(k):
            pe.wait_ge(self.y_in.sem, self.y_in.at(16 * (k + 1)))
            for f in range(FT):
                mm = pe.transpose(c.bank[6][:, P * f:P * f + P], self.y[:, P * f:P * f + P], c.identf[:, :])
            mm.then_inc(self.y_turned.sem, 1)

        def up(k):
            own = owner(k)
            pe.wait_ge(self.y_set.sem, self.y_set.at(k + 1))
            for half in range(2):
                for w, bank, done in ((self.wg, c.bank[half], self.gprod), (self.wu, c.bank[2 + half], self.uprod)):
                    for f in range(FT):
                        mm = pe.matmul(bank[:, :], self.yt[:, f, :],
                                       w[:, f, bass.ds(own * self.hidden + 512 * half, 512)],
                                       start=(f == 0), stop=(f == FT - 1))
                    mm.then_inc(done.sem, 1)

        def turn_h(k):
            for half in range(2):
                pe.wait_ge(self.h_done.sem, self.h_done.at(2 * k + half + 1))
                for q in range(4):
                    at = 512 * half + P * q
                    mm = pe.transpose(c.bank[4 + half][:, P * q:P * q + P], self.h[:, at:at + P], c.identf[:, :])
                mm.then_inc(self.h_turned.sem, 1)

        def down(k, first):
            own = owner(k)
            pe.wait_ge(self.ht0.sem, self.ht0.at(k + 1))
            pe.wait_ge(self.ht1.sem, self.ht1.at(k + 1))
            if not first:
                pe.wait_ge(self.o_set.sem, self.o_set.at(k))
            last = self.hidden // P - 1
            for j in range(last + 1):
                mm = pe.matmul(c.bank[7][:, 0:D], self.ht[:, j, :], self.wd[:, bass.ds((own * (last + 1) + j) * D, D)],
                               start=(j == 0), stop=(j == last))
            mm.then_inc(self.down.sem, 1)

        def step(k, first, last):
            up(k)
            if not last:
                turn_y(k + 1)
            if not first:
                down(k - 1, isinstance(k, int) and k == 1)
            turn_h(k)

        turn_y(0)
        step(0, True, False)
        step(1, False, False)
        with pe.Fori(2, self.tiles - 1) as k:
            step(k, False, False)
        step(self.tiles - 1, False, True)
        down(self.tiles - 1, False)

    def scalar(self, act):
        super().scalar(act)
        c = self.c

        def out(k, first):
            act.wait_ge(self.down.sem, self.down.at(k + 1))
            if not first:
                act.wait_ge(self.o_out.sem, self.o_out.at(16 * k))
            act.activation(self.o, c.bank[7][:, 0:D], ACT.Copy).then_inc(self.o_set.sem, 1)

        def step(k, first, last):
            for half in range(2):
                act.wait_ge(self.gprod.sem, self.gprod.at(2 * k + half + 1))
                act.activation(self.g[:, 512 * half:512 * half + 512], c.bank[half][:, :], ACT.Silu)\
                    .then_inc(self.silu.sem, 1)
            if not first:
                out(k - 1, isinstance(k, int) and k == 1)
            act.wait_ge(self.h_turned.sem, self.h_turned.at(2 * k + 1))
            act.activation(self.ht[:, 0:4, :].rearrange("p j t -> p (j t)"), c.bank[4][:, :], ACT.Copy)\
                .then_inc(self.ht0.sem, 1)

        step(0, True, False)
        step(1, False, False)
        with act.Fori(2, self.tiles - 1) as k:
            step(k, False, False)
        step(self.tiles - 1, False, True)
        out(self.tiles - 1, False)

    def vector(self, dve):
        c, e, then = self.c, self.e, self.then
        self.choose(dve)
        dve.tensor_copy(self.hitb, self.hit).then_inc(self.hits.sem, 1)
        then(dve, dve.tensor_reduce(self.weight, self.comb, AX_X, ALU.max))
        before = c.bank[3][:, 0:e * (NT + 1)].rearrange("p (t e) -> p t e", e=e)
        dve.wait_ge(self.const_in.sem, self.const_in.at(64))
        dve.wait_ge(self.before.sem, self.before.at(1))
        then(dve, dve.tensor_tensor(self.over_edge, over(before[:, NT, :], 2, NT), over(self.edges, 1, e), ALU.is_gt))
        then(dve, dve.tensor_reduce(self.shares, self.over_edge, AX_X, ALU.add))
        then(dve, dve.memset(self.starts, 0.0))
        for k in range(1, e):
            then(dve, dve.tensor_tensor(self.starts[:, k:k + 1], self.starts[:, k - 1:k], self.shares[:, k - 1:k],
                                        ALU.add))
        then(dve, dve.tensor_scalar(self.start_rows, self.starts, float(P), None, ALU.mult))
        then(dve, dve.tensor_tensor(self.place, before[:, 0:NT, :], over(self.start_rows, 1, NT), ALU.add))
        then(dve, dve.tensor_tensor(self.place, self.place, self.hit, ALU.mult))
        then(dve, dve.tensor_reduce(self.placef, self.place, AX_X, ALU.add))
        dve.tensor_copy(self.placei, self.placef).then_inc(self.places.sem, 1)
        then(dve, dve.tensor_tensor(self.past, over(self.numbers, 2, e - 1), over(self.starts[:, 1:e], 1, self.tiles),
                                    ALU.is_ge))
        then(dve, dve.tensor_reduce(self.ownerf, self.past, AX_X, ALU.add))
        dve.tensor_copy(self.owner, self.ownerf).then_inc(self.owners.sem, 1)

        def set_y(k):
            dve.wait_ge(self.y_turned.sem, self.y_turned.at(k + 1))
            dve.tensor_copy(self.yt.rearrange("p f t -> p (f t)"), c.bank[6][:, 0:D]).then_inc(self.y_set.sem, 1)

        def step(k, first, last):
            for half in range(2):
                at = slice(512 * half, 512 * half + 512)
                dve.wait_ge(self.uprod.sem, self.uprod.at(2 * k + half + 1))
                dve.wait_ge(self.silu.sem, self.silu.at(2 * k + half + 1))
                dve.tensor_tensor(self.h[:, at], c.bank[2 + half][:, :], self.g[:, at], ALU.mult)\
                    .then_inc(self.h_done.sem, 1)
            if not last:
                set_y(k + 1)
            dve.wait_ge(self.h_turned.sem, self.h_turned.at(2 * k + 2))
            dve.tensor_copy(self.ht[:, 4:8, :].rearrange("p j t -> p (j t)"), c.bank[5][:, :])\
                .then_inc(self.ht1.sem, 1)

        set_y(0)
        self.every_tile(dve, step)
        for t in range(NT):
            if t % 4 == 0:
                dve.wait_ge(self.gathered[t // 4].sem, self.gathered[t // 4].at(64))
            dve.scalar_tensor_tensor(out=c.x[:, t, :], in0=c.yn[:, t, :], scalar=self.weight[:, t:t + 1],
                                     in1=c.x[:, t, :], op0=ALU.mult, op1=ALU.add).then_inc(self.added.sem, 1)
        dve.wait_ge(self.added.sem, self.added.at(NT))


class Experts(Stage):

    def __init__(self, c, name, ln, gate, hidden, weights, weights_in, spread, carve):
        self.c, self.ln, self.gate, self.hidden = c, ln, gate, hidden
        self.wg, self.wu, self.wd = weights
        self.weights_in = weights_in
        self.nj = -(-hidden // P)
        r = carve
        self.spread_dram = spread
        self.spread = r.take([hidden], BF16)
        self.act_g = [r.take([512]) for _ in range(2)]
        self.gu = [r.take([512]) for _ in range(2)]
        self.h = [r.take([512]) for _ in range(3)]
        n = self.nj * NG
        (self.spread_in, self.gprod, self.silu, self.mul, self.cprod, self.h_done, self.down, self.added) = \
            self.count(c, "experts", spread_in=16, gprod=n, silu=n, mul=n, cprod=n, h_done=n, down=n, added=NT)

    def sync(self, sp):
        sp.dma_start(self.spread[0:96, :], self.spread_dram).then_inc(self.spread_in.sem, 16)

    def rows(self, j):
        return min(P, self.hidden - P * j)


    def tensor(self, pe):
        c, nj = self.c, self.nj
        self.weights_in(pe)
        pe.wait_ge(self.spread_in.sem, self.spread_in.at(16))

        def up(g, j):
            n, m = g * nj + j, self.rows(j)
            if isinstance(n, int) and n < 2:
                pass
            else:
                pe.wait_ge(self.mul.sem, self.mul.at(n - 1))
            for k, w in enumerate((self.wg, self.wu)):
                bank = c.bank[2 * (j % 2) + k][0:m, :]
                for f in range(FT):
                    mm = pe.matmul(bank, w[:, f, P * j:P * j + m], c.yt[:, f, bass.ds(g * 512, 512)],
                                   start=(f == 0), stop=(f == FT - 1))
            mm.then_inc(self.gprod.sem, 1)

        def weigh(g, j, first):
            n, m = g * nj + j, self.rows(j)
            if not (first and j < 2):
                pe.wait_ge(self.h_done.sem, self.h_done.at(n - 1))
            pe.matmul(c.bank[4 + j % 2][0:m, :], self.spread[0:96, P * j:P * j + m],
                      self.gate.rows[0:96, bass.ds(g * 512, 512)], start=True, stop=True).then_inc(self.cprod.sem, 1)

        def down(g, j):
            n, m = g * nj + j, self.rows(j)
            pe.wait_ge(self.h_done.sem, self.h_done.at(n + 1))
            for q in range(4):
                mm = pe.matmul(c.bank[6 + q // 2][:, D * (q % 2):D * (q % 2) + D],
                               self.h[j % 3][0:m, P * q:P * q + P], self.wd[0:m, j, :],
                               start=(j == 0 and q % 2 == 0), stop=(j == nj - 1), skip_group_check=True)
            mm.then_inc(self.down.sem, 1)

        def group(g, first=False):
            for j in range(nj + 2):
                if j < nj:
                    up(g, j)
                if first and j == 0:
                    self.gate.turn(pe)
                    pe.wait_ge(self.gate.rows_set.sem, self.gate.rows_set.at(2))
                if j < nj:
                    weigh(g, j, first)
                if j == 2 and not first:
                    pe.wait_ge(self.added.sem, self.added.at(g * 4))
                if j >= 2:
                    down(g, j - 2)

        group(0, first=True)
        with pe.Fori(1, NG) as g:
            group(g)

    def scalar(self, act):
        c, nj = self.c, self.nj

        def group(g, first=False):
            for j in range(nj):
                n, m = g * nj + j, self.rows(j)
                act.wait_ge(self.gprod.sem, self.gprod.at(n + 1))
                if not (first and j < 2):
                    act.wait_ge(self.mul.sem, self.mul.at(n - 1))
                act.activation(self.act_g[j % 2][0:m, :], c.bank[2 * (j % 2)][0:m, :], ACT.Silu).then_inc(self.silu.sem, 1)

        group(0, first=True)
        with act.Fori(1, NG) as g:
            group(g)

    def vector(self, dve):
        c, nj = self.c, self.nj

        def group(g, first=False):
            for j in range(nj):
                n, m = g * nj + j, self.rows(j)
                dve.wait_ge(self.silu.sem, self.silu.at(n + 1))
                if not (first and j < 2):
                    dve.wait_ge(self.h_done.sem, self.h_done.at(n - 1))
                dve.tensor_tensor(self.gu[j % 2][0:m, :], c.bank[2 * (j % 2) + 1][0:m, :], self.act_g[j % 2][0:m, :],
                                  ALU.mult).then_inc(self.mul.sem, 1)
                dve.wait_ge(self.mul.sem, self.mul.at(n + 1))
                dve.wait_ge(self.cprod.sem, self.cprod.at(n + 1))
                if j >= 3:
                    dve.wait_ge(self.down.sem, self.down.at(n - 2))
                elif not first:
                    dve.wait_ge(self.down.sem, self.down.at(g * nj))
                dve.tensor_tensor(self.h[j % 3][0:m, :], c.bank[4 + j % 2][0:m, :], self.gu[j % 2][0:m, :],
                                  ALU.mult).then_inc(self.h_done.sem, 1)
            dve.wait_ge(self.down.sem, self.down.at(g * nj + nj))
            xf = c.x[:, :, :].rearrange("p t d -> p (t d)")
            for half in range(2):
                xs = xf[:, bass.ds(g * (4 * D) + 2 * D * half, 2 * D)]
                dve.tensor_tensor(xs, c.bank[6 + half][:, :], xs, ALU.add).then_inc(self.added.sem, 2)

        group(0, first=True)
        with dve.Fori(1, NG) as g:
            group(g)
        dve.wait_ge(self.added.sem, self.added.at(NT))


class KeyedSum(Stage):

    def __init__(self, c, name, ln, w, bias, cos, sin, wo, bias_out):
        self.c, self.ln = c, ln
        self.dram = (w, bias, cos, sin, wo, bias_out)
        r = Carve(c.region["a"])
        self.w = r.take([FT, 3 * D])
        self.bias = r.take([3 * D])
        self.cos = r.take([BT, P])
        self.sin = r.take([BT, P])
        self.wo = r.take([FT, D])
        self.bias_out = r.take([D])
        self.k = r.take([NT, D])
        self.ta = [r.take([2, P]) for _ in range(2)]
        self.tb = [r.take([2, P]) for _ in range(2)]
        self.ws = [r.take([FT, D]) for _ in range(NB)]
        self.ones = r.take([1])
        self.ss = r.take([NT])
        self.norm = r.take([NT])
        self.rnorm = r.take([NT])
        (self.w_in, self.prod, self.lin, self.v_done, self.cosm, self.sinm, self.rot, self.square, self.root,
         self.floor, self.rec, self.kv, self.sums, self.scaled, self.xy, self.biased, self.one) = (
            c.sem(f"{name}_{n}") for n in
            "w_in prod lin v_done cosm sinm rot square root floor rec kv sums scaled xy biased one".split())

    def sync(self, sp):
        w, bias, cos, sin, wo, bias_out = self.dram
        for dst, src in ((self.w, w.rearrange("(f p) n -> p f n", p=P)), (self.bias, bias.partition_broadcast(P)),
                         (self.cos, cos.rearrange("(t p) n -> p t n", p=P)),
                         (self.sin, sin.rearrange("(t p) n -> p t n", p=P)),
                         (self.wo, wo.rearrange("(f p) n -> p f n", p=P)),
                         (self.bias_out, bias_out.partition_broadcast(P))):
            sp.dma_start(dst, src).then_inc(self.w_in, 16)

    def gpsimd(self, pool):
        c = self.c
        pool.wait_ge(self.w_in, 96)
        pool.memset(self.ones, 1.0).then_inc(self.one, 1)
        for t in range(NT):
            self.ln.normed(pool, t)
            pool.tensor_tensor(c.x[:, t, :], c.x[:, t, :], c.yn[:, t, :], ALU.add).then_inc(self.xy, 1)
            pool.wait_ge(self.xy, t + 1)
            pool.tensor_tensor(c.x[:, t, :], c.x[:, t, :], self.bias_out, ALU.add).then_inc(self.biased, 1)
        for b in range(NB):
            s = slice(b * BT, b * BT + BT)
            pool.wait_ge(self.square, (b + 1) * BT)
            pool.tensor_tensor(self.norm[:, s], self.ss[:, s], c.half[:, s], ALU.pow).then_inc(self.root, 1)

    def tensor(self, pe):
        c = self.c
        pe.wait_ge(self.w_in, 96)
        for g in range(NG):
            self.ln.ready(pe, g)
            for t in range(4 * g, 4 * g + 4):
                if t >= 2:
                    pe.wait_ge(self.lin, 2 * (t - 1))
                    pe.wait_ge(self.v_done, t - 1)
                for bank, lo, n in ((2 * (t % 2), D, 2 * D), (2 * (t % 2) + 1, 0, D)):
                    for f in range(FT):
                        mm = pe.matmul(c.bank[bank][:, 0:n], c.yt[:, f, P * t:P * t + P], self.w[:, f, lo:lo + n],
                                       start=(f == 0), stop=(f == FT - 1))
                mm.then_inc(self.prod, 1)
        pe.wait_ge(self.one, 1)
        for b in range(NB):
            pe.wait_ge(self.kv, (b + 1) * BT)
            for f in range(FT):
                for t in range(b * BT, b * BT + BT):
                    mm = pe.matmul(c.bank[4 + b][:, f:f + 1], self.k[:, t, P * f:P * f + P], self.ones,
                                   start=(t == b * BT), stop=(t == b * BT + BT - 1))
            mm.then_inc(self.sums, 1)

    def scalar(self, act):
        c = self.c
        self.ln.ready(act, NG - 1)
        for t in range(NT):
            act.wait_ge(self.rot, 2 * t + 2)
            if t:
                act.wait_ge(self.square, t)
            act.activation(c.bank[6][:, 0:D], self.k[:, t, :], ACT.Square,
                           accum_out=self.ss[:, t:t + 1]).then_inc(self.square, 1)

    def vector(self, dve):
        c = self.c
        dve.wait_ge(self.w_in, 96)
        cx = c.cx[:, :].rearrange("p (t d) -> p t d", d=D)

        def product(b):
            s = slice(b * BT, b * BT + BT)
            dve.wait_ge(self.root, b + 1)
            dve.tensor_scalar(self.norm[:, s], self.norm[:, s], 1e-12, None, ALU.max).then_inc(self.floor, 1)
            dve.wait_ge(self.floor, b + 1)
            dve.reciprocal(self.rnorm[:, s], self.norm[:, s]).then_inc(self.rec, 1)
            dve.wait_ge(self.rec, b + 1)
            for t in range(b * BT, b * BT + BT):
                dve.scalar_tensor_tensor(out=self.k[:, t, :], in0=self.k[:, t, :], scalar=self.rnorm[:, t:t + 1],
                                         in1=c.yn[:, t, :], op0=ALU.mult, op1=ALU.mult).then_inc(self.kv, 1)

        for t in range(NT):
            kv, q = c.bank[2 * (t % 2)], c.bank[2 * (t % 2) + 1]
            bt = t % BT
            dve.wait_ge(self.prod, t + 1)
            dve.tensor_tensor(cx[:, t, :], q[:, 0:D], self.bias[:, 0:D], ALU.add).then_inc(self.lin, 1)
            dve.tensor_tensor(self.k[:, t, :], kv[:, 0:D], self.bias[:, D:2 * D], ALU.add).then_inc(self.lin, 1)
            dve.wait_ge(self.xy, t + 1)
            self.ln.ready(dve, t // 4)
            dve.tensor_tensor(c.yn[:, t, :], kv[:, D:2 * D], self.bias[:, 2 * D:3 * D], ALU.add).then_inc(self.v_done, 1)
            dve.wait_ge(self.lin, 2 * t + 2)
            if t >= 2:
                dve.wait_ge(self.rot, 2 * t - 2)
            a, b = self.ta[t % 2], self.tb[t % 2]
            sin = self.sin[:, bt, :].rearrange("p (n e) -> p n e", e=2)
            for n, z in enumerate((cx[:, t, 0:P], self.k[:, t, 0:P])):
                pair = z.rearrange("p (n e) -> p n e", e=2)
                bp = b[:, n, :].rearrange("p (n e) -> p n e", e=2)
                dve.tensor_tensor(a[:, n, :], z, self.cos[:, bt, :], ALU.mult).then_inc(self.cosm, 1)
                for e in range(2):
                    dve.tensor_tensor(bp[:, :, e], pair[:, :, 1 - e], sin[:, :, e], ALU.mult).then_inc(self.sinm, 1)
            dve.wait_ge(self.cosm, 2 * t + 2)
            dve.wait_ge(self.sinm, 4 * t + 4)
            for n, z in enumerate((cx[:, t, 0:P], self.k[:, t, 0:P])):
                dve.tensor_tensor(z, a[:, n, :], b[:, n, :], ALU.add).then_inc(self.rot, 1)
            if t == BT + 1:
                dve.wait_ge(self.v_done, BT)
                product(0)
        dve.wait_ge(self.v_done, NT)
        product(1)
        for b in range(NB):
            dve.wait_ge(self.sums, b + 1)
            for f in range(FT):
                dve.tensor_scalar(self.ws[b][:, f, :], self.wo[:, f, :], c.bank[4 + b][:, f:f + 1], None,
                                  ALU.mult).then_inc(self.scaled, 1)
        dve.wait_ge(self.biased, NT)

    def source(self, t, f):
        return self.c.cx[:, D * t + P * f:D * t + P * f + P]

    def out_weights(self, t, f):
        return self.ws[t // BT][:, f, :]

    def finished(self, pe, g):
        if g == 0:
            pe.wait_ge(self.rot, 2 * NT)
            pe.wait_ge(self.scaled, NB * FT)


class LinearAttention(Stage):

    HEAD = 16
    EPS = 1e-6

    def __init__(self, c, name, ln, wq, wkv, bq, bkv, wo, bo, decay, block, member, at):
        self.c, self.ln = c, ln
        self.dram = (wq, wkv, bq, bkv, wo, bo, decay, block, member)
        r = Carve(c.region["a"])
        self.wq = r.take([FT, D])
        self.wkv = r.take([FT, 2 * D])
        self.wo = r.take([FT, D])
        self.bq = r.take([FT])
        self.bkv = r.take([2 * D])
        self.bo = r.take([D])
        self.decay = r.take([BT])
        self.block = r.take([P])
        self.member = r.take([P // self.HEAD])
        self.kt = [r.take([D]) for _ in range(2)]
        self.nh = P // self.HEAD
        self.bd = [r.take([FT, P + self.nh]) for _ in range(NB)]
        self.den = [r.take([FT, self.nh]) for _ in range(2)]
        self.rden = [r.take([FT, self.nh]) for _ in range(2)]
        self.k = r.take([NT, D])
        r = Carve(c.region["w"], at)
        self.v = r.take([NT, FT, P + 1])
        self.qt = r.take([FT, NTOK])
        (self.w_in, self.qprod, self.q_done, self.kvprod, self.k_lin, self.v_done, self.k_done, self.one,
         self.sums, self.bd_done, self.outp, self.dn, self.rc, self.rd, self.o_done, self.biased) = (
            c.sem(f"{name}_{n}") for n in
            "w_in qprod q_done kvprod k_lin v_done k_done one sums bd_done outp dn rc rd o_done biased".split())

    def sync(self, sp):
        wq, wkv, bq, bkv, wo, bo, decay, block, member = self.dram
        for dst, src in ((self.wq, wq.rearrange("(f p) n -> p f n", p=P)),
                         (self.wkv, wkv.rearrange("(f p) n -> p f n", p=P)),
                         (self.wo, wo.rearrange("(f p) n -> p f n", p=P)), (self.bq, bq),
                         (self.bkv, bkv.partition_broadcast(P)), (self.bo, bo.partition_broadcast(P)),
                         (self.decay, decay), (self.block, block), (self.member, member)):
            sp.dma_start(dst, src).then_inc(self.w_in, 16)

    W_IN = 9 * 16

    def gpsimd(self, pool):
        c = self.c
        pool.wait_ge(self.w_in, self.W_IN)
        pool.memset(self.v[:, :, :, P:P + 1], 1.0).then_inc(self.one, 1)
        for t in range(NT):
            self.ln.normed(pool, t)
            pool.tensor_tensor(c.x[:, t, :], c.x[:, t, :], self.bo, ALU.add).then_inc(self.biased, 1)

    def tensor(self, pe):
        c, nh = self.c, self.nh
        pe.wait_ge(self.w_in, self.W_IN)
        for g in range(NG):
            self.ln.ready(pe, g)
            for o in range(FT):
                if g:
                    pe.wait_ge(self.q_done, FT * (g - 1) + o + 1)
                for f in range(FT):
                    mm = pe.matmul(c.bank[o][:, :], self.wq[:, f, P * o:P * o + P], c.yt[:, f, 512 * g:512 * g + 512],
                                   start=(f == 0), stop=(f == FT - 1))
                mm.then_inc(self.qprod, 1)
            for t in range(4 * g, 4 * g + 4):
                if t >= 2:
                    pe.wait_ge(self.k_lin, t - 1)
                    pe.wait_ge(self.v_done, t - 1)
                for f in range(FT):
                    mm = pe.matmul(c.bank[2 + t % 2][:, :], c.yt[:, f, P * t:P * t + P], self.wkv[:, f, :],
                                   start=(f == 0), stop=(f == FT - 1))
                mm.then_inc(self.kvprod, 1)
        pe.wait_ge(self.one, 1)
        for b in range(NB):
            pe.wait_ge(self.k_done, (b + 1) * BT)
            pe.wait_ge(self.v_done, (b + 1) * BT)
            for f in range(FT):
                for t in range(b * BT, b * BT + BT):
                    mm = pe.matmul(c.bank[4 + b][:, D * f:D * f + P + 1], self.k[:, t, P * f:P * f + P],
                                   self.v[:, t, f, :], start=(t == b * BT), stop=(t == b * BT + BT - 1))
            mm.then_inc(self.sums, 1)
        pe.wait_ge(self.q_done, FT * NG)
        for t in range(NT):
            pe.wait_ge(self.bd_done, 2 * FT * (t // BT + 1))
            if t >= 4:
                pe.wait_ge(self.o_done, t - 3)
            for f in range(FT):
                mm = pe.matmul(c.bank[t % 4][:, (P + nh) * f:(P + nh) * (f + 1)], self.qt[:, f, P * t:P * t + P],
                               self.bd[t // BT][:, f, :], start=True, stop=True)
            mm.then_inc(self.outp, 1)

    def scalar(self, act):
        c = self.c
        act.wait_ge(self.w_in, self.W_IN)
        for g in range(NG):
            for o in range(FT):
                act.wait_ge(self.qprod, FT * g + o + 1)
                act.activation(self.qt[:, o, 512 * g:512 * g + 512], c.bank[o][:, :], ACT.Relu,
                               bias=self.bq[:, o:o + 1]).then_inc(self.q_done, 1)

    def vector(self, dve):
        c, nh = self.c, self.nh
        dve.wait_ge(self.w_in, self.W_IN)
        halves = lambda z: z.rearrange("p (f e) -> p f e", f=FT)
        for t in range(NT):
            z = c.bank[2 + t % 2]
            dve.wait_ge(self.kvprod, t + 1)
            if t >= 2:
                dve.wait_ge(self.k_done, t - 1)
            dve.tensor_tensor(self.kt[t % 2], z[:, 0:D], self.bkv[:, 0:D], ALU.add).then_inc(self.k_lin, 1)
            dve.tensor_tensor(self.v[:, t, :, 0:P], halves(z[:, D:2 * D]), halves(self.bkv[:, D:2 * D]),
                              ALU.add).then_inc(self.v_done, 1)
            dve.wait_ge(self.k_lin, t + 1)
            dve.tensor_scalar(self.k[:, t, :], self.kt[t % 2], 0.0, self.decay[:, t % BT:t % BT + 1], ALU.max,
                              ALU.mult).then_inc(self.k_done, 1)
        for b in range(NB):
            dve.wait_ge(self.sums, b + 1)
            for f in range(FT):
                z = c.bank[4 + b][:, D * f:D * f + P + 1]
                dve.tensor_tensor(self.bd[b][:, f, 0:P], z[:, 0:P], self.block, ALU.mult).then_inc(self.bd_done, 1)
                dve.tensor_scalar(self.bd[b][:, f, P:P + nh], self.member, z[:, P:P + 1], None,
                                  ALU.mult).then_inc(self.bd_done, 1)
        for t in range(NT):
            z = c.bank[t % 4][:, 0:FT * (P + nh)].rearrange("p (f e) -> p f e", f=FT)
            den, rden = self.den[t % 2], self.rden[t % 2]
            decay = self.decay[:, t % BT:t % BT + 1]
            dve.wait_ge(self.outp, t + 1)
            dve.tensor_scalar(den, z[:, :, P:P + nh], decay, self.EPS, ALU.mult, ALU.add).then_inc(self.dn, 1)
            dve.wait_ge(self.dn, t + 1)
            dve.reciprocal(rden, den).then_inc(self.rc, 1)
            dve.wait_ge(self.rc, t + 1)
            dve.tensor_scalar(den, rden, decay, None, ALU.mult).then_inc(self.rd, 1)
            dve.wait_ge(self.rd, t + 1)
            dve.tensor_tensor(c.cx[:, D * t:D * t + D].rearrange("p (f h e) -> p f h e", f=FT, h=nh),
                              z[:, :, 0:P].rearrange("p f (h e) -> p f h e", h=nh), over(den, 3, self.HEAD),
                              ALU.mult).then_inc(self.o_done, 1)
        dve.wait_ge(self.biased, NT)

    def source(self, t, f):
        return self.c.cx[:, D * t + P * f:D * t + P * f + P]

    def finished(self, pe, g):
        pe.wait_ge(self.o_done, 4 * g + 4 if g else NT)


class Weights(Stage):

    def __init__(self, c, name, wg, wu, wd, hidden):
        self.c, self.hidden, self.dram = c, hidden, (wg, wu, wd)
        r = Carve(c.region["w"])
        self.nj = -(-hidden // P)
        self.wg, self.wu, self.wd = r.take([FT, hidden]), r.take([FT, hidden]), r.take([self.nj, D])
        self.end = r.at
        self.loaded = c.sem(name + "_loaded")

    def sync(self, sp):
        wg, wu, wd = self.dram
        full = self.hidden // P
        sp.dma_start(self.wg, wg.rearrange("(f p) n -> p f n", p=P)).then_inc(self.loaded, 16)
        sp.dma_start(self.wu, wu.rearrange("(f p) n -> p f n", p=P)).then_inc(self.loaded, 16)
        sp.dma_start(self.wd[:, 0:full, :], wd[0:full * P, :].rearrange("(j p) n -> p j n", p=P)).then_inc(self.loaded, 16)
        if full < self.nj:
            sp.dma_start(self.wd[0:self.hidden - full * P, full, :], wd[full * P:, :]).then_inc(self.loaded, 16)

    def wait(self, eng):
        eng.wait_ge(self.loaded, 16 * (3 + (self.hidden % P > 0)))


class After(Stage):

    def __init__(self, sem, count):
        self.sem, self.count = sem, count

    def sync(self, sp):
        sp.wait_ge(self.sem, self.count)

    gpsimd = sync


class Finish(Stage):
    def __init__(self, c, out, added, count):
        self.c, self.out, self.added, self.count, self.out_done = c, out, added, count, c.sem("out_done")

    def sync(self, sp):
        out = self.out.rearrange("b (t p) d -> p (b t) d", p=P)
        sp.wait_ge(self.added, self.count)
        for g in range(NG):
            sp.dma_start(out[:, 4 * g:4 * g + 4, :], self.c.x[:, 4 * g:4 * g + 4, :]).then_inc(self.out_done, 16)
        sp.wait_ge(self.out_done, 16 * NG)


def build(nc, t, out):
    with ExitStack() as ctx:
        c = Core(nc, ctx)
        stages = [Start(c, t["x"], t["identf"], t["identb"])]
        w0 = Weights(c, "w0", t["f0_wg"], t["f0_wu"], t["f0_wd"], t["f0_wg"].shape[1])
        w1 = Weights(c, "w1", t["f1_wg"], t["f1_wu"], t["f1_wd"], t["f1_wg"].shape[1])
        last = [None]
        counts = {"ln": 0, "project": 0}

        def begin(name):
            if last[0] is not None:
                stages.append(After(*last[0]))
            ln = LayerNorm(c, counts["ln"])
            counts["ln"] += 1
            stages.append(ln)
            return ln

        def project(name, mixer, w):
            p = Project(c, counts["project"], mixer.source, w, mixer.finished)
            counts["project"] += 1
            stages.append(p)
            last[0] = (p.added, NT * counts["project"])

        def attention(name, hd, w, wo, tables, bias, bias_out):
            ln = begin(name)
            a = Attention(c, name, ln, hd, t[w], t[wo], (t[tables + "_cos"], t[tables + "_sin"]), t[bias], t[bias_out],
                          t["mask_q"], t["mask_k"])
            stages.append(a)
            project(name, a, lambda tt, f: a.wo[:, f, :])

        def experts(name, weights, n, top, shared, w, bias, spread):
            ln = begin(name)
            r = Carve(c.region["a"])
            gate = Gate(c, ln, n, top, shared, t[w], t[bias] if bias else None, r)
            e = Experts(c, name, ln, gate, weights.hidden, (weights.wg, weights.wu, weights.wd), weights.wait,
                        t[spread], r)
            stages.extend([gate, e])
            last[0] = (e.added.sem, e.added.at(NT))

        def routed(name, weights, n, w, bias):
            ln = begin(name)
            m = Routed(c, ln, n, weights, t[w], t[bias], t, Carve(c.region["a"]))
            stages.append(m)
            last[0] = (m.added.sem, m.added.at(NT))

        def s1():
            attention("a0", 8, "a0_w", "a0_wo", "a0", "a0_bias", "a0_bo")

        def s2():
            routed("f0", w0, 4, "f0_wr", "f0_br")

        def s3():
            ln = begin("b0")
            m = KeyedSum(c, "b0", ln, t["b0_w"], t["b0_bias"], t["b0_cos"], t["b0_sin"], t["b0_wo"], t["b0_bo"])
            stages.append(m)
            project("b0", m, m.out_weights)

        def s4():
            routed("f0b", w0, 4, "f0_wr", "f0_br")

        def s5():
            ln = begin("a1")
            stages.append(w1)
            m = LinearAttention(c, "a1", ln, t["a1_wq"], t["a1_wkv"], t["a1_bq"], t["a1_bkv"], t["a1_wo"], t["a1_bo"],
                                t["decay"], t["block"], t["member"], w1.end)
            stages.append(m)
            project("a1", m, lambda tt, f: m.wo[:, f, :])

        def s6():
            experts("f1", w1, 8, 2, True, "f1_gate", None, "spread1")

        def s7():
            attention("b1", 16, "b1_w", "b1_wo", "b1", "b1_bias", "b1_bo")

        def s8():
            experts("f1b", w1, 8, 2, True, "f1_gate", None, "spread1")

        stages.append(w0)
        for stage in (s1, s2, s3, s4, s5, s6, s7, s8):
            stage()
        stages.append(Finish(c, out, *last[0]))

        block = ctx.enter_context(nc.Block())

        @block.sync
        def _(sp):
            for s in stages:
                s.sync(sp)

        @block.gpsimd
        def _(pool):
            for s in stages:
                s.gpsimd(pool)

        @block.scalar
        def _(act):
            for s in stages:
                s.scalar(act)

        @block.tensor
        def _(pe):
            for s in stages:
                s.tensor(pe)

        @block.vector
        def _(dve):
            for s in stages:
                s.vector(dve)



def constants():
    import numpy as np

    f = np.float32
    bf = mybir.dt.np(BF16)
    pos = np.arange(SEQ, dtype=f)
    out = {}

    inv = (f(1) / np.power(f(10000), np.arange(0, 8, 2, dtype=f) / f(8))).astype(f)
    th = np.outer(pos, inv).astype(f)
    out["a0_cos"] = np.concatenate([np.cos(th), np.cos(th)], 1)
    out["a0_sin"] = np.concatenate([-np.sin(th), np.sin(th)], 1)

    inv = (f(1) / np.power(f(10000), np.arange(0, P, 2, dtype=f) / f(P))).astype(f)
    th = np.repeat(pos[:, None] * inv[None, :], 2, 1).astype(f)
    sign = np.tile(np.array([-1, 1], f), P // 2)
    out["b0_cos"], out["b0_sin"] = np.cos(th), np.sin(th) * sign

    inv = np.power(f(10000), f(-2) * np.arange(8, dtype=f) / f(16)).astype(f)
    th = (pos[:, None] * inv[None, :]).astype(f)
    out["b1_cos"], out["b1_sin"] = np.tile(np.cos(th), (1, 2)), np.tile(np.sin(th), (1, 2))

    out["decay"] = np.exp(-pos / f(SEQ)).reshape(BT, P).T
    q = np.arange(P)
    out["mask_q"] = np.where(q[None, :] > q[:, None], f(NEG), f(0)).astype(bf)
    out["mask_k"] = out["mask_q"].T
    out["block"] = (q[:, None] // 16 == q[None, :] // 16).astype(f)
    out["member"] = (q[:, None] // 16 == np.arange(8)[None, :]).astype(f)
    out["identf"] = np.eye(P, dtype=f)
    out["identb"] = np.eye(P, dtype=f).astype(bf)
    owner1 = np.concatenate([np.repeat(np.arange(8), 176), np.full(352, 8)])
    s = np.zeros((96, len(owner1)), f)
    for part in range(3):
        s[part * 9 + owner1, np.arange(len(owner1))] = 1
    out["spread1"] = s.astype(bf)
    out["lower"] = (q[:, None] < q[None, :]).astype(bf)
    out["ones"] = np.ones((P, P), bf)
    out["edges"] = np.arange(NT, dtype=f) * P
    out["numbers"] = np.arange(NT + L0_EXPERTS - 1, dtype=f)
    out["a0_bias"] = np.zeros(3 * P, f)
    return {k: np.ascontiguousarray(v) for k, v in out.items()}


def kernel(**i):
    import numpy as np
    import concourse.bacc as bacc
    from concourse.bass_utils import run_bass_kernel_spmd

    i = {k: np.asarray(v) for k, v in i.items()}
    cat = lambda *a: np.concatenate(a, -1)
    by_feature = lambda w: np.transpose(w, (1, 0, 2)).reshape(w.shape[1], -1)
    arrays = {
        "x": i["L0_attn_a_x"],
        "a0_w": cat(i["L0_attn_a_Wq"], i["L0_attn_a_Wk"], i["L0_attn_a_Wv"]),
        "a0_wo": i["L0_attn_a_Wo"], "a0_bo": i["L0_attn_a_b_out"],
        "f0_wr": i["L0_ffn_Wr"], "f0_br": i["L0_ffn_br"],
        "f0_wg": by_feature(i["L0_ffn_Wg"]), "f0_wu": by_feature(i["L0_ffn_Wu"]),
        "f0_wd": i["L0_ffn_Wd"].reshape(-1, D),
        "b0_w": i["L0_attn_b_W_in"].T, "b0_bias": i["L0_attn_b_b_in"],
        "b0_wo": i["L0_attn_b_W_out"].T, "b0_bo": i["L0_attn_b_b_out"],
        "a1_wq": i["L1_attn_a_Wq"].T, "a1_wkv": cat(i["L1_attn_a_Wk"].T, i["L1_attn_a_Wv"].T),
        "a1_bq": i["L1_attn_a_bq"].reshape(FT, P).T, "a1_bkv": cat(i["L1_attn_a_bk"], i["L1_attn_a_bv"]),
        "a1_wo": i["L1_attn_a_Wo"].T, "a1_bo": i["L1_attn_a_bo"],
        "f1_gate": i["L1_ffn_gate_w"],
        "f1_wg": cat(by_feature(i["L1_ffn_w_gate"]), i["L1_ffn_sw_gate"]),
        "f1_wu": cat(by_feature(i["L1_ffn_w_up"]), i["L1_ffn_sw_up"]),
        "f1_wd": np.concatenate([i["L1_ffn_w_down"].reshape(-1, D), i["L1_ffn_sw_down"]], 0),
        "b1_w": cat(i["L1_attn_b_Wq"].T, i["L1_attn_b_Wk"].T, i["L1_attn_b_Wv"].T),
        "b1_bias": cat(i["L1_attn_b_bq"], i["L1_attn_b_bk"], i["L1_attn_b_bv"]),
        "b1_wo": i["L1_attn_b_Wo"].T, "b1_bo": i["L1_attn_b_bo"],
        **constants(),
    }
    arrays = {"in_" + k: np.ascontiguousarray(v) for k, v in arrays.items()}
    nc = bacc.Bacc("TRN2", target_bir_lowering=False, num_devices=1)
    tensors = {k[3:]: nc.dram_tensor(k, v.shape, mybir.dt.from_np(v.dtype), kind="ExternalInput").ap()
               for k, v in arrays.items()}
    out = nc.dram_tensor("out", [NB, SEQ, D], F32, kind="ExternalOutput").ap()
    build(nc, tensors, out)
    r = run_bass_kernel_spmd(nc, [arrays], core_ids=[0])
    return r.results[0]["out"]
```

```python
from contextlib import ExitStack

import concourse.bass as bass
from concourse import mybir

ALU = mybir.AluOpType
ACT = mybir.ActivationFunctionType
AX_X = mybir.AxisListType.X
F32 = mybir.dt.float32
BF16 = mybir.dt.bfloat16
U32 = mybir.dt.uint32

P = 128
D = 256
FT = D // P
NB, SEQ = 2, 1024
NTOK = NB * SEQ
NT = NTOK // P
BT = SEQ // P
NG = NT // 4
LN_EPS = 1e-5
L1_TILES = 2 * NT + 8 - 1
RING = 3
GQ = 4
QK_COLS = D + D // GQ
NEG = -1e30
KROWS = 96
SROWS = KROWS + 3
STEPS = [(i, j) for i in range(BT) for j in range(i + 1)]
MAX_STEPS = [(0, i, h) for i in range(4) for h in (0, 2)] + [(1, i, h) for i in range(4, 8) for h in range(GQ)]
SLOTS = 3
ST_BANK, ACC_BANK, TURN_BANK = 4, 6, 7


class Core:

    def __init__(self, nc, ctx):
        self.nc, self.ctx, self.shared, self.counted = nc, ctx, {}, {}
        self.x = self.sb("x_res", [P, NT, D], F32)
        self.yn = self.sb("y_norm", [P, NT, D], F32)
        self.yt = self.sb("y_t", [P, FT, NTOK], F32)
        self.cx_pad = self.sb("ctx", [P, NT * D + D], F32)
        self.cx = self.cx_pad[:, 0:NT * D]
        self.stats = self.sb("ln_stats", [P, NT, 6], F32)
        self.mv = self.sb("ln_mv", [P, NT, 2], F32)
        self.rstd = self.sb("ln_rstd", [P, NT], F32)
        self.vareps = self.sb("ln_vareps", [P, NT], F32)
        self.mhalf = self.sb("minus_half", [P, NT], F32)
        self.half = self.sb("plus_half", [P, NT], F32)
        self.identf = self.sb("identf", [P, P], F32)
        self.identb = self.sb("identb", [P, P], BF16)
        self.region = {"w": self.sb("region_w", [P, 24576], F32), "a": self.sb("region_a", [P, 11450], F32)}
        self.psum = ctx.enter_context(nc.psum_tensor("psum", [P, 8, 512], F32))
        self.bank = [self.psum[:, i, :] for i in range(8)]
        self.sorted = nc.dram_tensor("sorted_rows", [L1_TILES * P, D], F32, kind="Internal").ap()
        self.results = nc.dram_tensor("result_rows", [L1_TILES * P, D], F32, kind="Internal").ap()
        self.zeros_out = self.sem("zeros_out")

    def sb(self, name, shape, dt):
        return self.ctx.enter_context(self.nc.sbuf_tensor(name, shape, dt))

    def sem(self, name):
        return self.ctx.enter_context(self.nc.semaphore(name))

    def shared_sem(self, name):
        if name not in self.shared:
            self.shared[name] = self.sem(name)
        return self.shared[name]


class Carve:

    def __init__(self, region, at=0):
        self.region, self.at = region, at

    def take(self, free, dt=F32, parts=P):
        n = 1
        for f in free:
            n *= f
        words = n if dt == F32 else (n + 1) // 2
        v = self.region[0:parts, self.at:self.at + words]
        self.at += words
        assert self.at <= self.region.shape[1], self.at
        if dt != F32:
            v = v.bitcast(dt)
        if len(free) == 2:
            v = v.rearrange("p (a b) -> p a b", a=free[0])
        if len(free) == 3:
            v = v.rearrange("p (a b c) -> p a b c", a=free[0], b=free[1])
        return v


def over(ap, axis, n):
    shape = list(ap.shape)
    return ap.unsqueeze(axis).to_broadcast(shape[:axis] + [n] + shape[axis:])


class Counted:

    def __init__(self, sem, base):
        self.sem, self.base = sem, base

    def at(self, n):
        return n + self.base if self.base else n


class Stage:

    def count(self, c, kind, **totals):
        counted = []
        for name, total in totals.items():
            key = f"{kind}_{name}"
            sem, base = c.counted.get(key) or (c.sem(key), 0)
            counted.append(Counted(sem, base))
            c.counted[key] = (sem, base + total)
        return counted

    def sync(self, sp): pass
    def gpsimd(self, pool): pass
    def scalar(self, act): pass
    def tensor(self, pe): pass
    def vector(self, dve): pass


class Start(Stage):

    def __init__(self, c, x, identf, identb):
        self.c, self.x_dram, self.identf, self.identb = c, x, identf, identb
        self.x_in = c.sem("x_in")
        self.const_in = c.sem("const_in")
        self.consts = c.sem("consts_set")
        self.zeros = c.cx_pad[:, NT * D:NT * D + D]

    def sync(self, sp):
        c = self.c
        sp.dma_start(c.identf[:, :], self.identf).then_inc(self.const_in, 16)
        sp.dma_start(c.identb[:, :], self.identb).then_inc(self.const_in, 16)
        x = self.x_dram.rearrange("b (t p) d -> p (b t) d", p=P)
        for g in range(NG):
            sp.dma_start(c.x[:, 4 * g:4 * g + 4, :], x[:, 4 * g:4 * g + 4, :]).then_inc(self.x_in, 16)
        sp.wait_ge(self.consts, 3)
        sp.dma_start(c.sorted.rearrange("(n p) d -> p n d", p=P), over(self.zeros, 1, c.sorted.shape[0] // P))\
            .then_inc(c.zeros_out, 16)

    def gpsimd(self, pool):
        c = self.c
        pool.memset(c.mhalf[:, :], -0.5).then_inc(self.consts, 1)
        pool.memset(c.half[:, :], 0.5).then_inc(self.consts, 1)
        pool.memset(self.zeros, 0.0).then_inc(self.consts, 1)
        pool.wait_ge(self.consts, 3)

    def vector(self, dve):
        dve.wait_ge(self.x_in, 16 * NG)

    def tensor(self, pe):
        pe.wait_ge(self.const_in, 32)


class LayerNorm(Stage):


    def __init__(self, c, k):
        self.c, self.k = c, k
        self.stat = c.shared_sem("ln_stat")
        self.aggr = c.shared_sem("ln_aggr")
        self.veps = c.shared_sem("ln_veps")
        self.rstd = c.shared_sem("ln_rstd")
        self.norm = c.shared_sem("ln_norm")
        self.turned = c.shared_sem("ln_turned")
        self.yt0 = c.shared_sem("ln_yt0")
        self.yt1 = c.shared_sem("ln_yt1")

    def ready(self, eng, g):
        eng.wait_ge(self.yt0, NG * self.k + g + 1)
        eng.wait_ge(self.yt1, NG * self.k + g + 1)

    def normed(self, eng, t):
        eng.wait_ge(self.norm, NT * self.k + t + 1)

    def vector(self, dve):
        c, k = self.c, self.k
        for t in range(NT):
            dve.bn_stats(c.stats[:, t, :], c.x[:, t, :]).then_inc(self.stat, 1)
        for t in range(NT):
            dve.wait_ge(self.stat, NT * k + t + 1)
            dve.bn_aggr(c.mv[:, t, :], c.stats[:, t, :]).then_inc(self.aggr, 1)

        def copies(g):
            dve.wait_ge(self.turned, FT * (NG * k + g + 1))
            dve.tensor_copy(c.yt[:, 1, 512 * g:512 * g + 512], c.bank[5 + 2 * (g % 2)][:, :]).then_inc(self.yt1, 1)

        for g in range(NG):
            dve.wait_ge(self.rstd, NG * k + g + 1)
            for t in range(4 * g, 4 * g + 4):
                dve.tensor_scalar(c.yn[:, t, :], c.x[:, t, :], c.mv[:, t, 0:1], c.rstd[:, t:t + 1],
                                  ALU.subtract, ALU.mult).then_inc(self.norm, 1)
            if g:
                copies(g - 1)
        copies(NG - 1)

    def gpsimd(self, pool):
        c, k = self.c, self.k
        for g in range(NG):
            s = slice(4 * g, 4 * g + 4)
            pool.wait_ge(self.aggr, NT * k + 4 * g + 4)
            pool.tensor_scalar(c.vareps[:, s], c.mv[:, s, 1], LN_EPS, None, ALU.add).then_inc(self.veps, 1)
            pool.wait_ge(self.veps, NG * k + g + 1)
            pool.tensor_tensor(c.rstd[:, s], c.vareps[:, s], c.mhalf[:, s], ALU.pow).then_inc(self.rstd, 1)

    def tensor(self, pe):
        c, k = self.c, self.k
        for g in range(NG):
            self.normed(pe, 4 * g + 3)
            for f in range(FT):
                if g >= 2:
                    pe.wait_ge([self.yt0, self.yt1][f], NG * k + g - 1)
                for q in range(4):
                    mm = pe.transpose(c.bank[4 + 2 * (g % 2) + f][:, P * q:P * q + P],
                                      c.yn[:, 4 * g + q, P * f:P * f + P], c.identf[:, :])
                mm.then_inc(self.turned, 1)

    def scalar(self, act):
        c, k = self.c, self.k
        for g in range(NG):
            act.wait_ge(self.turned, FT * (NG * k + g) + 1)
            act.activation(c.yt[:, 0, 512 * g:512 * g + 512], c.bank[4 + 2 * (g % 2)][:, :],
                           ACT.Copy).then_inc(self.yt0, 1)


class Project(Stage):


    def __init__(self, c, k, source, w, before):
        self.c, self.k, self.source, self.w, self.before = c, k, source, w, before
        self.turned = c.shared_sem("project_turned")
        self.ot0 = c.shared_sem("project_ot0")
        self.ot1 = c.shared_sem("project_ot1")
        self.prod = c.shared_sem("project_prod")
        self.added = c.shared_sem("project_added")

    def tensor(self, pe):
        c, k = self.c, self.k

        def turn(g):
            self.before(pe, g)
            for f in range(FT):
                if g >= 2:
                    pe.wait_ge([self.ot0, self.ot1][f], NG * k + g - 1)
                for q in range(4):
                    mm = pe.transpose(c.bank[4 + 2 * (g % 2) + f][:, P * q:P * q + P],
                                      self.source(4 * g + q, f), c.identf[:, :])
                mm.then_inc(self.turned, 1)

        def multiply(g):
            pe.wait_ge(self.ot0, NG * k + g + 1)
            pe.wait_ge(self.ot1, NG * k + g + 1)
            for q in range(4):
                t = 4 * g + q
                if t >= 4:
                    pe.wait_ge(self.added, NT * k + t - 3)
                for f in range(FT):
                    mm = pe.matmul(c.bank[q][:, 0:D], c.yt[:, f, P * t:P * t + P], self.w(t, f),
                                   start=(f == 0), stop=(f == FT - 1))
                mm.then_inc(self.prod, 1)

        for g in range(NG):
            turn(g)
            if g:
                multiply(g - 1)
        multiply(NG - 1)

    def scalar(self, act):
        c, k = self.c, self.k
        for g in range(NG):
            act.wait_ge(self.turned, FT * (NG * k + g) + 1)
            act.activation(c.yt[:, 0, 512 * g:512 * g + 512], c.bank[4 + 2 * (g % 2)][:, :],
                           ACT.Copy).then_inc(self.ot0, 1)

    def vector(self, dve):
        c, k = self.c, self.k

        def adds(g):
            for t in range(4 * g, 4 * g + 4):
                dve.wait_ge(self.prod, NT * k + t + 1)
                dve.tensor_tensor(c.x[:, t, :], c.bank[t % 4][:, 0:D], c.x[:, t, :], ALU.add).then_inc(self.added, 1)

        for g in range(NG):
            dve.wait_ge(self.turned, FT * (NG * k + g + 1))
            dve.tensor_copy(c.yt[:, 1, 512 * g:512 * g + 512], c.bank[5 + 2 * (g % 2)][:, :]).then_inc(self.ot1, 1)
            if g:
                adds(g - 1)
        adds(NG - 1)
        dve.wait_ge(self.added, NT * (k + 1))


class Attention(Stage):

    def __init__(self, c, name, ln, hd, w, wo, tables, bias, bias_out, mask_q, mask_k):
        self.c, self.ln, self.hd = c, ln, hd
        self.nkv = D // GQ // hd
        self.units = NB * self.nkv
        self.scale = float(hd) ** -0.5
        self.dram = dict(w=w, wo=wo, tables=tables, bias=bias, bias_out=bias_out, mq=mask_q, mk=mask_k)
        pairs = [(a, b) for a in range(3) for b in range(3)]
        self.terms = pairs if hd == 8 else [(a, b) for a, b in pairs if a + b <= 2]
        assert len(self.terms) * hd <= KROWS
        nc = c.nc
        self.q_dram = nc.dram_tensor(name + "_q", [3, NB * D, SEQ], BF16, kind="Internal").ap()
        self.k_dram = nc.dram_tensor(name + "_k", [3, NB * D // GQ, SEQ], BF16, kind="Internal").ap()
        r = Carve(c.region["a"])
        self.wo = r.take([FT, D])
        self.v = r.take([self.units, BT, hd])
        self.bias_out = r.take([D])
        self.mq = r.take([P], BF16)
        self.mk = r.take([P], BF16)
        self.kp = [r.take([SEQ], BF16) for _ in range(SLOTS)]
        self.vp = [r.take([BT, 32]) for _ in range(SLOTS)]
        self.mparts = [r.take([4, P], BF16) for _ in range(2)]
        yn, yt = Carve(c.yn.rearrange("p t d -> p (t d)")), Carve(c.yt[:, 0, :])
        self.qp = [at.take([GQ, SEQ], BF16) for at in (yn, yn, yt)]
        both = r.at
        self.w = r.take([FT, 3 * P])
        self.cos = r.take([BT, hd])
        self.sin = r.take([BT, hd])
        self.bias = r.take([3 * P])
        self.rot = [r.take([QK_COLS]) for _ in range(2)]
        self.rotb = [r.take([QK_COLS]) for _ in range(2)]
        self.qk = [r.take([QK_COLS]) for _ in range(4)]
        self.parts = [r.take([3, 512], BF16) for _ in range(2)]
        self.rest = [r.take([512]) for _ in range(2)]
        r = Carve(c.region["a"], both)
        self.p = [r.take([GQ, P]) for _ in range(3)]
        self.acc = r.take([512])
        self.mx = [r.take([4, GQ]) for _ in range(2)]
        self.mneg = [r.take([4, GQ]) for _ in range(2)]
        self.mrest = [r.take([4, GQ]) for _ in range(2)]
        self.mrows = [r.take([512], BF16) for _ in range(2)]
        self.rden = r.take([4, GQ])
        u, n = self.units, len(self.terms)
        (self.w_in, self.wo_in, self.q_in, self.k_in, self.prod, self.rotm, self.qk_done, self.v_done,
         self.turned, self.part1, self.rest_done, self.part2, self.part3, self.parts_out0, self.parts_out1,
         self.pads, self.vp_in, self.max_prod, self.max_done, self.m_neg, self.m_chain, self.m_in0, self.m_in1,
         self.st, self.exp, self.pv, self.acc_out, self.tb, self.den, self.drained, self.biased) = \
            self.count(c, "attn", w_in=64, wo_in=64, q_in=16 * n * u, k_in=48 * u, prod=NT, rotm=3 * NT if hd == 8 else NT + 1,
            qk_done=NT, v_done=NT, turned=3 * NG, part1=3 * NG, rest_done=3 * NG, part2=3 * NG, part3=3 * NG,
            parts_out0=24 * NG, parts_out1=24 * NG, pads=2 + 5 * SLOTS, vp_in=u, max_prod=len(MAX_STEPS) * u,
            max_done=len(MAX_STEPS) * u, m_neg=10 * u, m_chain=2 * u, m_in0=16 * u, m_in1=16 * u,
            st=len(STEPS) * u, exp=len(STEPS) * u, pv=len(STEPS) * u, acc_out=2 * u, tb=4 * u, den=2 * u,
            drained=2 * u, biased=NT)
        self.parts_out = [self.parts_out0, self.parts_out1]
        self.m_in = [self.m_in0, self.m_in1]

    def all_parts_out(self, eng):
        for s in self.parts_out:
            eng.wait_ge(s.sem, s.at(16 * 3 * NG // 2))

    def first_parts_out(self, eng):
        for s in self.parts_out:
            eng.wait_ge(s.sem, s.at(16 * 3 * NG // 2 // NB))

    def every_unit(self, eng, unit, ahead=1):
        unit(0, 0, left=self.units - 1)
        rounds = (self.units - 1 - ahead) // SLOTS
        with eng.Fori(0, rounds) as k:
            for i in range(1, SLOTS + 1):
                unit(k * SLOTS + i, i % SLOTS, left=ahead)
        for u in range(1 + rounds * SLOTS, self.units):
            unit(u, u % SLOTS, left=self.units - 1 - u)


    def turned_max(self, u, half):
        if half == 1:
            return u * 4 + 2
        return 1 if isinstance(u, int) and u == 0 else u * 4

    def turned_out(self, u, half):
        if half == 0:
            return u * 4 + 3
        return u * 4 + (4 if isinstance(u, int) and u == self.units - 1 else 5)

    def sync(self, sp):
        d, hd = self.dram, self.hd
        for dst, src in ((self.w, d["w"].rearrange("(f p) n -> p f n", p=P)),
                         (self.cos, d["tables"][0].rearrange("(t p) n -> p t n", p=P)),
                         (self.sin, d["tables"][1].rearrange("(t p) n -> p t n", p=P)),
                         (self.bias, d["bias"].partition_broadcast(P))):
            sp.dma_start(dst, src).then_inc(self.w_in.sem, 16)
        for dst, src in ((self.wo, d["wo"].rearrange("(f p) n -> p f n", p=P)),
                         (self.bias_out, d["bias_out"].partition_broadcast(P)),
                         (self.mq, d["mq"]), (self.mk, d["mk"])):
            sp.dma_start(dst, src).then_inc(self.wo_in.sem, 16)
        def load(u, slot):
            for n, (a, b) in enumerate(self.terms):
                src = self.q_dram[a, bass.ds(u * (GQ * hd), GQ * hd), :].rearrange("(h d) t -> d h t", d=hd)
                sp.dma_start(self.qp[slot][hd * n:hd * n + hd, :, :], src).then_inc(self.q_in.sem, 16)
            row = 0
            for a in range(3):
                n = sum(1 for term in self.terms if term[0] == a)
                sp.dma_start(self.kp[slot][row:row + hd * n, :], self.k_dram[0:n, bass.ds(u * hd, hd), :])\
                    .then_inc(self.k_in.sem, 16)
                row += hd * n

        def load_max(u, half, slot):
            sp.wait_ge(self.m_chain.sem, self.m_chain.at(u * 2 + half + 1))
            sp.dma_start(self.qp[slot][KROWS:SROWS, :, 512 * half:512 * half + 512],
                         self.mrows[half][0:3 * GQ, :]).then_inc(self.m_in[half].sem, 16)

        for n in range(3 * NG):
            g, f = divmod(n, 3)
            b, at = divmod(512 * g, SEQ)
            rows = P if f < FT else QK_COLS - D
            if f < FT:
                dst = self.q_dram[:, b * D + P * f:b * D + P * f + P, at:at + 512]
            else:
                dst = self.k_dram[:, b * rows:b * rows + rows, at:at + 512]
            sp.wait_ge(self.part1.sem, self.part1.at(n + 1))
            sp.wait_ge(self.part2.sem, self.part2.at(n + 1))
            sp.wait_ge(self.part3.sem, self.part3.at(n + 1))
            sp.dma_start(dst.rearrange("a f t -> f a t"), self.parts[n % 2][0:rows, :, :]).then_inc(self.parts_out[n % 2].sem, 16)
            if n == 3 * NG - 4:
                self.first_parts_out(sp)
                sp.wait_ge(self.pads.sem, self.pads.at(2 + 5 * 2))
                load(0, 0)
        sp.wait_ge(self.q_in.sem, self.q_in.at(16 * len(self.terms)))
        sp.wait_ge(self.k_in.sem, self.k_in.at(48))
        load(1, 1)
        load_max(0, 0, 0)
        self.all_parts_out(sp)
        sp.wait_ge(self.pads.sem, self.pads.at(2 + 5 * SLOTS))

        def unit(u, slot, left):
            if left > 1:
                sp.wait_ge(self.max_prod.sem, self.max_prod.at((u + 1) * len(MAX_STEPS) + 1))
                load(u + 2, (slot + 2) % SLOTS)
            load_max(u, 1, slot)
            if left:
                load_max(u + 1, 0, (slot + 1) % SLOTS)

        self.every_unit(sp, unit, ahead=2)

    def gpsimd(self, pool):
        c, hd = self.c, self.hd
        self.ln.ready(pool, NG - 1)
        pads = [(parts, 0.0) for parts in self.mparts]
        for slot in range(SLOTS):
            pads += [(self.vp[slot], 0.0), (self.vp[slot][:, :, hd:hd + 1], 1.0),
                     (self.kp[slot][64:KROWS, :], 0.0), (self.kp[slot][KROWS:SROWS, :], 1.0),
                     (self.qp[slot][64:SROWS, :, :], 0.0)]
        for n, (rows, value) in enumerate(pads):
            if n == 12:
                pool.wait_ge(self.prod.sem, self.prod.at(NT))
            if n:
                pool.wait_ge(self.pads.sem, self.pads.at(n))
            pool.memset(rows, value).then_inc(self.pads.sem, 1)
        pool.wait_ge(self.pads.sem, self.pads.at(len(pads)))
        pool.wait_ge(self.wo_in.sem, self.wo_in.at(64))
        for t in range(NT):
            self.ln.normed(pool, t)
            pool.tensor_tensor(c.x[:, t, :], c.x[:, t, :], self.bias_out, ALU.add).then_inc(self.biased.sem, 1)
        v_flat = self.v.rearrange("p u b d -> p (u b d)")

        def copy_v(u, slot):
            pool.tensor_copy(self.vp[slot][:, :, 0:hd],
                             v_flat[:, bass.ds(u * (BT * hd), BT * hd)].rearrange("p (b d) -> p b d", d=hd))\
                .then_inc(self.vp_in.sem, 1)

        def unit(u, slot, left):
            if left:
                if not (isinstance(u, int) and u == 0):
                    pool.wait_ge(self.pv.sem, self.pv.at(u * len(STEPS)))
                copy_v(u + 1, (slot + 1) % SLOTS)

        pool.wait_ge(self.v_done.sem, self.v_done.at(NT))
        pool.wait_ge(self.pads.sem, self.pads.at(2 + 5 * SLOTS))
        copy_v(0, 0)
        self.every_unit(pool, unit)

    def vector(self, dve):
        c, hd = self.c, self.hd
        heads = QK_COLS // hd
        by_head = lambda z: z.rearrange("p (n d) -> p n d", d=hd)
        dve.wait_ge(self.w_in.sem, self.w_in.at(64))
        if hd != 8:
            dve.tensor_tensor(self.cos, self.cos, self.sin, ALU.add).then_inc(self.rotm.sem, 1)

        def rotate(t):
            bt = t % BT
            z = by_head(c.bank[t % 4][:, 0:QK_COLS])
            zv = by_head(c.bank[t % 4][:, QK_COLS:3 * P])
            a, b, out = self.rot[t % 2], self.rotb[t % 2], by_head(self.qk[t % 4])
            aa, bb = by_head(a), by_head(b)
            cos = over(self.cos[:, bt, :], 1, heads)
            v = self.v[:, (t // BT) * self.nkv:(t // BT + 1) * self.nkv, bt, :]
            dve.wait_ge(self.prod.sem, self.prod.at(t + 1))
            if t >= 4:
                dve.wait_ge(self.turned.sem, self.turned.at(3 * (t // 4)))
            if t >= 2:
                dve.wait_ge(self.qk_done.sem, self.qk_done.at(t - 1))
            if hd == 8:
                h = hd // 2
                dve.tensor_tensor(aa, z, cos, ALU.mult).then_inc(self.rotm.sem, 1)
                dve.tensor_tensor(bb[:, :, 0:h], z[:, :, h:hd], over(self.sin[:, bt, 0:h], 1, heads),
                                  ALU.mult).then_inc(self.rotm.sem, 1)
                dve.tensor_tensor(bb[:, :, h:hd], z[:, :, 0:h], over(self.sin[:, bt, h:hd], 1, heads),
                                  ALU.mult).then_inc(self.rotm.sem, 1)
                dve.tensor_copy(v, zv).then_inc(self.v_done.sem, 1)
                dve.wait_ge(self.rotm.sem, self.rotm.at(3 * t + 3))
                dve.tensor_tensor(out, aa, bb, ALU.add).then_inc(self.qk_done.sem, 1)
            else:
                dve.tensor_tensor(aa, z, by_head(self.bias[:, 0:QK_COLS]), ALU.add).then_inc(self.rotm.sem, 1)
                dve.tensor_tensor(v, zv, by_head(self.bias[:, QK_COLS:3 * P]), ALU.add).then_inc(self.v_done.sem, 1)
                dve.wait_ge(self.rotm.sem, self.rotm.at(t + 2))
                dve.tensor_tensor(out, aa, cos, ALU.mult).then_inc(self.qk_done.sem, 1)

        def cut(n):
            rows = P if n % 3 < FT else QK_COLS - D
            z, parts, rest = c.bank[4 + n % 4][0:rows, :], self.parts[n % 2][0:rows], self.rest[n % 2][0:rows]
            dve.wait_ge(self.part1.sem, self.part1.at(n + 1))
            if n >= 2:
                dve.wait_ge(self.part3.sem, self.part3.at(n - 1))
            dve.tensor_tensor(rest, z, parts[:, 0, :], ALU.subtract).then_inc(self.rest_done.sem, 1)
            dve.wait_ge(self.part2.sem, self.part2.at(n + 1))
            dve.tensor_tensor(parts[:, 2, :], rest, parts[:, 1, :], ALU.subtract).then_inc(self.part3.sem, 1)

        for g in range(NG + 1):
            if g < NG:
                for t in range(4 * g, 4 * g + 4):
                    rotate(t)
            if g:
                for f in range(3):
                    cut(3 * (g - 1) + f)
        self.all_parts_out(dve)

        def maxima(u, k0, k1):
            for k in range(k0, k1):
                half, i, h = MAX_STEPS[k]
                n = (i + 1) * P
                both = c.psum[:, 2 * (k % 2):2 * (k % 2) + 2, :]
                if half == 0:
                    src, dst = both[:, :, 0:n], self.mx[0][:, i, h:h + 2]
                else:
                    src, dst = both.rearrange("p a b -> p (a b)")[:, 0:n], self.mx[1][:, i - 4, h:h + 1]
                dve.wait_ge(self.max_prod.sem, self.max_prod.at(u * len(MAX_STEPS) + k + 1))
                dve.tensor_reduce(dst, src, AX_X, ALU.max).then_inc(self.max_done.sem, 1)

        def split_max(u, half):
            neg, rest = self.mneg[half], self.mrest[half]
            part = [self.mparts[half][:, :, GQ * i:GQ * i + GQ] for i in range(3)]
            done = u * 10 + 5 * half
            dve.wait_ge(self.max_done.sem, self.max_done.at(u * len(MAX_STEPS) + (8 if half == 0 else len(MAX_STEPS))))
            dve.tensor_scalar(neg, self.mx[half], -1.0, None, ALU.mult).then_inc(self.m_neg.sem, 1)
            dve.wait_ge(self.m_neg.sem, self.m_neg.at(done + 1))
            dve.tensor_copy(part[0], neg).then_inc(self.m_neg.sem, 1)
            dve.wait_ge(self.m_neg.sem, self.m_neg.at(done + 2))
            dve.tensor_tensor(rest, neg, part[0], ALU.subtract).then_inc(self.m_neg.sem, 1)
            dve.wait_ge(self.m_neg.sem, self.m_neg.at(done + 3))
            dve.tensor_copy(part[1], rest).then_inc(self.m_neg.sem, 1)
            dve.wait_ge(self.m_neg.sem, self.m_neg.at(done + 4))
            dve.tensor_tensor(part[2], rest, part[1], ALU.subtract).then_inc(self.m_neg.sem, 1)

        def rows_out(u, half):
            dve.wait_ge(self.tb.sem, self.tb.at(self.turned_max(u, half)))
            if not (isinstance(u, int) and u == 0):
                dve.wait_ge(self.m_in[half].sem, self.m_in[half].at(u * 16))
            dve.tensor_copy(self.mrows[half][0:3 * GQ, :],
                            c.bank[TURN_BANK][0:3 * GQ, 0:256].bitcast(BF16)).then_inc(self.m_chain.sem, 1)

        def normalize(u, half):
            z = c.bank[TURN_BANK].rearrange("p (i h e) -> p i h e", i=4, e=32)
            at = u * (GQ * hd) + (u // self.nkv) * (BT * D - D) + 4 * half * D
            dst = c.cx_pad[:, bass.ds(at, 4 * D)].rearrange("p (i n) -> p i n", i=4)[:, :, 0:GQ * hd]
            dve.wait_ge(self.tb.sem, self.tb.at(self.turned_out(u, half)))
            dve.reciprocal(self.rden, z[:, :, :, hd]).then_inc(self.den.sem, 1)
            dve.wait_ge(self.den.sem, self.den.at(u * 2 + half + 1))
            dve.tensor_tensor(dst.rearrange("p i (h d) -> p i h d", d=hd), z[:, :, :, 0:hd],
                              over(self.rden, 3, hd), ALU.mult).then_inc(self.drained.sem, 1)

        def unit(u, slot, left):
            if left:
                maxima(u + 1, 0, 2)
            if not (isinstance(u, int) and u == 0):
                normalize(u - 1, 1)
            rows_out(u, 1)
            if left:
                maxima(u + 1, 2, 8)
                split_max(u + 1, 0)
                maxima(u + 1, 8, 10)
            normalize(u, 0)
            if left:
                maxima(u + 1, 10, 11)
                rows_out(u + 1, 0)
                maxima(u + 1, 11, len(MAX_STEPS))
                split_max(u + 1, 1)

        maxima(0, 0, 8)
        split_max(0, 0)
        rows_out(0, 0)
        maxima(0, 8, len(MAX_STEPS))
        split_max(0, 1)
        self.every_unit(dve, unit)
        normalize(self.units - 1, 1)
        dve.wait_ge(self.biased.sem, self.biased.at(NT))

    def scalar(self, act):
        c = self.c
        for n in range(3 * NG):
            rows = P if n % 3 < FT else QK_COLS - D
            parts, rest = self.parts[n % 2][0:rows], self.rest[n % 2][0:rows]
            act.wait_ge(self.turned.sem, self.turned.at(n + 1))
            if n >= 2:
                act.wait_ge(self.parts_out[n % 2].sem, self.parts_out[n % 2].at(16 * (n // 2)))
            act.activation(parts[:, 0, :], c.bank[4 + n % 4][0:rows, :], ACT.Copy).then_inc(self.part1.sem, 1)
            act.wait_ge(self.rest_done.sem, self.rest_done.at(n + 1))
            act.activation(parts[:, 1, :], rest, ACT.Copy).then_inc(self.part2.sem, 1)
        act.wait_ge(self.pads.sem, self.pads.at(2 + 5 * SLOTS))

        def unit(u, slot, left):
            first = isinstance(u, int) and u == 0
            for s in range(len(STEPS)):
                act.wait_ge(self.st.sem, self.st.at(u * len(STEPS) + s + 1))
                if not (first and s < 3):
                    act.wait_ge(self.pv.sem, self.pv.at(u * len(STEPS) + (s - 2)))
                act.activation(self.p[s % 3].rearrange("p h t -> p (h t)"), c.bank[ST_BANK + s % 2][:, :], ACT.Exp,
                               scale=self.scale).then_inc(self.exp.sem, 1)
                for half, after, steps in ((0, 11, 10), (1, 35, 36)):
                    if s == after:
                        act.wait_ge(self.pv.sem, self.pv.at(u * len(STEPS) + steps))
                        if not (first and half == 0):
                            act.wait_ge(self.tb.sem, self.tb.at(self.turned_out(u, 0) if half else self.turned_out(u - 1, 1)))
                        act.activation(self.acc, c.bank[ACC_BANK][:, :], ACT.Copy).then_inc(self.acc_out.sem, 1)

        self.every_unit(act, unit)

    def tensor(self, pe):
        c, hd = self.c, self.hd
        pe.wait_ge(self.w_in.sem, self.w_in.at(64))

        def turn(g):
            pe.wait_ge(self.qk_done.sem, self.qk_done.at(4 * g + 4))
            self.ln.ready(pe, NG - 1)
            for f in range(3):
                n = 3 * g + f
                rows = P if f < FT else QK_COLS - D
                if n >= 4:
                    pe.wait_ge(self.rest_done.sem, self.rest_done.at(n - 3))
                for q in range(4):
                    mm = pe.transpose(c.bank[4 + n % 4][0:rows, P * q:P * q + P],
                                      self.qk[q][:, P * f:P * f + rows], c.identf[:, :])
                mm.then_inc(self.turned.sem, 1)

        for g in range(NG):
            self.ln.ready(pe, g)
            for t in range(4 * g, 4 * g + 4):
                if t >= 4:
                    pe.wait_ge(self.rotm.sem, self.rotm.at(3 * (t - 3) if hd == 8 else t - 2))
                    pe.wait_ge(self.v_done.sem, self.v_done.at(t - 3))
                for f in range(FT):
                    mm = pe.matmul(c.bank[t % 4][:, 0:3 * P], c.yt[:, f, P * t:P * t + P], self.w[:, f, :],
                                   start=(f == 0), stop=(f == FT - 1))
                mm.then_inc(self.prod.sem, 1)
            if g:
                turn(g - 1)
        turn(NG - 1)

        pe.wait_ge(self.rest_done.sem, self.rest_done.at(3 * NG))
        pe.wait_ge(self.v_done.sem, self.v_done.at(NT))
        pe.wait_ge(self.rotm.sem, self.rotm.at(3 * NT if hd == 8 else NT + 1))
        pe.wait_ge(self.wo_in.sem, self.wo_in.at(64))

        def max_scores(u, k, slot):
            half, i, h = MAX_STEPS[k]
            qp, kp = self.qp[slot], self.kp[slot]
            if k == 0:
                pe.wait_ge(self.q_in.sem, self.q_in.at((u + 1) * (16 * len(self.terms))))
                pe.wait_ge(self.k_in.sem, self.k_in.at((u + 1) * 48))
            if not (isinstance(u, int) and u == 0 and k < 2):
                pe.wait_ge(self.max_done.sem, self.max_done.at(u * len(MAX_STEPS) + (k - 1)))
            for b in range(2):
                bank = c.bank[2 * (k % 2) + b]
                head = h + b if half == 0 else h
                q = qp[0:KROWS, head, P * i:P * i + P]
                lo = 512 * b * half
                n = min(512, (i + 1) * P - lo)
                diag = half == 0 or b == 1
                mm = pe.matmul(bank[:, 0:n], q, kp[0:KROWS, lo:lo + n], start=True, stop=not diag,
                               skip_group_check=True)
                if diag:
                    mm = pe.matmul(bank[:, n - P:n], c.identb[:, :], self.mq, start=False, stop=True,
                                   skip_group_check=True)
            mm.then_inc(self.max_prod.sem, 1)

        def turn_max(u, half):
            pe.wait_ge(self.m_neg.sem, self.m_neg.at(u * 10 + (5 * half + 5)))
            if isinstance(u, int) and u == 0:
                if half == 1:
                    pe.wait_ge(self.m_chain.sem, self.m_chain.at(1))
            else:
                pe.wait_ge(self.drained.sem, self.drained.at(u * 2 if half else u * 2 - 1))
            for i in range(4):
                mm = pe.transpose(c.bank[TURN_BANK].bitcast(BF16)[:, P * i:P * i + P], self.mparts[half][:, i, :],
                                  c.identb[:, :])
            mm.then_inc(self.tb.sem, 1)

        def turn_out(u, half):
            pe.wait_ge(self.acc_out.sem, self.acc_out.at(u * 2 + half + 1))
            if half == 1 and isinstance(u, int) and u == self.units - 1:
                pe.wait_ge(self.drained.sem, self.drained.at(u * 2 + 1))
            else:
                pe.wait_ge(self.m_chain.sem, self.m_chain.at(u * 2 + half + 2))
            for i in range(4):
                mm = pe.transpose(c.bank[TURN_BANK][:, P * i:P * i + P], self.acc[:, P * i:P * i + P],
                                  c.identf[:, :])
            mm.then_inc(self.tb.sem, 1)

        def scores(u, s, slot, first):
            i, j = STEPS[s]
            if s == 0 or s == 10:
                rows_in = self.m_in[0 if s == 0 else 1]
                pe.wait_ge(rows_in.sem, rows_in.at((u + 1) * 16))
            if not (first and s < 2):
                pe.wait_ge(self.exp.sem, self.exp.at(u * len(STEPS) + (s - 1)))
            bank = c.bank[ST_BANK + s % 2]
            mm = pe.matmul(bank[:, :], self.kp[slot][0:SROWS, P * j:P * j + P],
                           self.qp[slot][0:SROWS, :, P * i:P * i + P],
                           start=True, stop=(j < i))
            if i == j:
                mm = pe.matmul(bank[:, :], c.identb[:, :], over(self.mk, 1, GQ), start=False, stop=True)
            mm.then_inc(self.st.sem, 1)

        def values(u, s, slot, first):
            i, j = STEPS[s]
            if s == 0:
                pe.wait_ge(self.vp_in.sem, self.vp_in.at(u + 1))
            if s == 10 or (s == 0 and not first):
                pe.wait_ge(self.acc_out.sem, self.acc_out.at(u * 2 + (1 if s else 0)))
            pe.wait_ge(self.exp.sem, self.exp.at(u * len(STEPS) + (s + 1)))
            for h in range(GQ):
                mm = pe.matmul(c.bank[ACC_BANK][32 * h:32 * h + 32, P * (i % 4):P * (i % 4) + P],
                               self.vp[slot][:, j, :], self.p[s % 3][:, h, :], start=(j == 0), stop=(j == i))
            mm.then_inc(self.pv.sem, 1)

        def unit(u, slot, left):
            first = isinstance(u, int) and u == 0
            for s in range(len(STEPS) + 2):
                if s < len(STEPS):
                    scores(u, s, slot, first)
                if s == 2 and not first:
                    turn_out(u - 1, 1)
                if s == 3:
                    turn_max(u, 1)
                if s == 14:
                    turn_out(u, 0)
                if s == 16 and left:
                    turn_max(u + 1, 0)
                if left and s < len(STEPS) and s % 3 < 2:
                    max_scores(u + 1, s - s // 3, (slot + 1) % SLOTS)
                if s >= 2:
                    values(u, s - 2, slot, first)

        for k in range(8):
            max_scores(0, k, 0)
        turn_max(0, 0)
        for k in range(8, len(MAX_STEPS)):
            max_scores(0, k, 0)
        self.every_unit(pe, unit)
        turn_out(self.units - 1, 1)

    def source(self, t, f):
        return self.c.cx[:, D * t + P * f:D * t + P * f + P]

    def finished(self, pe, g):
        if g == 0:
            pe.wait_ge(self.drained.sem, self.drained.at(2 * self.units))


class Routing(Stage):

    def __init__(self, c, kind, ln, experts, top, w, bias, const, carve, **more):
        self.c, self.ln, self.e, self.top, self.dram_w, self.dram_b = c, ln, experts, top, w, bias
        self.tiles = top * NT + experts - 1
        self.const = const
        assert experts * (NT + 1) <= 512 and self.tiles <= L1_TILES
        r, e = carve, experts
        self.w = r.take([FT, e])
        self.b = r.take([e])
        self.order = r.take([e])
        t = lambda: r.take([NT, e])
        self.z, self.pr, self.left, self.eq, self.place = t(), t(), t(), t(), t()
        self.hit = [t() for _ in range(top)]
        self.weight = [r.take([NT]) for _ in range(top)]
        self.s = r.take([NT])
        self.rs = r.take([NT])
        self.hitb = r.take([NT, e], BF16)
        self.lower = r.take([P], BF16)
        self.ones = r.take([P], BF16)
        self.edges = r.take([NT])
        self.numbers = r.take([self.tiles])
        self.over_edge = r.take([e, NT])
        self.shares = r.take([e])
        self.starts = r.take([e])
        self.start_rows = r.take([e])
        self.placef = r.take([NT])
        self.placei = [r.take([NT]).bitcast(U32) for _ in range(top)]
        self.past = r.take([self.tiles, e - 1])
        self.ownerf = r.take([self.tiles])
        self.owner = r.take([self.tiles]).bitcast(U32)
        self.steps = 0
        all_steps = 5 + 6 * top - 1 + (top - 1) + 7 + (e - 1) + 2 * top
        (self.w_in, self.const_in, self.prod, self.step, self.shifted, self.exp, self.orders, self.hits, self.before,
         self.places, self.owners, self.scattered, *self.more) = self.count(
            c, kind, w_in=16 * (1 + (bias is not None)), const_in=64, prod=1, step=all_steps, shifted=1, exp=1,
            orders=e, hits=1, before=1, places=top, owners=1, scattered=16 * top * NT, **more)

    def sync(self, sp):
        sp.dma_start(self.w, self.dram_w.rearrange("(f p) e -> p f e", p=P)).then_inc(self.w_in.sem, 16)
        if self.dram_b is not None:
            sp.dma_start(self.b, self.dram_b.partition_broadcast(P)).then_inc(self.w_in.sem, 16)
        q = self.const
        for dst, src in ((self.lower, q["lower"]), (self.ones, q["ones"]),
                         (self.edges, q["edges"].partition_broadcast(P)),
                         (self.numbers, q["numbers"][0:self.tiles].partition_broadcast(P))):
            sp.dma_start(dst, src).then_inc(self.const_in.sem, 16)

    def w_loaded(self, eng):
        eng.wait_ge(self.w_in.sem, self.w_in.at(32 if self.dram_b is not None else 16))

    def gpsimd(self, pool):
        for e in range(self.e):
            pool.memset(self.order[:, e:e + 1], float(self.e - e)).then_inc(self.orders.sem, 1)

    def tensor(self, pe):
        c, e = self.c, self.e
        self.w_loaded(pe)
        for g in range(NG):
            self.ln.ready(pe, g)
            for t in range(4 * g, 4 * g + 4):
                for f in range(FT):
                    mm = pe.matmul(c.bank[2][:, e * t:e * t + e], c.yt[:, f, P * t:P * t + P], self.w[:, f, :],
                                   start=(f == 0), stop=(f == FT - 1))
        mm.then_inc(self.prod.sem, 1)

    def scalar(self, act):
        act.wait_ge(self.shifted.sem, self.shifted.at(1))
        act.activation(self.pr, self.z, ACT.Exp).then_inc(self.exp.sem, 1)

    def then(self, dve, ins):
        self.steps += 1
        ins.then_inc(self.step.sem, 1)
        dve.wait_ge(self.step.sem, self.step.at(self.steps))

    def choose(self, dve):
        c, e = self.c, self.e
        wide = lambda v: over(v, 2, e)
        by_token = lambda v: over(v, 1, NT)
        logits = c.bank[2][:, 0:NT * e].rearrange("p (t e) -> p t e", e=e)
        dve.wait_ge(self.prod.sem, self.prod.at(1))
        self.w_loaded(dve)
        if self.dram_b is not None:
            self.then(dve, dve.tensor_tensor(self.z, logits, by_token(self.b), ALU.add))
        else:
            self.then(dve, dve.tensor_copy(self.z, logits))
        self.then(dve, dve.tensor_reduce(self.s, self.z, AX_X, ALU.max))
        dve.tensor_tensor(self.z, self.z, wide(self.s), ALU.subtract).then_inc(self.shifted.sem, 1)
        dve.wait_ge(self.exp.sem, self.exp.at(1))
        self.then(dve, dve.tensor_reduce(self.s, self.pr, AX_X, ALU.add))
        self.then(dve, dve.reciprocal(self.rs, self.s))
        self.then(dve, dve.tensor_tensor(self.pr, self.pr, wide(self.rs), ALU.mult))
        dve.wait_ge(self.orders.sem, self.orders.at(e))
        left = self.pr
        for k in range(self.top):
            hit, weight = self.hit[k], self.weight[k]
            self.then(dve, dve.tensor_reduce(weight, left, AX_X, ALU.max))
            self.then(dve, dve.tensor_tensor(self.eq, left, wide(weight), ALU.is_equal))
            self.then(dve, dve.tensor_tensor(self.eq, self.eq, by_token(self.order), ALU.mult))
            self.then(dve, dve.tensor_reduce(self.s, self.eq, AX_X, ALU.max))
            self.then(dve, dve.tensor_tensor(hit, self.eq, wide(self.s), ALU.is_equal))
            if k + 1 < self.top:
                flat = lambda v: v.rearrange("p t e -> p (t e)")
                self.then(dve, dve.scalar_tensor_tensor(out=flat(self.left), in0=flat(hit), scalar=-2.0,
                                                        in1=flat(self.pr), op0=ALU.mult, op1=ALU.add))
                left = self.left
        if self.top == 2:
            self.then(dve, dve.tensor_tensor(self.eq, self.hit[0], self.hit[1], ALU.add))
        assert self.top <= 2
        dve.tensor_copy(self.hitb, self.eq if self.top == 2 else self.hit[0]).then_inc(self.hits.sem, 1)

    def count_before(self, pe):
        e, before = self.e, self.c.bank[3]
        pe.wait_ge(self.const_in.sem, self.const_in.at(64))
        pe.wait_ge(self.hits.sem, self.hits.at(1))
        pe.matmul(before[:, 0:NT * e], self.lower, self.hitb.rearrange("p t e -> p (t e)"), start=True, stop=False,
                  skip_group_check=True)
        pe.matmul(before[:, NT * e:NT * e + e], self.ones, self.hitb[:, NT - 1, :], start=False, stop=False,
                  skip_group_check=True)
        for t in range(NT - 1):
            mm = pe.matmul(before[:, e * (t + 1):e * (NT + 1)], self.ones, over(self.hitb[:, t, :], 1, NT - t),
                           start=False, stop=(t == NT - 2), skip_group_check=True)
        mm.then_inc(self.before.sem, 1)

    def find_places(self, dve):
        e = self.e
        then = self.then
        before = self.c.bank[3][:, 0:e * (NT + 1)].rearrange("p (t e) -> p t e", e=e)
        dve.wait_ge(self.const_in.sem, self.const_in.at(64))
        dve.wait_ge(self.before.sem, self.before.at(1))
        then(dve, dve.tensor_tensor(self.over_edge, over(before[:, NT, :], 2, NT), over(self.edges, 1, e), ALU.is_gt))
        then(dve, dve.tensor_reduce(self.shares, self.over_edge, AX_X, ALU.add))
        then(dve, dve.memset(self.starts, 0.0))
        for k in range(1, e):
            then(dve, dve.tensor_tensor(self.starts[:, k:k + 1], self.starts[:, k - 1:k], self.shares[:, k - 1:k],
                                        ALU.add))
        then(dve, dve.tensor_scalar(self.start_rows, self.starts, float(P), None, ALU.mult))
        then(dve, dve.tensor_tensor(self.place, before[:, 0:NT, :], over(self.start_rows, 1, NT), ALU.add))
        for k in range(self.top):
            then(dve, dve.tensor_tensor(self.eq, self.place, self.hit[k], ALU.mult))
            then(dve, dve.tensor_reduce(self.placef, self.eq, AX_X, ALU.add))
            dve.tensor_copy(self.placei[k], self.placef).then_inc(self.places.sem, 1)
            if k + 1 < self.top:
                dve.wait_ge(self.places.sem, self.places.at(k + 1))
        then(dve, dve.tensor_tensor(self.past, over(self.numbers, 2, e - 1), over(self.starts[:, 1:e], 1, self.tiles),
                                    ALU.is_ge))
        then(dve, dve.tensor_reduce(self.ownerf, self.past, AX_X, ALU.add))
        dve.tensor_copy(self.owner, self.ownerf).then_inc(self.owners.sem, 1)

    def scatter(self, pool):
        c = self.c
        pool.wait_ge(self.places.sem, self.places.at(self.top))
        pool.wait_ge(c.zeros_out, 16)
        for t in range(NT):
            self.ln.normed(pool, t)
            for k in range(self.top):
                pool.indirect_dma_start(c.sorted[:, :],
                                        bass.IndirectOffsetOnAxis(ap=self.placei[k][:, t:t + 1], axis=0),
                                        c.yn[:, t, :], None).then_inc(self.scattered.sem, 16)

    def all_scattered(self, eng):
        eng.wait_ge(self.scattered.sem, self.scattered.at(16 * self.top * NT))

    def gather(self, pool, into, gathered):
        for t in range(NT):
            for k in range(self.top):
                pool.indirect_dma_start(into[k][:, t, :], None, self.c.results[0:self.tiles * P, :],
                                        bass.IndirectOffsetOnAxis(ap=self.placei[k][:, t:t + 1], axis=0))\
                    .then_inc(gathered[t // 4].sem, 16)

    def tile_owner(self, pe, k):
        return pe.value_load(self.owner[0:1, bass.ds(k, 1)], min_val=0, max_val=self.e - 1)


class Routed(Routing):

    def __init__(self, c, ln, experts, weights, w, bias, const, carve):
        tiles = NT + experts - 1
        super().__init__(
            c, "routed", ln, experts, 1, w, bias, const, carve, y_in=16 * tiles, y_turned=tiles, y_set=tiles,
            gprod=2 * tiles, uprod=2 * tiles, silu=2 * tiles, h_done=2 * tiles, h_turned=2 * tiles, ht0=tiles,
            ht1=tiles, down=tiles, o_set=tiles, o_out=16 * tiles, gathered0=64, gathered1=64, gathered2=64,
            gathered3=64, added=NT)
        (self.y_in, self.y_turned, self.y_set, self.gprod, self.uprod, self.silu, self.h_done, self.h_turned,
         self.ht0, self.ht1, self.down, self.o_set, self.o_out, *gathered, self.added) = self.more
        self.gathered = gathered
        self.weights, self.hidden = weights, weights.hidden // experts
        self.wg, self.wu = weights.wg, weights.wu
        self.wd = weights.wd.rearrange("p j d -> p (j d)")
        assert self.hidden == 1024
        r = carve
        self.y = r.take([D])
        self.yt = r.take([FT, P])
        self.g = r.take([self.hidden])
        self.h = r.take([self.hidden])
        self.ht = r.take([self.hidden // P, P])
        self.o = r.take([D])


    def every_tile(self, eng, step):
        step(0, True, False)
        with eng.Fori(1, self.tiles - 1) as k:
            step(k, False, False)
        step(self.tiles - 1, False, True)

    def sync(self, sp):
        super().sync(sp)
        c = self.c
        self.all_scattered(sp)

        def load(k):
            sp.dma_start(self.y, c.sorted[bass.ds(k * P, P), :]).then_inc(self.y_in.sem, 16)

        def store(k):
            sp.wait_ge(self.o_set.sem, self.o_set.at(k + 1))
            sp.dma_start(c.results[bass.ds(k * P, P), :], self.o).then_inc(self.o_out.sem, 16)

        def step(k, first, last):
            if not last:
                sp.wait_ge(self.y_turned.sem, self.y_turned.at(k + 1))
                load(k + 1)
            if not first:
                store(k - 1)

        load(0)
        self.every_tile(sp, step)
        store(self.tiles - 1)

    def gpsimd(self, pool):
        super().gpsimd(pool)
        self.scatter(pool)
        pool.wait_ge(self.o_out.sem, self.o_out.at(16 * self.tiles))
        self.gather(pool, [self.c.yn], self.gathered)

    def tensor(self, pe):
        super().tensor(pe)
        c = self.c
        self.count_before(pe)
        self.weights.wait(pe)
        pe.wait_ge(self.owners.sem, self.owners.at(1))

        def turn_y(k):
            pe.wait_ge(self.y_in.sem, self.y_in.at(16 * (k + 1)))
            for f in range(FT):
                mm = pe.transpose(c.bank[6][:, P * f:P * f + P], self.y[:, P * f:P * f + P], c.identf[:, :])
            mm.then_inc(self.y_turned.sem, 1)

        def up(k):
            own = self.tile_owner(pe, k)
            pe.wait_ge(self.y_set.sem, self.y_set.at(k + 1))
            for half in range(2):
                for w, bank, done in ((self.wg, c.bank[half], self.gprod), (self.wu, c.bank[2 + half], self.uprod)):
                    for f in range(FT):
                        mm = pe.matmul(bank[:, :], self.yt[:, f, :],
                                       w[:, f, bass.ds(own * self.hidden + 512 * half, 512)],
                                       start=(f == 0), stop=(f == FT - 1))
                    mm.then_inc(done.sem, 1)

        def turn_h(k):
            for half in range(2):
                pe.wait_ge(self.h_done.sem, self.h_done.at(2 * k + half + 1))
                for q in range(4):
                    at = 512 * half + P * q
                    mm = pe.transpose(c.bank[4 + half][:, P * q:P * q + P], self.h[:, at:at + P], c.identf[:, :])
                mm.then_inc(self.h_turned.sem, 1)

        def down(k, first):
            own = self.tile_owner(pe, k)
            pe.wait_ge(self.ht0.sem, self.ht0.at(k + 1))
            pe.wait_ge(self.ht1.sem, self.ht1.at(k + 1))
            if not first:
                pe.wait_ge(self.o_set.sem, self.o_set.at(k))
            last = self.hidden // P - 1
            for j in range(last + 1):
                mm = pe.matmul(c.bank[7][:, 0:D], self.ht[:, j, :], self.wd[:, bass.ds((own * (last + 1) + j) * D, D)],
                               start=(j == 0), stop=(j == last))
            mm.then_inc(self.down.sem, 1)

        def step(k, first, last):
            up(k)
            if not last:
                turn_y(k + 1)
            if not first:
                down(k - 1, isinstance(k, int) and k == 1)
            turn_h(k)

        turn_y(0)
        step(0, True, False)
        step(1, False, False)
        with pe.Fori(2, self.tiles - 1) as k:
            step(k, False, False)
        step(self.tiles - 1, False, True)
        down(self.tiles - 1, False)

    def scalar(self, act):
        super().scalar(act)
        c = self.c

        def out(k, first):
            act.wait_ge(self.down.sem, self.down.at(k + 1))
            if not first:
                act.wait_ge(self.o_out.sem, self.o_out.at(16 * k))
            act.activation(self.o, c.bank[7][:, 0:D], ACT.Copy).then_inc(self.o_set.sem, 1)

        def step(k, first, last):
            for half in range(2):
                act.wait_ge(self.gprod.sem, self.gprod.at(2 * k + half + 1))
                act.activation(self.g[:, 512 * half:512 * half + 512], c.bank[half][:, :], ACT.Silu)\
                    .then_inc(self.silu.sem, 1)
            if not first:
                out(k - 1, isinstance(k, int) and k == 1)
            act.wait_ge(self.h_turned.sem, self.h_turned.at(2 * k + 1))
            act.activation(self.ht[:, 0:4, :].rearrange("p j t -> p (j t)"), c.bank[4][:, :], ACT.Copy)\
                .then_inc(self.ht0.sem, 1)

        step(0, True, False)
        step(1, False, False)
        with act.Fori(2, self.tiles - 1) as k:
            step(k, False, False)
        step(self.tiles - 1, False, True)
        out(self.tiles - 1, False)

    def vector(self, dve):
        c = self.c
        self.choose(dve)
        self.find_places(dve)

        def set_y(k):
            dve.wait_ge(self.y_turned.sem, self.y_turned.at(k + 1))
            dve.tensor_copy(self.yt.rearrange("p f t -> p (f t)"), c.bank[6][:, 0:D]).then_inc(self.y_set.sem, 1)

        def step(k, first, last):
            for half in range(2):
                at = slice(512 * half, 512 * half + 512)
                dve.wait_ge(self.uprod.sem, self.uprod.at(2 * k + half + 1))
                dve.wait_ge(self.silu.sem, self.silu.at(2 * k + half + 1))
                dve.tensor_tensor(self.h[:, at], c.bank[2 + half][:, :], self.g[:, at], ALU.mult)\
                    .then_inc(self.h_done.sem, 1)
            if not last:
                set_y(k + 1)
            dve.wait_ge(self.h_turned.sem, self.h_turned.at(2 * k + 2))
            dve.tensor_copy(self.ht[:, 4:8, :].rearrange("p j t -> p (j t)"), c.bank[5][:, :])\
                .then_inc(self.ht1.sem, 1)

        set_y(0)
        self.every_tile(dve, step)
        for t in range(NT):
            if t % 4 == 0:
                dve.wait_ge(self.gathered[t // 4].sem, self.gathered[t // 4].at(64))
            dve.scalar_tensor_tensor(out=c.x[:, t, :], in0=c.yn[:, t, :], scalar=self.weight[0][:, t:t + 1],
                                     in1=c.x[:, t, :], op0=ALU.mult, op1=ALU.add).then_inc(self.added.sem, 1)
        dve.wait_ge(self.added.sem, self.added.at(NT))


class TopTwo(Routing):

    def __init__(self, c, ln, experts, weights, w, const, carve):
        tiles = 2 * NT + experts - 1
        assert tiles % RING == 0
        n = weights.shared_tiles * NG
        per_slot = 16 * (tiles // RING)
        super().__init__(
            c, "top_two", ln, experts, 2, w, None, const, carve, y_in0=per_slot, y_in1=per_slot, y_in2=per_slot,
            y_turned=tiles, y_set=tiles, gu=tiles, silu=tiles, h_clear=RING, h_done=tiles, h_turned=tiles,
            ht_set=tiles, down=tiles, o_set=tiles, o_out0=per_slot, o_out1=per_slot, o_out2=per_slot, gathered0=128,
            gathered1=128, gathered2=128, gathered3=128, added1=NT, added=NT, s_prod=n, s_silu=n, s_mul=n, s_down=n,
            s_added=2 * NG)
        (y_in0, y_in1, y_in2, self.y_turned, self.y_set, self.gu, self.silu, self.h_clear, self.h_done,
         self.h_turned, self.ht_set, self.down, self.o_set, o_out0, o_out1, o_out2, g0, g1, g2, g3, self.added1,
         self.added, self.s_prod, self.s_silu, self.s_mul, self.s_down, self.s_added) = self.more
        self.y_in, self.o_out, self.gathered = [y_in0, y_in1, y_in2], [o_out0, o_out1, o_out2], [g0, g1, g2, g3]
        self.weights, self.hidden = weights, weights.hidden
        r = carve
        take = lambda free: [r.take(free) for _ in range(RING)]
        self.y, self.yt, self.g, self.h = take([D]), take([FT, P]), take([self.hidden]), take([2 * P])
        self.ht, self.o = take([2, P]), take([D])
        self.sg = [r.take([512]) for _ in range(2)]
        self.sh = [r.take([512]) for _ in range(3)]
        self.back = [c.yn, Carve(c.region["w"], weights.end).take([NT, D])]
        self.gu_bank = [c.bank[i] for i in range(RING)]
        self.y_bank = [c.bank[i][:, 0:D] for i in (3, 6, 7)]
        self.ht_bank, self.o_bank = c.bank[4][:, 0:D], c.bank[5][:, 0:D]


    def every_tile(self, eng, step):
        rounds = self.tiles // RING
        for j in range(RING):
            step(0, j, j, self.tiles - 1 - j)
        with eng.Fori(1, rounds - 1) as i:
            for j in range(RING):
                step(i, j, i * RING + j, RING)
        for j in range(RING):
            step(rounds - 1, j, (rounds - 1) * RING + j, RING - 1 - j)

    def later(self, i, j, n):
        return i + (j + n) // RING, (j + n) % RING, i * RING + (j + n)

    def sync(self, sp):
        super().sync(sp)
        c = self.c
        self.all_scattered(sp)

        def load(j, k):
            sp.dma_start(self.y[j], c.sorted[bass.ds(k * P, P), :]).then_inc(self.y_in[j].sem, 16)

        def store(i, j, k):
            sp.wait_ge(self.o_set.sem, self.o_set.at(k + 1))
            sp.dma_start(c.results[bass.ds(k * P, P), :], self.o[j]).then_inc(self.o_out[j].sem, 16)

        def step(i, j, k, left):
            if left >= RING:
                sp.wait_ge(self.y_turned.sem, self.y_turned.at(k + 1))
                load(j, k + RING)
            if not (isinstance(k, int) and k < 2):
                store(*self.later(i, j, -2))

        for j in range(RING):
            load(j, j)
        self.every_tile(sp, step)
        for n in (2, 1):
            store(*self.later(self.tiles // RING, 0, -n))

    def gpsimd(self, pool):
        super().gpsimd(pool)
        self.scatter(pool)
        for slot in self.o_out:
            pool.wait_ge(slot.sem, slot.at(16 * (self.tiles // RING)))
        self.gather(pool, self.back, self.gathered)


    def shared_steps(self, groups, up, down):
        m = self.weights.shared_tiles
        lo, hi = groups[0] * m, groups[-1] * m + m
        for n in range(lo, hi + 2):
            if n < hi:
                up(n)
            if n >= lo + 2:
                down(n - 2)

    def tensor(self, pe):
        super().tensor(pe)
        c, w = self.c, self.weights
        w.wait(pe)

        def shared_up(n):
            g, j = divmod(n, w.shared_tiles)
            m = w.rows(j)
            if n >= 2:
                pe.wait_ge(self.s_mul.sem, self.s_mul.at(n - 1))
            for k, weight in enumerate((w.sg, w.su)):
                for f in range(FT):
                    mm = pe.matmul(c.bank[6 * (n % 2) + k][0:m, :], weight[:, f, P * j:P * j + m],
                                   c.yt[:, f, 512 * g:512 * g + 512], start=(f == 0), stop=(f == FT - 1))
            mm.then_inc(self.s_prod.sem, 1)
            if n == 1:
                self.count_before(pe)

        def shared_down(n):
            g, j = divmod(n, w.shared_tiles)
            m = w.rows(j)
            pe.wait_ge(self.s_mul.sem, self.s_mul.at(n + 1))
            if j == 0 and g:
                pe.wait_ge(self.s_added.sem, self.s_added.at(2 * g))
            for q in range(4):
                mm = pe.matmul(c.bank[4 + q // 2][:, D * (q % 2):D * (q % 2) + D], self.sh[n % 3][0:m, P * q:P * q + P],
                               w.sd[0:m, j, :], start=(j == 0 and q % 2 == 0), stop=(j == w.shared_tiles - 1),
                               skip_group_check=True)
            mm.then_inc(self.s_down.sem, 1)

        def turn_y(i, j, k):
            pe.wait_ge(self.y_in[j].sem, self.y_in[j].at(16 * (i + 1)))
            for f in range(FT):
                mm = pe.transpose(self.y_bank[j][:, P * f:P * f + P], self.y[j][:, P * f:P * f + P], c.identf[:, :])
            mm.then_inc(self.y_turned.sem, 1)

        def up(i, j, k):
            own = self.tile_owner(pe, k)
            pe.wait_ge(self.y_set.sem, self.y_set.at(k + 1))
            for f in range(FT):
                mm = pe.matmul(self.gu_bank[j][:, 0:2 * self.hidden], self.yt[j][:, f, :],
                               w.wgu[:, f, bass.ds(own * (2 * self.hidden), 2 * self.hidden)],
                               start=(f == 0), stop=(f == FT - 1))
            mm.then_inc(self.gu.sem, 1)

        def turn_h(i, j, k):
            pe.wait_ge(self.h_done.sem, self.h_done.at(k + 1))
            if not (isinstance(k, int) and k == 0):
                pe.wait_ge(self.ht_set.sem, self.ht_set.at(k))
            for f in range(2):
                mm = pe.transpose(self.ht_bank[:, P * f:P * f + P], self.h[j][:, P * f:P * f + P], c.identf[:, :])
            mm.then_inc(self.h_turned.sem, 1)

        def down(i, j, k):
            own = self.tile_owner(pe, k)
            pe.wait_ge(self.ht_set.sem, self.ht_set.at(k + 1))
            if not (isinstance(k, int) and k == 0):
                pe.wait_ge(self.o_set.sem, self.o_set.at(k))
            rest = self.hidden - P
            pe.matmul(self.o_bank, self.ht[j][:, 0, :], w.wd0[:, bass.ds(own * D, D)], start=True, stop=False)
            pe.matmul(self.o_bank, self.ht[j][0:rest, 1, :], w.wd1[0:rest, bass.ds(own * D, D)], start=False,
                      stop=True).then_inc(self.down.sem, 1)

        def step(i, j, k, left):
            if left >= 2:
                turn_y(*self.later(i, j, 2))
            if left >= 1:
                up(*self.later(i, j, 1))
            turn_h(i, j, k)
            if not (isinstance(k, int) and k == 0):
                down(*self.later(i, j, -1))

        self.shared_steps((0, 1), shared_up, shared_down)
        pe.wait_ge(self.owners.sem, self.owners.at(1))
        pe.wait_ge(self.s_added.sem, self.s_added.at(2 * 2))
        for j in range(2):
            turn_y(0, j, j)
        up(0, 0, 0)
        self.every_tile(pe, step)
        down(self.tiles // RING - 1, RING - 1, self.tiles - 1)
        pe.wait_ge(self.o_set.sem, self.o_set.at(self.tiles))
        self.shared_steps((2, 3), shared_up, shared_down)

    def scalar(self, act):
        super().scalar(act)
        c, w = self.c, self.weights

        def shared_silu(n):
            m = w.rows(n % w.shared_tiles)
            act.wait_ge(self.s_prod.sem, self.s_prod.at(n + 1))
            if n >= 2:
                act.wait_ge(self.s_mul.sem, self.s_mul.at(n - 1))
            act.activation(self.sg[n % 2][0:m, :], c.bank[6 * (n % 2)][0:m, :], ACT.Silu).then_inc(self.s_silu.sem, 1)

        def silu(i, j, k):
            act.wait_ge(self.gu.sem, self.gu.at(k + 1))
            act.activation(self.g[j], self.gu_bank[j][:, 0:self.hidden], ACT.Silu).then_inc(self.silu.sem, 1)

        def out(i, j, k):
            act.wait_ge(self.down.sem, self.down.at(k + 1))
            if not (isinstance(i, int) and i == 0):
                act.wait_ge(self.o_out[j].sem, self.o_out[j].at(16 * i))
            act.activation(self.o[j], self.o_bank, ACT.Copy).then_inc(self.o_set.sem, 1)

        def step(i, j, k, left):
            if left >= 1:
                silu(*self.later(i, j, 1))
            if not (isinstance(k, int) and k == 0):
                out(*self.later(i, j, -1))

        m = w.shared_tiles
        for n in range(2 * m):
            shared_silu(n)
        silu(0, 0, 0)
        self.every_tile(act, step)
        out(self.tiles // RING - 1, RING - 1, self.tiles - 1)
        for n in range(2 * m, 4 * m):
            shared_silu(n)

    def vector(self, dve):
        c, w = self.c, self.weights
        for h in self.h:
            dve.memset(h, 0.0).then_inc(self.h_clear.sem, 1)
        self.choose(dve)
        self.find_places(dve)

        def shared_group(g):
            for n in range(g * w.shared_tiles, g * w.shared_tiles + w.shared_tiles):
                m = w.rows(n % w.shared_tiles)
                dve.wait_ge(self.s_silu.sem, self.s_silu.at(n + 1))
                if n >= 3:
                    dve.wait_ge(self.s_down.sem, self.s_down.at(n - 2))
                dve.tensor_tensor(self.sh[n % 3][0:m, :], c.bank[6 * (n % 2) + 1][0:m, :], self.sg[n % 2][0:m, :],
                                  ALU.mult).then_inc(self.s_mul.sem, 1)
            dve.wait_ge(self.s_down.sem, self.s_down.at((g + 1) * w.shared_tiles))
            for half in range(2):
                x = c.x[:, 4 * g + 2 * half:4 * g + 2 * half + 2, :].rearrange("p t d -> p (t d)")
                dve.tensor_tensor(x, c.bank[4 + half][:, :], x, ALU.add).then_inc(self.s_added.sem, 1)

        def set_y(i, j, k):
            dve.wait_ge(self.y_turned.sem, self.y_turned.at(k + 1))
            dve.tensor_copy(self.yt[j].rearrange("p f t -> p (f t)"), self.y_bank[j]).then_inc(self.y_set.sem, 1)

        def mul(i, j, k):
            dve.wait_ge(self.silu.sem, self.silu.at(k + 1))
            dve.tensor_tensor(self.h[j][:, 0:self.hidden], self.gu_bank[j][:, self.hidden:2 * self.hidden], self.g[j],
                              ALU.mult).then_inc(self.h_done.sem, 1)

        def step(i, j, k, left):
            if left >= 2:
                set_y(*self.later(i, j, 2))
            if left >= 1:
                mul(*self.later(i, j, 1))
            dve.wait_ge(self.h_turned.sem, self.h_turned.at(k + 1))
            dve.tensor_copy(self.ht[j].rearrange("p f t -> p (f t)"), self.ht_bank).then_inc(self.ht_set.sem, 1)

        shared_group(0)
        shared_group(1)
        dve.wait_ge(self.h_clear.sem, self.h_clear.at(RING))
        for j in range(2):
            set_y(0, j, j)
        mul(0, 0, 0)
        self.every_tile(dve, step)
        shared_group(2)
        shared_group(3)
        dve.wait_ge(self.s_added.sem, self.s_added.at(2 * NG))
        for g in range(NG):
            dve.wait_ge(self.gathered[g].sem, self.gathered[g].at(128))
            for k, done in ((0, self.added1), (1, self.added)):
                if k:
                    dve.wait_ge(self.added1.sem, self.added1.at(4 * g + 4))
                for t in range(4 * g, 4 * g + 4):
                    dve.scalar_tensor_tensor(out=c.x[:, t, :], in0=self.back[k][:, t, :],
                                             scalar=self.weight[k][:, t:t + 1], in1=c.x[:, t, :], op0=ALU.mult,
                                             op1=ALU.add).then_inc(done.sem, 1)
        dve.wait_ge(self.added.sem, self.added.at(NT))


class KeyedSum(Stage):

    def __init__(self, c, name, ln, w, bias, cos, sin, wo, bias_out):
        self.c, self.ln = c, ln
        self.dram = (w, bias, cos, sin, wo, bias_out)
        r = Carve(c.region["a"])
        self.w = r.take([FT, 3 * D])
        self.bias = r.take([3 * D])
        self.cos = r.take([BT, P])
        self.sin = r.take([BT, P])
        self.wo = r.take([FT, D])
        self.bias_out = r.take([D])
        self.k = r.take([NT, D])
        self.ta = [r.take([2, P]) for _ in range(2)]
        self.tb = [r.take([2, P]) for _ in range(2)]
        self.ws = [r.take([FT, D]) for _ in range(NB)]
        self.ones = r.take([1])
        self.ss = r.take([NT])
        self.norm = r.take([NT])
        self.rnorm = r.take([NT])
        (self.w_in, self.prod, self.lin, self.v_done, self.cosm, self.sinm, self.rot, self.square, self.root,
         self.floor, self.rec, self.kv, self.sums, self.scaled, self.xy, self.biased, self.one) = (
            c.sem(f"{name}_{n}") for n in
            "w_in prod lin v_done cosm sinm rot square root floor rec kv sums scaled xy biased one".split())

    def sync(self, sp):
        w, bias, cos, sin, wo, bias_out = self.dram
        for dst, src in ((self.w, w.rearrange("(f p) n -> p f n", p=P)), (self.bias, bias.partition_broadcast(P)),
                         (self.cos, cos.rearrange("(t p) n -> p t n", p=P)),
                         (self.sin, sin.rearrange("(t p) n -> p t n", p=P)),
                         (self.wo, wo.rearrange("(f p) n -> p f n", p=P)),
                         (self.bias_out, bias_out.partition_broadcast(P))):
            sp.dma_start(dst, src).then_inc(self.w_in, 16)

    def gpsimd(self, pool):
        c = self.c
        pool.wait_ge(self.w_in, 96)
        pool.memset(self.ones, 1.0).then_inc(self.one, 1)
        for t in range(NT):
            self.ln.normed(pool, t)
            pool.tensor_tensor(c.x[:, t, :], c.x[:, t, :], c.yn[:, t, :], ALU.add).then_inc(self.xy, 1)
            pool.wait_ge(self.xy, t + 1)
            pool.tensor_tensor(c.x[:, t, :], c.x[:, t, :], self.bias_out, ALU.add).then_inc(self.biased, 1)
        for b in range(NB):
            s = slice(b * BT, b * BT + BT)
            pool.wait_ge(self.square, (b + 1) * BT)
            pool.tensor_tensor(self.norm[:, s], self.ss[:, s], c.half[:, s], ALU.pow).then_inc(self.root, 1)

    def tensor(self, pe):
        c = self.c
        pe.wait_ge(self.w_in, 96)
        for g in range(NG):
            self.ln.ready(pe, g)
            for t in range(4 * g, 4 * g + 4):
                if t >= 2:
                    pe.wait_ge(self.lin, 2 * (t - 1))
                    pe.wait_ge(self.v_done, t - 1)
                for bank, lo, n in ((2 * (t % 2), D, 2 * D), (2 * (t % 2) + 1, 0, D)):
                    for f in range(FT):
                        mm = pe.matmul(c.bank[bank][:, 0:n], c.yt[:, f, P * t:P * t + P], self.w[:, f, lo:lo + n],
                                       start=(f == 0), stop=(f == FT - 1))
                mm.then_inc(self.prod, 1)
        pe.wait_ge(self.one, 1)
        for b in range(NB):
            pe.wait_ge(self.kv, (b + 1) * BT)
            for f in range(FT):
                for t in range(b * BT, b * BT + BT):
                    mm = pe.matmul(c.bank[4 + b][:, f:f + 1], self.k[:, t, P * f:P * f + P], self.ones,
                                   start=(t == b * BT), stop=(t == b * BT + BT - 1))
            mm.then_inc(self.sums, 1)

    def scalar(self, act):
        c = self.c
        self.ln.ready(act, NG - 1)
        for t in range(NT):
            act.wait_ge(self.rot, 2 * t + 2)
            if t:
                act.wait_ge(self.square, t)
            act.activation(c.bank[6][:, 0:D], self.k[:, t, :], ACT.Square,
                           accum_out=self.ss[:, t:t + 1]).then_inc(self.square, 1)

    def vector(self, dve):
        c = self.c
        dve.wait_ge(self.w_in, 96)
        cx = c.cx[:, :].rearrange("p (t d) -> p t d", d=D)

        def product(b):
            s = slice(b * BT, b * BT + BT)
            dve.wait_ge(self.root, b + 1)
            dve.tensor_scalar(self.norm[:, s], self.norm[:, s], 1e-12, None, ALU.max).then_inc(self.floor, 1)
            dve.wait_ge(self.floor, b + 1)
            dve.reciprocal(self.rnorm[:, s], self.norm[:, s]).then_inc(self.rec, 1)
            dve.wait_ge(self.rec, b + 1)
            for t in range(b * BT, b * BT + BT):
                dve.scalar_tensor_tensor(out=self.k[:, t, :], in0=self.k[:, t, :], scalar=self.rnorm[:, t:t + 1],
                                         in1=c.yn[:, t, :], op0=ALU.mult, op1=ALU.mult).then_inc(self.kv, 1)

        for t in range(NT):
            kv, q = c.bank[2 * (t % 2)], c.bank[2 * (t % 2) + 1]
            bt = t % BT
            dve.wait_ge(self.prod, t + 1)
            dve.tensor_tensor(cx[:, t, :], q[:, 0:D], self.bias[:, 0:D], ALU.add).then_inc(self.lin, 1)
            dve.tensor_tensor(self.k[:, t, :], kv[:, 0:D], self.bias[:, D:2 * D], ALU.add).then_inc(self.lin, 1)
            dve.wait_ge(self.xy, t + 1)
            self.ln.ready(dve, t // 4)
            dve.tensor_tensor(c.yn[:, t, :], kv[:, D:2 * D], self.bias[:, 2 * D:3 * D], ALU.add).then_inc(self.v_done, 1)
            dve.wait_ge(self.lin, 2 * t + 2)
            if t >= 2:
                dve.wait_ge(self.rot, 2 * t - 2)
            a, b = self.ta[t % 2], self.tb[t % 2]
            sin = self.sin[:, bt, :].rearrange("p (n e) -> p n e", e=2)
            for n, z in enumerate((cx[:, t, 0:P], self.k[:, t, 0:P])):
                pair = z.rearrange("p (n e) -> p n e", e=2)
                bp = b[:, n, :].rearrange("p (n e) -> p n e", e=2)
                dve.tensor_tensor(a[:, n, :], z, self.cos[:, bt, :], ALU.mult).then_inc(self.cosm, 1)
                for e in range(2):
                    dve.tensor_tensor(bp[:, :, e], pair[:, :, 1 - e], sin[:, :, e], ALU.mult).then_inc(self.sinm, 1)
            dve.wait_ge(self.cosm, 2 * t + 2)
            dve.wait_ge(self.sinm, 4 * t + 4)
            for n, z in enumerate((cx[:, t, 0:P], self.k[:, t, 0:P])):
                dve.tensor_tensor(z, a[:, n, :], b[:, n, :], ALU.add).then_inc(self.rot, 1)
            if t == BT + 1:
                dve.wait_ge(self.v_done, BT)
                product(0)
        dve.wait_ge(self.v_done, NT)
        product(1)
        for b in range(NB):
            dve.wait_ge(self.sums, b + 1)
            for f in range(FT):
                dve.tensor_scalar(self.ws[b][:, f, :], self.wo[:, f, :], c.bank[4 + b][:, f:f + 1], None,
                                  ALU.mult).then_inc(self.scaled, 1)
        dve.wait_ge(self.biased, NT)

    def source(self, t, f):
        return self.c.cx[:, D * t + P * f:D * t + P * f + P]

    def out_weights(self, t, f):
        return self.ws[t // BT][:, f, :]

    def finished(self, pe, g):
        if g == 0:
            pe.wait_ge(self.rot, 2 * NT)
            pe.wait_ge(self.scaled, NB * FT)


class LinearAttention(Stage):

    HEAD = 16
    EPS = 1e-6

    def __init__(self, c, name, ln, wq, wkv, bq, bkv, wo, bo, decay, block, member, at):
        self.c, self.ln = c, ln
        self.dram = (wq, wkv, bq, bkv, wo, bo, decay, block, member)
        r = Carve(c.region["a"])
        self.wq = r.take([FT, D])
        self.wkv = r.take([FT, 2 * D])
        self.wo = r.take([FT, D])
        self.bq = r.take([FT])
        self.bkv = r.take([2 * D])
        self.bo = r.take([D])
        self.decay = r.take([BT])
        self.block = r.take([P])
        self.member = r.take([P // self.HEAD])
        self.kt = [r.take([D]) for _ in range(2)]
        self.nh = P // self.HEAD
        self.bd = [r.take([FT, P + self.nh]) for _ in range(NB)]
        self.den = [r.take([FT, self.nh]) for _ in range(2)]
        self.rden = [r.take([FT, self.nh]) for _ in range(2)]
        self.k = r.take([NT, D])
        r = Carve(c.region["w"], at)
        self.v = r.take([NT, FT, P + 1])
        self.qt = r.take([FT, NTOK])
        (self.w_in, self.qprod, self.q_done, self.kvprod, self.k_lin, self.v_done, self.k_done, self.one,
         self.sums, self.bd_done, self.outp, self.dn, self.rc, self.rd, self.o_done, self.biased) = (
            c.sem(f"{name}_{n}") for n in
            "w_in qprod q_done kvprod k_lin v_done k_done one sums bd_done outp dn rc rd o_done biased".split())

    def sync(self, sp):
        wq, wkv, bq, bkv, wo, bo, decay, block, member = self.dram
        for dst, src in ((self.wq, wq.rearrange("(f p) n -> p f n", p=P)),
                         (self.wkv, wkv.rearrange("(f p) n -> p f n", p=P)),
                         (self.wo, wo.rearrange("(f p) n -> p f n", p=P)), (self.bq, bq),
                         (self.bkv, bkv.partition_broadcast(P)), (self.bo, bo.partition_broadcast(P)),
                         (self.decay, decay), (self.block, block), (self.member, member)):
            sp.dma_start(dst, src).then_inc(self.w_in, 16)

    W_IN = 9 * 16

    def gpsimd(self, pool):
        c = self.c
        pool.wait_ge(self.w_in, self.W_IN)
        pool.memset(self.v[:, :, :, P:P + 1], 1.0).then_inc(self.one, 1)
        for t in range(NT):
            self.ln.normed(pool, t)
            pool.tensor_tensor(c.x[:, t, :], c.x[:, t, :], self.bo, ALU.add).then_inc(self.biased, 1)

    def tensor(self, pe):
        c, nh = self.c, self.nh
        pe.wait_ge(self.w_in, self.W_IN)
        for g in range(NG):
            self.ln.ready(pe, g)
            for o in range(FT):
                if g:
                    pe.wait_ge(self.q_done, FT * (g - 1) + o + 1)
                for f in range(FT):
                    mm = pe.matmul(c.bank[o][:, :], self.wq[:, f, P * o:P * o + P], c.yt[:, f, 512 * g:512 * g + 512],
                                   start=(f == 0), stop=(f == FT - 1))
                mm.then_inc(self.qprod, 1)
            for t in range(4 * g, 4 * g + 4):
                if t >= 2:
                    pe.wait_ge(self.k_lin, t - 1)
                    pe.wait_ge(self.v_done, t - 1)
                for f in range(FT):
                    mm = pe.matmul(c.bank[2 + t % 2][:, :], c.yt[:, f, P * t:P * t + P], self.wkv[:, f, :],
                                   start=(f == 0), stop=(f == FT - 1))
                mm.then_inc(self.kvprod, 1)
        pe.wait_ge(self.one, 1)
        for b in range(NB):
            pe.wait_ge(self.k_done, (b + 1) * BT)
            pe.wait_ge(self.v_done, (b + 1) * BT)
            for f in range(FT):
                for t in range(b * BT, b * BT + BT):
                    mm = pe.matmul(c.bank[4 + b][:, D * f:D * f + P + 1], self.k[:, t, P * f:P * f + P],
                                   self.v[:, t, f, :], start=(t == b * BT), stop=(t == b * BT + BT - 1))
            mm.then_inc(self.sums, 1)
        pe.wait_ge(self.q_done, FT * NG)
        for t in range(NT):
            pe.wait_ge(self.bd_done, 2 * FT * (t // BT + 1))
            if t >= 4:
                pe.wait_ge(self.o_done, t - 3)
            for f in range(FT):
                mm = pe.matmul(c.bank[t % 4][:, (P + nh) * f:(P + nh) * (f + 1)], self.qt[:, f, P * t:P * t + P],
                               self.bd[t // BT][:, f, :], start=True, stop=True)
            mm.then_inc(self.outp, 1)

    def scalar(self, act):
        c = self.c
        act.wait_ge(self.w_in, self.W_IN)
        for g in range(NG):
            for o in range(FT):
                act.wait_ge(self.qprod, FT * g + o + 1)
                act.activation(self.qt[:, o, 512 * g:512 * g + 512], c.bank[o][:, :], ACT.Relu,
                               bias=self.bq[:, o:o + 1]).then_inc(self.q_done, 1)

    def vector(self, dve):
        c, nh = self.c, self.nh
        dve.wait_ge(self.w_in, self.W_IN)
        halves = lambda z: z.rearrange("p (f e) -> p f e", f=FT)
        for t in range(NT):
            z = c.bank[2 + t % 2]
            dve.wait_ge(self.kvprod, t + 1)
            if t >= 2:
                dve.wait_ge(self.k_done, t - 1)
            dve.tensor_tensor(self.kt[t % 2], z[:, 0:D], self.bkv[:, 0:D], ALU.add).then_inc(self.k_lin, 1)
            dve.tensor_tensor(self.v[:, t, :, 0:P], halves(z[:, D:2 * D]), halves(self.bkv[:, D:2 * D]),
                              ALU.add).then_inc(self.v_done, 1)
            dve.wait_ge(self.k_lin, t + 1)
            dve.tensor_scalar(self.k[:, t, :], self.kt[t % 2], 0.0, self.decay[:, t % BT:t % BT + 1], ALU.max,
                              ALU.mult).then_inc(self.k_done, 1)
        for b in range(NB):
            dve.wait_ge(self.sums, b + 1)
            for f in range(FT):
                z = c.bank[4 + b][:, D * f:D * f + P + 1]
                dve.tensor_tensor(self.bd[b][:, f, 0:P], z[:, 0:P], self.block, ALU.mult).then_inc(self.bd_done, 1)
                dve.tensor_scalar(self.bd[b][:, f, P:P + nh], self.member, z[:, P:P + 1], None,
                                  ALU.mult).then_inc(self.bd_done, 1)
        for t in range(NT):
            z = c.bank[t % 4][:, 0:FT * (P + nh)].rearrange("p (f e) -> p f e", f=FT)
            den, rden = self.den[t % 2], self.rden[t % 2]
            decay = self.decay[:, t % BT:t % BT + 1]
            dve.wait_ge(self.outp, t + 1)
            dve.tensor_scalar(den, z[:, :, P:P + nh], decay, self.EPS, ALU.mult, ALU.add).then_inc(self.dn, 1)
            dve.wait_ge(self.dn, t + 1)
            dve.reciprocal(rden, den).then_inc(self.rc, 1)
            dve.wait_ge(self.rc, t + 1)
            dve.tensor_scalar(den, rden, decay, None, ALU.mult).then_inc(self.rd, 1)
            dve.wait_ge(self.rd, t + 1)
            dve.tensor_tensor(c.cx[:, D * t:D * t + D].rearrange("p (f h e) -> p f h e", f=FT, h=nh),
                              z[:, :, 0:P].rearrange("p f (h e) -> p f h e", h=nh), over(den, 3, self.HEAD),
                              ALU.mult).then_inc(self.o_done, 1)
        dve.wait_ge(self.biased, NT)

    def source(self, t, f):
        return self.c.cx[:, D * t + P * f:D * t + P * f + P]

    def finished(self, pe, g):
        pe.wait_ge(self.o_done, 4 * g + 4 if g else NT)


class Weights(Stage):

    def __init__(self, c, name, wg, wu, wd, hidden):
        self.c, self.hidden, self.dram = c, hidden, (wg, wu, wd)
        r = Carve(c.region["w"])
        self.nj = -(-hidden // P)
        self.wg, self.wu, self.wd = r.take([FT, hidden]), r.take([FT, hidden]), r.take([self.nj, D])
        self.end = r.at
        self.loaded = c.sem(name + "_loaded")

    def sync(self, sp):
        wg, wu, wd = self.dram
        full = self.hidden // P
        sp.dma_start(self.wg, wg.rearrange("(f p) n -> p f n", p=P)).then_inc(self.loaded, 16)
        sp.dma_start(self.wu, wu.rearrange("(f p) n -> p f n", p=P)).then_inc(self.loaded, 16)
        sp.dma_start(self.wd[:, 0:full, :], wd[0:full * P, :].rearrange("(j p) n -> p j n", p=P)).then_inc(self.loaded, 16)
        if full < self.nj:
            sp.dma_start(self.wd[0:self.hidden - full * P, full, :], wd[full * P:, :]).then_inc(self.loaded, 16)

    def wait(self, eng):
        eng.wait_ge(self.loaded, 16 * (3 + (self.hidden % P > 0)))


class SharedWeights(Stage):

    def __init__(self, c, name, wgu, wd, sg, su, sd):
        self.c, self.dram = c, (wgu, wd, sg, su, sd)
        self.experts, self.hidden, self.shared = wd.shape[0], wd.shape[1], sd.shape[0]
        self.shared_tiles = -(-self.shared // P)
        r = Carve(c.region["w"])
        self.wgu = r.take([FT, self.experts * 2 * self.hidden])
        self.wd0, self.wd1 = r.take([self.experts * D]), r.take([self.experts * D])
        self.sg, self.su, self.sd = r.take([FT, self.shared]), r.take([FT, self.shared]), r.take([self.shared_tiles, D])
        self.end = r.at
        self.loaded = c.sem(name + "_loaded")

    def rows(self, j):
        return min(P, self.shared - P * j)

    def sync(self, sp):
        wgu, wd, sg, su, sd = self.dram
        full = self.shared // P
        rest = self.hidden - P
        by_expert = lambda v: v.rearrange("p (e d) -> p e d", d=D)
        for dst, src in ((self.sg, sg.rearrange("(f p) n -> p f n", p=P)), (self.su, su.rearrange("(f p) n -> p f n", p=P)),
                         (self.sd[:, 0:full, :], sd[0:full * P, :].rearrange("(j p) n -> p j n", p=P)),
                         (self.sd[0:self.shared - full * P, full, :], sd[full * P:, :]),
                         (self.wgu, wgu.rearrange("(f p) n -> p f n", p=P)),
                         (by_expert(self.wd0), wd[:, 0:P, :].rearrange("e p d -> p e d")),
                         (by_expert(self.wd1)[0:rest], wd[:, P:, :].rearrange("e p d -> p e d"))):
            sp.dma_start(dst, src).then_inc(self.loaded, 16)

    def wait(self, eng):
        eng.wait_ge(self.loaded, 16 * 7)


class After(Stage):

    def __init__(self, sem, count):
        self.sem, self.count = sem, count

    def sync(self, sp):
        sp.wait_ge(self.sem, self.count)

    gpsimd = sync


class Finish(Stage):
    def __init__(self, c, out, added, count):
        self.c, self.out, self.added, self.count, self.out_done = c, out, added, count, c.sem("out_done")

    def sync(self, sp):
        out = self.out.rearrange("b (t p) d -> p (b t) d", p=P)
        sp.wait_ge(self.added, self.count)
        for g in range(NG):
            sp.dma_start(out[:, 4 * g:4 * g + 4, :], self.c.x[:, 4 * g:4 * g + 4, :]).then_inc(self.out_done, 16)
        sp.wait_ge(self.out_done, 16 * NG)


def build(nc, t, out):
    with ExitStack() as ctx:
        c = Core(nc, ctx)
        stages = [Start(c, t["x"], t["identf"], t["identb"])]
        w0 = Weights(c, "w0", t["f0_wg"], t["f0_wu"], t["f0_wd"], t["f0_wg"].shape[1])
        w1 = SharedWeights(c, "w1", t["f1_wgu"], t["f1_wd"], t["f1_sg"], t["f1_su"], t["f1_sd"])
        last = [None]
        counts = {"ln": 0, "project": 0}

        def begin(name):
            if last[0] is not None:
                stages.append(After(*last[0]))
            ln = LayerNorm(c, counts["ln"])
            counts["ln"] += 1
            stages.append(ln)
            return ln

        def project(name, mixer, w):
            p = Project(c, counts["project"], mixer.source, w, mixer.finished)
            counts["project"] += 1
            stages.append(p)
            last[0] = (p.added, NT * counts["project"])

        def attention(name, hd, w, wo, tables, bias, bias_out):
            ln = begin(name)
            a = Attention(c, name, ln, hd, t[w], t[wo], (t[tables + "_cos"], t[tables + "_sin"]), t[bias], t[bias_out],
                          t["mask_q"], t["mask_k"])
            stages.append(a)
            project(name, a, lambda tt, f: a.wo[:, f, :])

        def top_two(name, weights, n, w):
            ln = begin(name)
            m = TopTwo(c, ln, n, weights, t[w], t, Carve(c.region["a"]))
            stages.append(m)
            last[0] = (m.added.sem, m.added.at(NT))

        def routed(name, weights, n, w, bias):
            ln = begin(name)
            m = Routed(c, ln, n, weights, t[w], t[bias], t, Carve(c.region["a"]))
            stages.append(m)
            last[0] = (m.added.sem, m.added.at(NT))

        def s1():
            attention("a0", 8, "a0_w", "a0_wo", "a0", "a0_bias", "a0_bo")

        def s2():
            routed("f0", w0, 4, "f0_wr", "f0_br")

        def s3():
            ln = begin("b0")
            m = KeyedSum(c, "b0", ln, t["b0_w"], t["b0_bias"], t["b0_cos"], t["b0_sin"], t["b0_wo"], t["b0_bo"])
            stages.append(m)
            project("b0", m, m.out_weights)

        def s4():
            routed("f0b", w0, 4, "f0_wr", "f0_br")

        def s5():
            ln = begin("a1")
            stages.append(w1)
            m = LinearAttention(c, "a1", ln, t["a1_wq"], t["a1_wkv"], t["a1_bq"], t["a1_bkv"], t["a1_wo"], t["a1_bo"],
                                t["decay"], t["block"], t["member"], w1.end)
            stages.append(m)
            project("a1", m, lambda tt, f: m.wo[:, f, :])

        def s6():
            top_two("f1", w1, 8, "f1_gate")

        def s7():
            attention("b1", 16, "b1_w", "b1_wo", "b1", "b1_bias", "b1_bo")

        def s8():
            top_two("f1b", w1, 8, "f1_gate")

        stages.append(w0)
        for stage in (s1, s2, s3, s4, s5, s6, s7, s8):
            stage()
        stages.append(Finish(c, out, *last[0]))

        block = ctx.enter_context(nc.Block())

        @block.sync
        def _(sp):
            for s in stages:
                s.sync(sp)

        @block.gpsimd
        def _(pool):
            for s in stages:
                s.gpsimd(pool)

        @block.scalar
        def _(act):
            for s in stages:
                s.scalar(act)

        @block.tensor
        def _(pe):
            for s in stages:
                s.tensor(pe)

        @block.vector
        def _(dve):
            for s in stages:
                s.vector(dve)



def constants():
    import numpy as np

    f = np.float32
    bf = mybir.dt.np(BF16)
    pos = np.arange(SEQ, dtype=f)
    out = {}

    inv = (f(1) / np.power(f(10000), np.arange(0, 8, 2, dtype=f) / f(8))).astype(f)
    th = np.outer(pos, inv).astype(f)
    out["a0_cos"] = np.concatenate([np.cos(th), np.cos(th)], 1)
    out["a0_sin"] = np.concatenate([-np.sin(th), np.sin(th)], 1)

    inv = (f(1) / np.power(f(10000), np.arange(0, P, 2, dtype=f) / f(P))).astype(f)
    th = np.repeat(pos[:, None] * inv[None, :], 2, 1).astype(f)
    sign = np.tile(np.array([-1, 1], f), P // 2)
    out["b0_cos"], out["b0_sin"] = np.cos(th), np.sin(th) * sign

    inv = np.power(f(10000), f(-2) * np.arange(8, dtype=f) / f(16)).astype(f)
    th = (pos[:, None] * inv[None, :]).astype(f)
    out["b1_cos"], out["b1_sin"] = np.tile(np.cos(th), (1, 2)), np.tile(np.sin(th), (1, 2))

    out["decay"] = np.exp(-pos / f(SEQ)).reshape(BT, P).T
    q = np.arange(P)
    out["mask_q"] = np.where(q[None, :] > q[:, None], f(NEG), f(0)).astype(bf)
    out["mask_k"] = out["mask_q"].T
    out["block"] = (q[:, None] // 16 == q[None, :] // 16).astype(f)
    out["member"] = (q[:, None] // 16 == np.arange(8)[None, :]).astype(f)
    out["identf"] = np.eye(P, dtype=f)
    out["identb"] = np.eye(P, dtype=f).astype(bf)
    out["lower"] = (q[:, None] < q[None, :]).astype(bf)
    out["ones"] = np.ones((P, P), bf)
    out["edges"] = np.arange(NT, dtype=f) * P
    out["numbers"] = np.arange(L1_TILES, dtype=f)
    out["a0_bias"] = np.zeros(3 * P, f)
    return {k: np.ascontiguousarray(v) for k, v in out.items()}


def kernel(**i):
    import numpy as np
    import concourse.bacc as bacc
    from concourse.bass_utils import run_bass_kernel_spmd

    i = {k: np.asarray(v) for k, v in i.items()}
    cat = lambda *a: np.concatenate(a, -1)
    by_feature = lambda w: np.transpose(w, (1, 0, 2)).reshape(w.shape[1], -1)
    arrays = {
        "x": i["L0_attn_a_x"],
        "a0_w": cat(i["L0_attn_a_Wq"], i["L0_attn_a_Wk"], i["L0_attn_a_Wv"]),
        "a0_wo": i["L0_attn_a_Wo"], "a0_bo": i["L0_attn_a_b_out"],
        "f0_wr": i["L0_ffn_Wr"], "f0_br": i["L0_ffn_br"],
        "f0_wg": by_feature(i["L0_ffn_Wg"]), "f0_wu": by_feature(i["L0_ffn_Wu"]),
        "f0_wd": i["L0_ffn_Wd"].reshape(-1, D),
        "b0_w": i["L0_attn_b_W_in"].T, "b0_bias": i["L0_attn_b_b_in"],
        "b0_wo": i["L0_attn_b_W_out"].T, "b0_bo": i["L0_attn_b_b_out"],
        "a1_wq": i["L1_attn_a_Wq"].T, "a1_wkv": cat(i["L1_attn_a_Wk"].T, i["L1_attn_a_Wv"].T),
        "a1_bq": i["L1_attn_a_bq"].reshape(FT, P).T, "a1_bkv": cat(i["L1_attn_a_bk"], i["L1_attn_a_bv"]),
        "a1_wo": i["L1_attn_a_Wo"].T, "a1_bo": i["L1_attn_a_bo"],
        "f1_gate": i["L1_ffn_gate_w"],
        "f1_wgu": by_feature(cat(i["L1_ffn_w_gate"], i["L1_ffn_w_up"])), "f1_wd": i["L1_ffn_w_down"],
        "f1_sg": i["L1_ffn_sw_gate"], "f1_su": i["L1_ffn_sw_up"], "f1_sd": i["L1_ffn_sw_down"],
        "b1_w": cat(i["L1_attn_b_Wq"].T, i["L1_attn_b_Wk"].T, i["L1_attn_b_Wv"].T),
        "b1_bias": cat(i["L1_attn_b_bq"], i["L1_attn_b_bk"], i["L1_attn_b_bv"]),
        "b1_wo": i["L1_attn_b_Wo"].T, "b1_bo": i["L1_attn_b_bo"],
        **constants(),
    }
    arrays = {"in_" + k: np.ascontiguousarray(v) for k, v in arrays.items()}
    nc = bacc.Bacc("TRN2", target_bir_lowering=False, num_devices=1)
    tensors = {k[3:]: nc.dram_tensor(k, v.shape, mybir.dt.from_np(v.dtype), kind="ExternalInput").ap()
               for k, v in arrays.items()}
    out = nc.dram_tensor("out", [NB, SEQ, D], F32, kind="ExternalOutput").ap()
    build(nc, tensors, out)
    r = run_bass_kernel_spmd(nc, [arrays], core_ids=[0])
    return r.results[0]["out"]
```
